# Optimizing a Trainium2 kernel written in Bass

```python
import numpy as np
import jax
import jax.numpy as jnp

def _softmax(x, axis=-1):
    return jax.nn.softmax(x, axis=axis)

def _gelu(x):
    return jax.nn.gelu(x, approximate=True)

def _silu(x):
    return jax.nn.silu(x)

def _sigmoid(x):
    return jax.nn.sigmoid(x)

def _layernorm(x, axis=-1, eps=1e-05):
    m = jnp.mean(x, axis=axis, keepdims=True)
    v = jnp.var(x, axis=axis, keepdims=True)
    return (x - m) / jnp.sqrt(v + eps)

def _scatter_add(tgt, idx, src, axis=0):
    return tgt.at[idx].add(src)

def _segment_sum(src, seg, n):
    return jax.ops.segment_sum(src, seg, n)
kernel_name = 'mk_recurrent_d1_jaxref_r8_7cc965'

def setup_inputs(seed: int=0):
    np.random.seed(seed)
    _w = jnp.asarray

    def _L0_attn_setup():
        import jax, jax.numpy as jnp
        import numpy as np
        B, H, D, K, F = (8, 16, 128, 64, 512)
        N, S = (4, 512)
        LN_EPS = 1e-06

        def _layer_norm(x, scale, bias):
            m = jnp.mean(x, axis=-1, keepdims=True)
            v = jnp.mean(jnp.square(x - m), axis=-1, keepdims=True)
            return (x - m) * jax.lax.rsqrt(v + LN_EPS) * scale + bias

        def _feature_map(x):
            return jax.nn.elu(x) + 1.0
        key = jax.random.key(seed)
        ks = jax.random.split(key, 9)
        w = lambda k, shape: jax.random.normal(k, shape, jnp.float32) * 0.02
        return {'x': jax.random.normal(ks[0], (N, S, D), jnp.float32), 'Wq': w(ks[1], (B, H, D, K)), 'bq': jnp.zeros((B, H, K), jnp.float32), 'Wk': w(ks[2], (B, H, D, K)), 'bk': jnp.zeros((B, H, K), jnp.float32), 'Wv': w(ks[3], (B, H, D, K)), 'bv': jnp.zeros((B, H, K), jnp.float32), 'Wo': w(ks[4], (B, H * K, D)), 'bo': jnp.zeros((B, D), jnp.float32), 'ln1_s': jnp.ones((B, D), jnp.float32), 'ln1_b': jnp.zeros((B, D), jnp.float32), 'W1': w(ks[5], (B, D, F)), 'b1': jnp.zeros((B, F), jnp.float32), 'W2': w(ks[6], (B, F, D)), 'b2': jnp.zeros((B, D), jnp.float32), 'ln2_s': jnp.ones((B, D), jnp.float32), 'ln2_b': jnp.zeros((B, D), jnp.float32)}
    _L0_attn_in = _L0_attn_setup()

    def _L0_ffn_setup():
        import jax, jax.numpy as jnp
        import numpy as np
        DIM = 128
        INTER = 64
        E = 32
        TOPK = 4
        GROUPS = 8
        TOPK_GROUPS = 4
        SHARED_INTER = 2 * INTER
        ROUTE_SCALE = 1.0
        B, S = (8, 512)

        def _gate(xf, gw, gb):
            T = xf.shape[0]
            scores = jax.nn.softmax((xf @ gw + gb).astype(jnp.float32), axis=-1)
            original_scores = scores
            scores_g = scores.reshape(T, GROUPS, E // GROUPS)
            group_scores = jnp.sum(jax.lax.top_k(scores_g, 2)[0], axis=-1)
            gidx = jax.lax.top_k(group_scores, TOPK_GROUPS)[1]
            keep = jnp.zeros((T, GROUPS), bool).at[jnp.arange(T)[:, None], gidx].set(True)
            masked = jnp.where(keep[:, :, None], scores_g, -jnp.inf).reshape(T, E)
            indices = jax.lax.top_k(masked, TOPK)[1]
            weights = jnp.take_along_axis(original_scores, indices, axis=1) * ROUTE_SCALE
            return (weights.astype(xf.dtype), indices)
        key = jax.random.key(seed)
        ks = jax.random.split(key, 16)

        def xav(k, shape):
            fan_in, fan_out = (shape[-2], shape[-1])
            lim = np.sqrt(6.0 / (fan_in + fan_out))
            return jax.random.uniform(k, shape, jnp.float32, -lim, lim)
        return {'x': jax.random.normal(ks[0], (B, S, DIM), jnp.float32), 'gw': xav(ks[1], (DIM, E)), 'gb': jnp.zeros((E,), jnp.float32), 'w1': xav(ks[2], (E, DIM, INTER)), 'b1': jnp.zeros((E, INTER), jnp.float32), 'w3': xav(ks[3], (E, DIM, INTER)), 'b3': jnp.zeros((E, INTER), jnp.float32), 'w2': xav(ks[4], (E, INTER, DIM)), 'b2': jnp.zeros((E, DIM), jnp.float32), 'sw1': xav(ks[5], (DIM, SHARED_INTER)), 'sb1': jnp.zeros((SHARED_INTER,), jnp.float32), 'sw3': xav(ks[6], (DIM, SHARED_INTER)), 'sb3': jnp.zeros((SHARED_INTER,), jnp.float32), 'sw2': xav(ks[7], (SHARED_INTER, DIM)), 'sb2': jnp.zeros((DIM,), jnp.float32)}
    _L0_ffn_in = _L0_ffn_setup()
    _d = {'L0_attn_x': _L0_attn_in['x'], 'L0_attn_Wq': _L0_attn_in['Wq'], 'L0_attn_bq': _L0_attn_in['bq'], 'L0_attn_Wk': _L0_attn_in['Wk'], 'L0_attn_bk': _L0_attn_in['bk'], 'L0_attn_Wv': _L0_attn_in['Wv'], 'L0_attn_bv': _L0_attn_in['bv'], 'L0_attn_Wo': _L0_attn_in['Wo'], 'L0_attn_bo': _L0_attn_in['bo'], 'L0_attn_ln1_s': _L0_attn_in['ln1_s'], 'L0_attn_ln1_b': _L0_attn_in['ln1_b'], 'L0_attn_W1': _L0_attn_in['W1'], 'L0_attn_b1': _L0_attn_in['b1'], 'L0_attn_W2': _L0_attn_in['W2'], 'L0_attn_b2': _L0_attn_in['b2'], 'L0_attn_ln2_s': _L0_attn_in['ln2_s'], 'L0_attn_ln2_b': _L0_attn_in['ln2_b'], 'L0_ffn_gw': _L0_ffn_in['gw'], 'L0_ffn_gb': _L0_ffn_in['gb'], 'L0_ffn_w1': _L0_ffn_in['w1'], 'L0_ffn_b1': _L0_ffn_in['b1'], 'L0_ffn_w3': _L0_ffn_in['w3'], 'L0_ffn_b3': _L0_ffn_in['b3'], 'L0_ffn_w2': _L0_ffn_in['w2'], 'L0_ffn_b2': _L0_ffn_in['b2'], 'L0_ffn_sw1': _L0_ffn_in['sw1'], 'L0_ffn_sb1': _L0_ffn_in['sb1'], 'L0_ffn_sw3': _L0_ffn_in['sw3'], 'L0_ffn_sb3': _L0_ffn_in['sb3'], 'L0_ffn_sw2': _L0_ffn_in['sw2'], 'L0_ffn_sb2': _L0_ffn_in['sb2']}
    _x0 = _d['L0_attn_x']
    _d['L0_attn_x'] = jax.random.normal(jax.random.fold_in(jax.random.key(seed), 1), (2, 1024, 128), dtype=_x0.dtype)
    del _x0
    return _d

def reference(L0_attn_x, L0_attn_Wq, L0_attn_bq, L0_attn_Wk, L0_attn_bk, L0_attn_Wv, L0_attn_bv, L0_attn_Wo, L0_attn_bo, L0_attn_ln1_s, L0_attn_ln1_b, L0_attn_W1, L0_attn_b1, L0_attn_W2, L0_attn_b2, L0_attn_ln2_s, L0_attn_ln2_b, L0_ffn_gw, L0_ffn_gb, L0_ffn_w1, L0_ffn_b1, L0_ffn_w3, L0_ffn_b3, L0_ffn_w2, L0_ffn_b2, L0_ffn_sw1, L0_ffn_sb1, L0_ffn_sw3, L0_ffn_sb3, L0_ffn_sw2, L0_ffn_sb2):

    def _L0_attn_ref(x, Wq, bq, Wk, bk, Wv, bv, Wo, bo, ln1_s, ln1_b, W1, b1, W2, b2, ln2_s, ln2_b):
        import jax, jax.numpy as jnp
        import numpy as np
        B, H, D, K, F = (8, 16, 128, 64, 512)
        N, S = (4, 512)
        LN_EPS = 1e-06

        def _layer_norm(x, scale, bias):
            m = jnp.mean(x, axis=-1, keepdims=True)
            v = jnp.mean(jnp.square(x - m), axis=-1, keepdims=True)
            return (x - m) * jax.lax.rsqrt(v + LN_EPS) * scale + bias

        def _feature_map(x):
            return jax.nn.elu(x) + 1.0
        n, s, _ = x.shape
        for i in range(B):
            residual = x
            Q = _feature_map(jnp.einsum('nsd,hdk->nshk', x, Wq[i]) + bq[i])
            Kf = _feature_map(jnp.einsum('nsd,hdk->nshk', x, Wk[i]) + bk[i])
            V = jnp.einsum('nsd,hdk->nshk', x, Wv[i]) + bv[i]
            KV = jnp.sum(Kf * V, axis=1)
            sumK = jnp.sum(Kf, axis=1)
            Z = 1.0 / (Q * sumK[:, None] + 1e-06)
            att = Q * KV[:, None] * Z
            att = att.reshape(n, s, H * K)
            y = jax.nn.gelu(att @ Wo[i] + bo[i])
            x = _layer_norm(y + residual, ln1_s[i], ln1_b[i])
            residual = x
            h = jax.nn.gelu(x @ W1[i] + b1[i])
            h = jax.nn.gelu(h @ W2[i] + b2[i])
            x = _layer_norm(h + residual, ln2_s[i], ln2_b[i])
        return x

    def _L0_ffn_ref(x, gw, gb, w1, b1, w3, b3, w2, b2, sw1, sb1, sw3, sb3, sw2, sb2):
        import jax, jax.numpy as jnp
        import numpy as np
        DIM = 128
        INTER = 64
        E = 32
        TOPK = 4
        GROUPS = 8
        TOPK_GROUPS = 4
        SHARED_INTER = 2 * INTER
        ROUTE_SCALE = 1.0
        B, S = (8, 512)

        def _gate(xf, gw, gb):
            T = xf.shape[0]
            scores = jax.nn.softmax((xf @ gw + gb).astype(jnp.float32), axis=-1)
            original_scores = scores
            scores_g = scores.reshape(T, GROUPS, E // GROUPS)
            group_scores = jnp.sum(jax.lax.top_k(scores_g, 2)[0], axis=-1)
            gidx = jax.lax.top_k(group_scores, TOPK_GROUPS)[1]
            keep = jnp.zeros((T, GROUPS), bool).at[jnp.arange(T)[:, None], gidx].set(True)
            masked = jnp.where(keep[:, :, None], scores_g, -jnp.inf).reshape(T, E)
            indices = jax.lax.top_k(masked, TOPK)[1]
            weights = jnp.take_along_axis(original_scores, indices, axis=1) * ROUTE_SCALE
            return (weights.astype(xf.dtype), indices)
        shape = x.shape
        xf = x.reshape(-1, DIM)
        T = xf.shape[0]
        weights, indices = _gate(xf, gw, gb)
        cw = jnp.zeros((T, E), xf.dtype).at[jnp.arange(T)[:, None], indices].add(weights)

        def body(y, p):
            w1e, b1e, w3e, b3e, w2e, b2e, we = p
            h = jax.nn.silu(xf @ w1e + b1e) * (xf @ w3e + b3e)
            return (y + we[:, None] * (h @ w2e + b2e), None)
        y0 = jnp.zeros_like(xf)
        y, _ = jax.lax.scan(body, y0, (w1, b1, w3, b3, w2, b2, cw.T))
        z = jax.nn.silu(xf @ sw1 + sb1) * (xf @ sw3 + sb3) @ sw2 + sb2
        return (y + z).reshape(shape)
    x = L0_attn_x
    xn = _layernorm(x, axis=-1)
    s = _L0_attn_ref(xn, L0_attn_Wq, L0_attn_bq, L0_attn_Wk, L0_attn_bk, L0_attn_Wv, L0_attn_bv, L0_attn_Wo, L0_attn_bo, L0_attn_ln1_s, L0_attn_ln1_b, L0_attn_W1, L0_attn_b1, L0_attn_W2, L0_attn_b2, L0_attn_ln2_s, L0_attn_ln2_b)
    g = _silu(_L0_ffn_ref(xn, L0_ffn_gw, L0_ffn_gb, L0_ffn_w1, L0_ffn_b1, L0_ffn_w3, L0_ffn_b3, L0_ffn_w2, L0_ffn_b2, L0_ffn_sw1, L0_ffn_sb1, L0_ffn_sw3, L0_ffn_sb3, L0_ffn_sw2, L0_ffn_sb2))
    x = x + s * g
    return x

_drawn_inputs = setup_inputs


def setup_inputs(seed=0):
    import zlib

    import numpy as np

    out = dict(_drawn_inputs(seed))
    spreads = {'L0_attn_bq': (0.0, 2.0),
     'L0_attn_bk': (0.0, 2.0),
     'L0_attn_bv': (0.0, 0.276),
     'L0_attn_bo': (0.0, 0.1),
     'L0_attn_ln1_s': (1.0, 0.2),
     'L0_attn_ln1_b': (0.0, 0.1),
     'L0_attn_b1': (0.0, 0.743),
     'L0_attn_b2': (0.0, 0.1),
     'L0_attn_ln2_s': (1.0, 0.2),
     'L0_attn_ln2_b': (0.0, 0.1),
     'L0_ffn_gb': (0.0, 0.413),
     'L0_ffn_b1': (0.0, 0.784),
     'L0_ffn_b3': (0.0, 0.8),
     'L0_ffn_b2': (0.0, 0.482),
     'L0_ffn_sb1': (0.0, 0.1),
     'L0_ffn_sb3': (0.0, 0.1),
     'L0_ffn_sb2': (0.0, 0.1)}
    factors = {'L0_attn_Wq': 64.0, 'L0_attn_Wk': 8.0, 'L0_attn_Wv': 2.955}
    for name, (base, spread) in spreads.items():
        noise = np.random.default_rng([zlib.crc32(name.encode()), seed]).standard_normal(out[name].shape)
        drawn = base * np.exp(spread * noise) if base else spread * noise
        out[name] = jnp.asarray(drawn.astype(out[name].dtype))
    for name, factor in factors.items():
        out[name] = (out[name] * factor).astype(out[name].dtype)
    return out
```

```python
from contextlib import ExitStack

import numpy as np

import concourse.bass as bass
from concourse import mybir

ALU = mybir.AluOpType
ACT = mybir.ActivationFunctionType
AXX = mybir.AxisListType.X
F32 = mybir.dt.float32
F32R = mybir.dt.float32r

P = 128
LN_EPS = 1e-6
Z_EPS = 1e-6
IN_EPS = 1e-5
TINY = 1e-38
EXP_LN = "natural_log_exp_and_others"


def at_least(engine, semaphore, value):
    if isinstance(value, int) and value <= 0:
        return
    engine.wait_ge(semaphore, value)


def over(ap, axis, shape):
    return ap.unsqueeze(axis).broadcast_to(shape)


def recurrent_attention_gated_by_experts(nc: bass.Bass, t: dict, out: bass.AP):
    x_in = t["L0_attn_x"]
    SEQS, S, D = x_in.shape
    LAYERS, HEADS, _, HK = t["L0_attn_Wq"].shape
    FF = t["L0_attn_W1"].shape[2]
    EXPERTS, _, INTER = t["L0_ffn_w1"].shape
    T = SEQS * S
    TB = T // P
    CB = HEADS * HK // P
    FB = FF // P
    PAIRS = EXPERTS // 2
    N = 512
    CHUNKS = T // N
    GROUPS, PER_GROUP, TOP_GROUPS, TOP = 8, EXPERTS // 8, 4, 4
    STAGES = SEQS * LAYERS
    assert D == P and SEQS == 2 and S == 2 * N and 2 * INTER == P and CB == 8 and FB == 4

    x_tokens = x_in.rearrange("n s d -> (n s) d").rearrange("(b p) d -> p b d", p=P)
    out_tokens = out.rearrange("n s d -> (n s) d").rearrange("(b p) d -> p b d", p=P)
    weights_by_pair = nc.dram_tensor("expert_weights", [EXPERTS, T], F32, kind="Internal").ap()

    with ExitStack() as whole:
        def sb(name, shape, dtype=F32, ctx=whole):
            return ctx.enter_context(nc.sbuf_tensor(name, shape, dtype))

        def sem(name, ctx=whole):
            return ctx.enter_context(nc.semaphore(name))

        ident = sb("ident", [P, P])
        centre = sb("centre", [P, P])
        average = sb("average", [P, P])
        ones = sb("ones", [P, 2])
        ln_eps = sb("ln_eps", [P, 1])
        x = sb("x", [P, TB, P])
        res = sb("res", [P, SEQS, S])
        res_h = sb("res_h", [P, SEQS, S], F32R)
        res_l = sb("res_l", [P, SEQS, S], F32R)
        gate = sb("gate", [P, T])
        rows_qk = sb("rows_qk", [P, P])
        rows_v1 = sb("rows_v1", [P, P])
        rows_misc = sb("rows_misc", [P, P])
        NF, NG = 5 * CB, FB + 6
        table_f = sb("table_f", [P, LAYERS, 5, CB])
        table_g = sb("table_g", [P, LAYERS, NG])
        moe_b13 = sb("moe_b13", [P, PAIRS + 1, 2])
        moe_sb2 = sb("moe_sb2", [P, 1])
        cwT = sb("cwT", [EXPERTS, T])

        with ExitStack() as c:
            gw = sb("gw", [P, EXPERTS], F32, c)
            gb = sb("gb", [P, EXPERTS], F32, c)
            xc = sb("xc", [P, TB, P], F32, c)
            sq = sb("sq", [P, TB, P], F32, c)
            mean = sb("mean", [P, TB], F32, c)
            var = sb("var", [P, TB], F32, c)
            root = sb("root", [P, TB], F32, c)
            rstd = sb("rstd", [P, TB], F32, c)
            corr = sb("corr", [P, TB], F32, c)
            lg = sb("lg", [P, TB, EXPERTS], F32, c)
            prob = sb("prob", [P, TB, EXPERTS], F32, c)
            col = sb("col", [P, TB], F32, c)
            tot = sb("tot", [P, TB], F32, c)
            hi2 = sb("hi2", [P, TB * GROUPS, 2], F32, c)
            lo2 = sb("lo2", [P, TB * GROUPS, 2], F32, c)
            first = sb("first", [P, TB * GROUPS], F32, c)
            second = sb("second", [P, TB * GROUPS], F32, c)
            score = sb("score", [P, TB, GROUPS], F32, c)
            above = sb("above", [P, TB, GROUPS, GROUPS], F32, c)
            equal = sb("equal", [P, TB, GROUPS, GROUPS], F32, c)
            earlier = sb("earlier", [P, GROUPS, GROUPS], F32, c)
            keep = sb("keep", [P, TB, GROUPS], F32, c)
            drop = sb("drop", [P, TB, GROUPS], F32, c)
            masked = sb("masked", [P, TB, EXPERTS], F32, c)
            best = sb("best", [P, TB, 8], F32, c)
            more = sb("more", [P, TB, EXPERTS], F32, c)
            tie = [sb(f"tie{k}", [P, TB, 2 * EXPERTS], F32, c) for k in range(2)]
            cw = sb("cw", [P, TB, EXPERTS], F32, c)
            ps = [c.enter_context(nc.psum_tensor(f"ps{k}", [P, N], F32)) for k in range(8)]

            x_in_sem, rows_in, gate_in = sem("x_loaded", c), sem("rows_loaded", c), sem("gate_weights_loaded", c)
            consts = sem("constants_ready", c)
            turned = sem("transposed", c)
            dve = sem("vector_steps", c)
            root_ready, exp_ready = sem("root_ready", c), sem("exp_ready", c)
            columns_ready = sem("weights_transposed", c)
            stored = sem("expert_weights_stored", c)

            block = c.enter_context(nc.Block())
            ROWS = []
            r = 0
            for name, tile in (("L0_attn_bq", rows_qk), ("L0_attn_bk", rows_qk)):
                ROWS.append((tile, r, t[name].rearrange("l h k -> l (h k)").rearrange("l (c p) -> (l c) p", p=P)))
                r += LAYERS * CB
            r = 0
            for ap in (t["L0_attn_bv"].rearrange("l h k -> l (h k)").rearrange("l (c p) -> (l c) p", p=P),
                       t["L0_attn_b1"].rearrange("l (c p) -> (l c) p", p=P),
                       t["L0_ffn_b1"].rearrange("e k -> (e k)").rearrange("(r p) -> r p", p=P),
                       t["L0_ffn_b3"].rearrange("e k -> (e k)").rearrange("(r p) -> r p", p=P)):
                ROWS.append((rows_v1, r, ap))
                r += ap.shape[0]
            r = 0
            for name in ("bo", "b2", "ln1_s", "ln1_b", "ln2_s", "ln2_b"):
                ROWS.append((rows_misc, r, t[f"L0_attn_{name}"]))
                r += LAYERS
            for name in ("sb1", "sb3", "sb2"):
                ROWS.append((rows_misc, r, t[f"L0_ffn_{name}"].rearrange("(r p) -> r p", p=P)))
                r += 1
            MISC = r

            mark = {}

            @block.vector
            def _(v):
                n = [0]

                def done(ins, name=None):
                    ins.then_inc(dve, 1)
                    n[0] += 1
                    if name:
                        mark[name] = n[0]
                    v.wait_ge(dve, n[0])

                def tt(o, a, b, op, name=None):
                    done(v.tensor_tensor(o, a, b, op), name)

                def ts(o, a, s1, s2, op0, op1=ALU.bypass, name=None):
                    done(v.tensor_scalar(o, a, s1, s2, op0, op1), name)

                wide = [P, TB, P]
                v.wait_ge(consts, 10)
                v.wait_ge(x_in_sem, 64)
                done(v.tensor_reduce(mean[:, :], x[:, :, :], AXX, ALU.add))
                ts(mean[:, :], mean[:, :], 1.0 / P, None, ALU.mult)
                tt(xc[:, :, :], x[:, :, :], over(mean[:, :], 2, wide), ALU.subtract)
                tt(sq[:, :, :], xc[:, :, :], xc[:, :, :], ALU.mult)
                done(v.tensor_reduce(var[:, :], sq[:, :, :], AXX, ALU.add))
                ts(var[:, :], var[:, :], 1.0 / P, IN_EPS, ALU.mult, ALU.add, name="var")
                v.wait_ge(root_ready, 1)
                done(v.reciprocal(rstd[:, :], root[:, :]))
                tt(corr[:, :], rstd[:, :], rstd[:, :], ALU.mult)
                tt(corr[:, :], corr[:, :], var[:, :], ALU.mult)
                ts(corr[:, :], corr[:, :], -0.5, 1.5, ALU.mult, ALU.add)
                tt(rstd[:, :], rstd[:, :], corr[:, :], ALU.mult)
                tt(xc[:, :, :], xc[:, :, :], over(rstd[:, :], 2, wide), ALU.mult, name="normed")
                done(v.tensor_scalar(centre[:, :], ident[:, :], -1.0 / P, None, ALU.add))
                v.wait_ge(turned, 1)
                rows = ps[0]
                qk = rows[:, 0:P].rearrange("p (m l c) -> p l m c", m=2, c=CB)
                done(v.tensor_copy(table_f[:, :, 0:2, :], qk))
                ts(table_f[:, :, 2:4, :], table_f[:, :, 0:2, :], 1.0, None, ALU.add)
                at = P
                done(v.tensor_copy(table_f[:, :, 4, :], rows[:, at:at + LAYERS * CB].rearrange("p (l c) -> p l c", c=CB)))
                at += LAYERS * CB
                done(v.tensor_copy(table_g[:, :, 6:6 + FB], rows[:, at:at + LAYERS * FB].rearrange("p (l c) -> p l c", c=FB)))
                at += LAYERS * FB
                done(v.tensor_copy(moe_b13[:, 0:PAIRS, 0], rows[:, at:at + PAIRS]))
                at += PAIRS
                done(v.tensor_copy(moe_b13[:, 0:PAIRS, 1], rows[:, at:at + PAIRS]))
                at += PAIRS
                done(v.tensor_copy(table_g[:, :, 0:6], rows[:, at:at + 6 * LAYERS].rearrange("p (k l) -> p l k", l=LAYERS)))
                at += 6 * LAYERS
                done(v.tensor_copy(moe_b13[:, PAIRS, :], rows[:, at:at + 2]))
                done(v.tensor_copy(moe_sb2[:, :], rows[:, at + 2:at + 3]))
                for q in range(CHUNKS):
                    s, h = q // 2, q % 2 * N
                    v.wait_ge(turned, 2 + q)
                    done(v.tensor_copy(res[:, s, h:h + N], ps[1 + q][:, :]), f"state{q}")
                for s in range(SEQS):
                    done(v.tensor_copy(res_h[:, s, :], res[:, s, :]))
                    tt(res_l[:, s, :], res[:, s, :], res_h[:, s, :].bitcast(F32), ALU.subtract)
                per = [P, TB, EXPERTS]
                v.wait_ge(turned, 2 + CHUNKS)
                v.wait_ge(gate_in, 32)
                logits = ps[5][:, :].rearrange("p (b e) -> p b e", e=EXPERTS)
                tt(lg[:, :, :], logits, over(gb[:, :], 1, per), ALU.add)
                done(v.tensor_reduce(col[:, :], lg[:, :, :], AXX, ALU.max))
                tt(lg[:, :, :], lg[:, :, :], over(col[:, :], 2, per), ALU.subtract, name="logits")
                v.wait_ge(exp_ready, 1)
                done(v.tensor_reduce(tot[:, :], prob[:, :, :], AXX, ALU.add))
                done(v.reciprocal(tot[:, :], tot[:, :]))
                tt(prob[:, :, :], prob[:, :, :], over(tot[:, :], 2, per), ALU.mult)
                fours = prob[:, :, :].rearrange("p b (g k) -> p (b g) k", k=PER_GROUP)
                tt(hi2[:, :, :], fours[:, :, 0:2], fours[:, :, 2:4], ALU.max)
                tt(lo2[:, :, :], fours[:, :, 0:2], fours[:, :, 2:4], ALU.min)
                tt(first[:, :], hi2[:, :, 0], hi2[:, :, 1], ALU.max)
                tt(second[:, :], hi2[:, :, 0], hi2[:, :, 1], ALU.min)
                tt(lo2[:, :, 0], lo2[:, :, 0], lo2[:, :, 1], ALU.max)
                tt(second[:, :], second[:, :], lo2[:, :, 0], ALU.max)
                tt(score[:, :, :].rearrange("p b g -> p (b g)"), first[:, :], second[:, :], ALU.add)
                by = [P, TB, GROUPS, GROUPS]
                theirs, own = over(score[:, :, :], 2, by), over(score[:, :, :], 3, by)
                tt(above[:, :, :, :], theirs, own, ALU.is_gt)
                tt(equal[:, :, :, :], theirs, own, ALU.is_equal)
                tt(equal[:, :, :, :], equal[:, :, :, :], over(earlier[:, :, :], 1, by), ALU.mult)
                tt(above[:, :, :, :], above[:, :, :, :], equal[:, :, :, :], ALU.add)
                done(v.tensor_reduce(keep[:, :, :], above[:, :, :, :], AXX, ALU.add))
                ts(keep[:, :, :], keep[:, :, :], float(TOP_GROUPS), None, ALU.is_lt)
                ts(drop[:, :, :], keep[:, :, :], -1.0, None, ALU.add)
                m4 = masked[:, :, :].rearrange("p b (g k) -> p (b g) k", k=PER_GROUP)
                grp = [P, TB * GROUPS, PER_GROUP]
                tt(m4, fours, over(keep[:, :, :].rearrange("p b g -> p (b g)"), 2, grp), ALU.mult)
                tt(m4, m4, over(drop[:, :, :].rearrange("p b g -> p (b g)"), 2, grp), ALU.add)
                for b in range(TB):
                    done(v.max(best[:, b, :], masked[:, b, :]))
                least = best[:, :, TOP - 1:TOP].broadcast_to(per)
                real = slice(EXPERTS, 2 * EXPERTS)
                tt(more[:, :, :], masked[:, :, :], least, ALU.is_gt)
                tt(tie[0][:, :, real], masked[:, :, :], least, ALU.is_equal)
                tt(cw[:, :, :], masked[:, :, :], least, ALU.is_equal)
                done(v.tensor_reduce(col[:, :], more[:, :, :], AXX, ALU.add))
                ts(col[:, :], col[:, :], -1.0, float(TOP), ALU.mult, ALU.add)
                k, a = 1, 0
                while k < EXPERTS:
                    tt(tie[1 - a][:, :, real], tie[a][:, :, real],
                       tie[a][:, :, EXPERTS - k:2 * EXPERTS - k], ALU.add)
                    k, a = 2 * k, 1 - a
                tt(lg[:, :, :], tie[a][:, :, real], over(col[:, :], 2, per), ALU.is_le)
                tt(cw[:, :, :], cw[:, :, :], lg[:, :, :], ALU.mult)
                tt(cw[:, :, :], cw[:, :, :], more[:, :, :], ALU.add)
                tt(cw[:, :, :], cw[:, :, :], prob[:, :, :], ALU.mult, name="weights")

            @block.sync
            def _(sp):
                for q in range(4):
                    sp.dma_start(x[:, 4 * q:4 * q + 4, :], x_tokens[:, 4 * q:4 * q + 4, :]).then_inc(x_in_sem, 16)
                sp.dma_start(gw[:, :], t["L0_ffn_gw"]).then_inc(gate_in, 16)
                sp.dma_start(gb[:, :], t["L0_ffn_gb"].rearrange("(a e) -> a e", a=1).broadcast_to([P, EXPERTS]))\
                    .then_inc(gate_in, 16)
                sp.wait_ge(columns_ready, CHUNKS)
                sp.dma_start(weights_by_pair, cwT[:, :]).then_inc(stored, 16)
                sp.wait_ge(stored, 16)

            @block.gpsimd
            def _(pool):
                pool.memset(ident[:, :], 0.0).then_inc(consts, 1)
                pool.memset(average[:, :], 1.0 / P).then_inc(consts, 1)
                pool.memset(ones[:, :], 1.0).then_inc(consts, 1)
                pool.memset(ln_eps[:, :], LN_EPS).then_inc(consts, 1)
                pool.memset(earlier[:, :, :], 1.0).then_inc(consts, 1)
                pool.memset(rows_misc[:, :], 0.0).then_inc(consts, 1)
                for k in range(2):
                    pool.memset(tie[k][:, :, :], 0.0).then_inc(consts, 1)
                pool.wait_ge(consts, 8)
                pool.affine_select(out=ident[:, :], in_=ident[:, :], compare_op=ALU.not_equal, fill=1.0, base=0,
                                   pattern=[[-1, P]], channel_multiplier=1).then_inc(consts, 1)
                pool.affine_select(out=earlier[:, :, :], in_=earlier[:, :, :], compare_op=ALU.is_gt, fill=0.0,
                                   base=0, pattern=[[1, GROUPS], [-1, GROUPS]], channel_multiplier=0)\
                    .then_inc(consts, 1)

            @block.scalar
            def _(sc):
                sc.wait_ge(consts, 8)
                for tile, row, ap in ROWS:
                    sc.dma_start(tile[row:row + ap.shape[0], :], ap).then_inc(rows_in, 16)
                sc.wait_ge(dve, mark["var"])
                sc.activation(root[:, :], var[:, :], ACT.Sqrt).then_inc(root_ready, 1)
                sc.wait_ge(dve, mark["logits"])
                sc.activation(prob[:, :, :], lg[:, :, :], ACT.Exp).then_inc(exp_ready, 1)
                for q in range(CHUNKS):
                    sc.wait_ge(turned, 3 + CHUNKS + q)
                    sc.activation(cwT[:, q * N:(q + 1) * N], ps[q if q else 6][0:EXPERTS, :], ACT.Copy)\
                        .then_inc(columns_ready, 1)

            @block.tensor
            def _(pe):
                pe.wait_ge(consts, 9)
                pe.wait_ge(rows_in, 16 * len(ROWS))
                pe.transpose(ps[0][:, 0:P], rows_qk[:, :], ident[:, :])
                pe.transpose(ps[0][:, P:2 * P], rows_v1[:, :], ident[:, :])
                pe.transpose(ps[0][:, 2 * P:3 * P], rows_misc[:, :], ident[:, :]).then_inc(turned, 1)
                pe.wait_ge(dve, mark["normed"])
                for q in range(CHUNKS):
                    for b in range(4):
                        ins = pe.transpose(ps[1 + q][:, b * P:(b + 1) * P], xc[:, 4 * q + b, :], ident[:, :])
                    ins.then_inc(turned, 1)
                pe.wait_ge(gate_in, 32)
                pe.wait_ge(dve, mark[f"state{CHUNKS - 1}"])
                for b in range(TB):
                    ins = pe.matmul(ps[5][:, b * EXPERTS:(b + 1) * EXPERTS],
                                    res[:, b // 8, (b % 8) * P:(b % 8 + 1) * P], gw[:, :], start=True, stop=True)
                ins.then_inc(turned, 1)
                pe.wait_ge(dve, mark["weights"])
                for q in range(CHUNKS):
                    for b in range(4):
                        ins = pe.transpose(ps[q if q else 6][0:EXPERTS, b * P:(b + 1) * P], cw[:, 4 * q + b, :],
                                           ident[:, :])
                    ins.then_inc(turned, 1)

        with ExitStack() as c:
            raw = [sb(f"expert_raw{k}", [P, 2, P], F32, c) for k in range(2)]
            w13_h = [sb(f"w13_h{k}", [P, 2, P], F32R, c) for k in range(2)]
            w13_l = [sb(f"w13_l{k}", [P, 2, P], F32R, c) for k in range(2)]
            w2 = [sb(f"w2_{k}", [P, P], F32, c) for k in range(2)]
            b13 = [sb(f"b13_{k}", [P, 2], F32, c) for k in range(2)]
            share = [sb(f"share{k}", [P, T], F32, c) for k in range(2)]
            b2 = sb("experts_b2", [EXPERTS, P], F32, c)
            act_a = [sb(f"act_a{k}", [P, N], F32, c) for k in range(2)]
            prod = [sb(f"prod{k}", [P, N], F32, c) for k in range(2)]
            hid = [sb(f"hid{k}", [P, N], F32, c) for k in range(2)]
            y = [c.enter_context(nc.psum_tensor(f"y{q}", [P, N], F32)) for q in range(CHUNKS)]
            a_ps = [c.enter_context(nc.psum_tensor(f"a_ps{k}", [P, N], F32)) for k in range(2)]
            c_ps = [c.enter_context(nc.psum_tensor(f"c_ps{k}", [P, N], F32)) for k in range(2)]

            b2_in = sem("b2_loaded", c)
            raw_in = [sem(f"w13_loaded{k}", c) for k in range(2)]
            w2_in = [sem(f"w2_loaded{k}", c) for k in range(2)]
            share_in = [sem(f"share_loaded{k}", c) for k in range(2)]
            bias_placed = sem("bias_placed", c)
            upper_ready, split_ready = sem("w13_upper_ready", c), sem("w13_split", c)
            up_ready = sem("a_and_c_ready", c)
            silu_ready = sem("silu_ready", c)
            prod_ready = sem("product_ready", c)
            hid_ready = sem("hidden_ready", c)
            down_done = sem("hidden_used", c)
            gate_ready = sem("gate_ready", c)

            block = c.enter_context(nc.Block())
            LOOPS = PAIRS // 2
            w1d, w3d, w2d = (t[f"L0_ffn_{n}"] for n in ("w1", "w3", "w2"))

            @block.sync
            def _(sp):
                def load(pair, k, used):
                    at_least(sp, split_ready, used[0])
                    for m, w in enumerate((w1d, w3d)):
                        sp.dma_start(raw[k][:, m, :].rearrange("d (e k) -> d e k", e=2),
                                     w[bass.ds(2 * pair, 2), :, :].rearrange("e d k -> d e k")).then_inc(raw_in[k], 16)
                    at_least(sp, down_done, used[1])
                    sp.dma_start(w2[k][:, :], w2d[bass.ds(2 * pair, 2), :, :].rearrange("e k d -> (e k) d"))\
                        .then_inc(w2_in[k], 16)
                    at_least(sp, hid_ready, used[1])
                    for e in range(2):
                        sp.dma_start(share[k][e * INTER:(e + 1) * INTER, :],
                                     weights_by_pair[bass.ds(2 * pair + e, 1), :].broadcast_to([INTER, T]))\
                            .then_inc(share_in[k], 16)

                sp.dma_start(b2[:, :], t["L0_ffn_b2"]).then_inc(b2_in, 16)
                load(0, 0, (0, 0))
                load(1, 1, (0, 0))
                with sp.Fori(0, LOOPS - 1) as i:
                    load(2 * i + 2, 0, (2 * i + 1, 8 * i + 4))
                    load(2 * i + 3, 1, (2 * i + 2, 8 * i + 8))
                sp.wait_ge(split_ready, PAIRS - 1)
                sp.dma_start(raw[0][:, 0, :], t["L0_ffn_sw1"]).then_inc(raw_in[0], 16)
                sp.dma_start(raw[0][:, 1, :], t["L0_ffn_sw3"]).then_inc(raw_in[0], 16)
                sp.wait_ge(down_done, 4 * PAIRS - 4)
                sp.dma_start(w2[0][:, :], t["L0_ffn_sw2"]).then_inc(w2_in[0], 16)

            @block.tensor
            def _(pe):
                def up(k, q, n, w_first):
                    if q == 0:
                        pe.wait_ge(split_ready, w_first)
                    s, h = q // 2, slice(q % 2 * N, q % 2 * N + N)
                    for m, bank in enumerate((a_ps[q % 2], c_ps[q % 2])):
                        pe.matmul(bank[:, :], w13_h[k][:, m, :], res_h[:, s, h], start=True, stop=False)
                        pe.matmul(bank[:, :], w13_h[k][:, m, :], res_l[:, s, h], start=False, stop=False)
                        ins = pe.matmul(bank[:, :], w13_l[k][:, m, :], res_h[:, s, h], start=False, stop=True)
                    ins.then_inc(up_ready, 1)

                def down(k, q, n, loads, last=False):
                    if q == 0:
                        pe.wait_ge(w2_in[k], 16 * loads)
                    pe.wait_ge(prod_ready if last else hid_ready, n + 1)
                    pe.matmul(y[q][:, :], w2[k][:, :], hid[q % 2][:, :], start=False, stop=last).then_inc(down_done, 1)

                pe.wait_ge(b2_in, 16)
                for q in range(CHUNKS):
                    pe.matmul(y[q][:, :], b2[:, :], cwT[:, q * N:(q + 1) * N], start=True, stop=False)
                up(0, 0, 0, 1)
                with pe.Fori(0, LOOPS) as i:
                    for m in range(8):
                        k1, q1 = (m + 1) // 4 % 2, (m + 1) % 4
                        up(k1, q1, 8 * i + m + 1, 2 * i + 1 + (m + 1) // 4)
                        down(m // 4, m % 4, 8 * i + m, i + 1)
                for q in range(CHUNKS):
                    if q < 3:
                        up(0, q + 1, 4 * PAIRS + q + 1, PAIRS + 1)
                    down(0, q, 4 * PAIRS + q, LOOPS + 1, last=True)

            @block.scalar
            def _(sc):
                def silu(k, q, n, pair):
                    if q == 0:
                        sc.wait_ge(split_ready, pair + 1)
                    sc.wait_ge(up_ready, n + 1)
                    sc.activation(act_a[q % 2][:, :], a_ps[q % 2][:, :], ACT.Silu,
                                  bias=b13[k][:, 0:1]).then_inc(silu_ready, 1)

                with sc.Fori(0, LOOPS) as i:
                    for m in range(8):
                        silu(m // 4, m % 4, 8 * i + m, 2 * i + m // 4)
                for q in range(CHUNKS):
                    silu(0, q, 4 * PAIRS + q, PAIRS)
                for q in range(CHUNKS):
                    if q == 0:
                        sc.wait_ge(down_done, 4 * PAIRS + CHUNKS)
                    sc.activation(gate[:, q * N:(q + 1) * N], y[q][:, :], ACT.Silu, bias=moe_sb2[:, 0:1])\
                        .then_inc(gate_ready, 1)

            @block.vector
            def _(v):
                def split(k, pair, loads):
                    v.wait_ge(raw_in[k], 32 * loads)
                    at_least(v, up_ready, 4 * (pair - 1))
                    v.tensor_scalar(b13[k][:, :], moe_b13[:, bass.ds(pair, 1), :].rearrange("p l k -> p (l k)"), 0.0, None,
                                    ALU.add).then_inc(bias_placed, 1)
                    v.wait_ge(bias_placed, pair + 1)
                    v.tensor_copy(w13_h[k][:, :, :], raw[k][:, :, :]).then_inc(upper_ready, 1)
                    v.wait_ge(upper_ready, pair + 1)
                    v.tensor_tensor(w13_l[k][:, :, :], raw[k][:, :, :], w13_h[k][:, :, :].bitcast(F32),
                                    ALU.subtract).then_inc(split_ready, 1)

                def product(q, n, k, loads, shared=False):
                    v.wait_ge(silu_ready, n + 1)
                    o = hid[q % 2] if shared else prod[q % 2]
                    v.scalar_tensor_tensor(out=o[:, :], in0=c_ps[q % 2][:, :], scalar=b13[k][:, 1:2],
                                           in1=act_a[q % 2][:, :], op0=ALU.add, op1=ALU.mult)\
                        .then_inc(prod_ready, 1)
                    if shared:
                        return
                    v.wait_ge(prod_ready, n + 1)
                    if q == 0:
                        v.wait_ge(share_in[k], 32 * loads)
                    v.tensor_tensor(hid[q % 2][:, :], o[:, :], share[k][:, q * N:(q + 1) * N], ALU.mult)\
                        .then_inc(hid_ready, 1)

                split(0, 0, 1)
                with v.Fori(0, LOOPS) as i:
                    for m in range(8):
                        if m == 0:
                            split(1, 2 * i + 1, i + 1)
                        product(m % 4, 8 * i + m, m // 4, i + 1)
                        if m == 5:
                            split(0, 2 * i + 2, i + 2)
                for q in range(CHUNKS):
                    product(q, 4 * PAIRS + q, 0, 0, shared=True)

        with ExitStack() as c:
            raw = [sb(f"qkv_raw{g}", [P, 3, S // 2], F32, c) for g in range(2)]
            wh = [sb(f"qkv_h{g}", [P, 3, S // 2], F32R, c) for g in range(2)]
            wl = [sb(f"qkv_l{g}", [P, 3, S // 2], F32R, c) for g in range(2)]
            wo = [sb(f"wo{g}", [P, 4, P], F32, c) for g in range(2)]
            wg = [sb(f"wo_scaled{s}", [P, CB, P], F32, c) for s in range(SEQS)]
            w1 = sb("ff1", [P, FF], F32, c)
            w2 = sb("ff2", [P, FB, P], F32, c)
            par_f = [sb(f"par_f{s}", [P, 5, CB], F32, c) for s in range(SEQS)]
            par_g = [sb(f"par_g{s}", [P, NG], F32, c) for s in range(SEQS)]
            ek, eq = sb("exp_k", [P, S], F32, c), sb("exp_q", [P, S], F32, c)
            phi_k = sb("phi_k", [P, S], F32, c)
            phi_q = [sb(f"phi_q{k}", [P, S], F32, c) for k in range(2)]
            lnq = sb("ln_q", [P, S], F32, c)
            miss = [sb(f"miss{k}", [P, S], F32, c) for k in range(2)]
            sum_k = [sb(f"sum_k{k}", [P, 1], F32, c) for k in range(2)]
            sum_kv = [sb(f"sum_kv{k}", [P, 1], F32, c) for k in range(2)]
            scale = [sb(f"scale{k}", [P, 1], F32, c) for k in range(2)]
            inv = [sb(f"inv{k}", [P, 1], F32, c) for k in range(2)]
            mean_v = [sb(f"mean_v{k}", [P, 1], F32, c) for k in range(2)]
            bias_y = sb("bias_y", [P, 1], F32, c)
            g_act = sb("g_act", [P, S], F32, c)
            r_sum = sb("r_sum", [P, S], F32, c)
            centred = sb("centred", [P, S], F32, c)
            square = sb("square", [P, S], F32, c)
            rstd = sb("rstd_t", [P, S], F32, c)
            mid = sb("mid", [P, S], F32, c)
            hid = sb("hidden", [P, FB, S], F32, c)

            z = [c.enter_context(nc.psum_tensor(f"z{k}", [P, S], F32)) for k in range(2)]
            yp = c.enter_context(nc.psum_tensor("yp", [P, S], F32))
            gp = c.enter_context(nc.psum_tensor("gp", [P, S], F32))

            raw_in = [sem(f"qkv_loaded{g}", c) for g in range(2)]
            wo_in = [sem(f"wo_loaded{g}", c) for g in range(2)]
            ff_in = sem("ff_loaded", c)
            w_upper, w_split = [[sem(f"{n}{g}", c) for g in range(2)] for n in ("qkv_upper_ready", "qkv_split")]
            z_ready = sem("z_ready", c)
            wo_done = sem("wo_done", c)
            exp_done = sem("exp_done", c)
            ln_done, miss_ready = sem("ln_done", c), sem("miss_ready", c)
            capped = sem("capped", c)
            phi_done = sem("phi_done", c)
            phi_q_ready = sem("phi_q_ready", c)
            kv_done = sem("kv_done", c)
            scale_ready, guarded, inv_ready = sem("scale_ready", c), sem("sum_guarded", c), sem("inverse_ready", c)
            mean_v_ready, wg_ready = sem("mean_v_ready", c), sem("wo_scaled_ready", c)
            par_f_ready, par_g_ready = sem("par_f_ready", c), sem("par_g_ready", c)
            const_ready, bias_ready = sem("constant_ready", c), sem("bias_ready", c)
            gelu_y = sem("gelu_y_ready", c)
            sum_ready = sem("residual_added", c)
            centred_ready, copied, squared, var_ready = (sem(n, c) for n in (
                "centred_ready", "centred_copied", "squared", "variance_ready"))
            ln_var, rstd_ready, normed = sem("ln_variance", c), sem("rstd_ready", c), sem("normed", c)
            state_ready = sem("state_ready", c)
            state_h, state_l = sem("state_upper_ready", c), sem("state_split", c)
            up_ready, hid_ready = sem("ff_up_ready", c), sem("ff_hidden_ready", c)
            down_ready, gelu_down = sem("ff_down_ready", c), sem("gelu_down_ready", c)

            block = c.enter_context(nc.Block())
            LOOPS = LAYERS - 1
            BO, B2, S1, _, S2, _, FF1 = range(7)


            @block.sync
            def _(sp):
                wq, wk, wv, wod = (t[f"L0_attn_{n}"] for n in ("Wq", "Wk", "Wv", "Wo"))

                def qkv(layer, g):
                    for m, w in enumerate((wk, wv, wq)):
                        heads = w[bass.ds(layer, 1), g * HEADS // 2:(g + 1) * HEADS // 2, :, :]
                        sp.dma_start(raw[g][:, m, :].rearrange("d (h k) -> d h k", k=HK),
                                     heads.rearrange("l h d k -> d (l h) k")).then_inc(raw_in[g], 16)

                def output(layer, g):
                    rows = wod[bass.ds(layer, 1), g * 4 * P:(g + 1) * 4 * P, :]
                    sp.dma_start(wo[g][:, :, :], rows.rearrange("l (c p) d -> p (l c) d", p=P)).then_inc(wo_in[g], 16)

                def ff(layer):
                    sp.dma_start(w1[:, :], t["L0_attn_W1"][bass.ds(layer, 1), :, :].rearrange("l d f -> (l d) f"))\
                        .then_inc(ff_in, 16)
                    sp.dma_start(w2[:, :, :], t["L0_attn_W2"][bass.ds(layer, 1), :, :]
                                 .rearrange("l (c p) d -> p (l c) d", p=P)).then_inc(ff_in, 16)

                for g in range(2):
                    qkv(0, g)
                for g in range(2):
                    output(0, g)
                ff(0)
                with sp.Fori(0, LOOPS) as i:
                    for g in range(2):
                        sp.wait_ge(w_split[g], 3 * (i + 1))
                        qkv(i + 1, g)
                    for g in range(2):
                        sp.wait_ge(wg_ready, 16 * i + 12 + 4 * g)
                        output(i + 1, g)
                    sp.wait_ge(down_ready, 2 * i + 2)
                    ff(i + 1)

            @block.tensor
            def _(pe):
                def project(s, u, j, m):
                    n = 3 * u + m
                    at_least(pe, *((kv_done, u), (phi_done, 2 * u), (phi_done, 2 * u + 1))[m])
                    zt, g = z[(3 * j + m) % 2], j // 4
                    cols = slice(j % 4 * P, j % 4 * P + P)
                    h, l = wh[g][:, m, cols], wl[g][:, m, cols]
                    for k in range(2):
                        at = slice(k * N, (k + 1) * N)
                        pe.matmul(zt[:, at], h, res_h[:, s, at], start=True, stop=False)
                        pe.matmul(zt[:, at], h, res_l[:, s, at], start=False, stop=False)
                        ins = pe.matmul(zt[:, at], l, res_h[:, s, at], start=False, stop=True)
                    ins.then_inc(z_ready, 1)

                def output(s, u, j):
                    pe.wait_ge(miss_ready, u + 1)
                    pe.wait_ge(wg_ready, u + 1)
                    for k in range(2):
                        at = slice(k * N, (k + 1) * N)
                        ins = pe.matmul(yp[:, at], wg[s][:, j, :], miss[j % 2][:, at], start=(j == 0),
                                        stop=(j == CB - 1))
                    ins.then_inc(wo_done, 1)

                def across(matrix, operand, ready):
                    for k in range(2):
                        at = slice(k * N, (k + 1) * N)
                        ins = pe.matmul(gp[:, at], matrix[:, :], operand[:, at], start=True, stop=True)
                    ins.then_inc(ready, 1)

                def up(n, k):
                    b, half = k // 2, k % 2
                    if k < 2:
                        pe.wait_ge(ln_var, 2 * n - 1)
                    else:
                        pe.wait_ge(hid_ready, 8 * (n - 1) + k - 1)
                    at = slice(half * N, (half + 1) * N)
                    pe.matmul(gp[:, at], w1[:, b * P:(b + 1) * P], mid[:, at], start=True, stop=True)\
                        .then_inc(up_ready, 1)

                def stage(n, s, layer=0, following=None, attention=True, rest=True):
                    for j in range(CB):
                        u = 8 * n + j
                        if attention:
                            if s == 0 and j % 4 == 0:
                                pe.wait_ge(w_split[j // 4], 3 * (layer_of(n) + 1))
                            if j == 0:
                                pe.wait_ge(state_l, n + 1)
                            project(s, u, j, 0)
                        if rest and j == 3:
                            pe.wait_ge(squared, 2 * n - 1)
                            pe.wait_ge(copied, 2 * n - 1)
                            across(average, square, var_ready)
                        if rest and j == 4:
                            pe.wait_ge(ff_in, 32 * (layer + 1))
                            pe.wait_ge(state_ready, 2 * n - 1)
                            for k in range(4):
                                up(n, k)
                        if rest and j == 7:
                            pe.wait_ge(squared, 2 * n)
                            pe.wait_ge(copied, 2 * n)
                            across(average, square, var_ready)
                        if attention:
                            project(s, u, j, 1)
                        if rest and j == 2:
                            pe.wait_ge(sum_ready, 2 * n - 1)
                            across(centre, r_sum, centred_ready)
                        if rest and j == 5:
                            pe.wait_ge(hid_ready, 8 * n)
                            for k in range(2):
                                at = slice(k * N, (k + 1) * N)
                                for b in range(FB):
                                    ins = pe.matmul(gp[:, at], w2[:, b, :], hid[:, b, at], start=(b == 0),
                                                    stop=(b == FB - 1))
                            ins.then_inc(down_ready, 1)
                        if rest and j == 6:
                            pe.wait_ge(sum_ready, 2 * n)
                            across(centre, r_sum, centred_ready)
                        if attention:
                            project(s, u, j, 2)
                        if j < 2 and rest:
                            output(1 - s, u - 2, CB - 2 + j)
                        elif j >= 2 and attention:
                            if j == 2:
                                at_least(pe, gelu_y, n)
                            output(s, u - 2, j - 2)
                        if rest and j == 1:
                            for b in range(CB):
                                ins = pe.matmul(gp[:, 0:1], wg[1 - s][:, b, :], ones[:, 0:1], start=(b == 0),
                                                stop=(b == CB - 1))
                            ins.then_inc(const_ready, 1)
                        if rest and j == 4:
                            for k in range(4, 8):
                                up(n, k)

                def layer_of(n):
                    return 0 if isinstance(n, int) else here[0]

                here = [None]
                stage(0, 0, rest=False)
                with pe.Fori(0, LOOPS) as i:
                    here[0] = i + 1
                    stage(2 * i + 1, 1, i)
                    stage(2 * i + 2, 0, i)
                stage(STAGES - 1, 1, LAYERS - 1)
                stage(STAGES, 0, LAYERS - 1, attention=False)

            @block.scalar
            def _(sc):
                def exponent(s, u, j, m, out_tile, read_by):
                    sc.wait_ge(z_ready, 3 * u + m + 1)
                    if j == 0 and m == 0:
                        sc.wait_ge(par_f_ready, stage_count[0] + 1)
                    at_least(sc, phi_done, read_by)
                    sc.activation(out_tile[:, :], z[(3 * j + m) % 2][:, :], ACT.Exp,
                                  bias=par_f[s][:, 1 if m == 0 else 0, j:j + 1]).then_inc(exp_done, 1)

                def logarithm(u, j):
                    sc.wait_ge(scale_ready, u + 1)
                    sc.wait_ge(phi_q_ready, u + 1)
                    at_least(sc, miss_ready, u)
                    sc.activation(lnq[:, :], phi_q[j % 2][:, :], ACT.Ln, scale=scale[j % 2][:, 0:1], bias=1.0)\
                        .then_inc(ln_done, 1)

                def negated(u, j):
                    sc.wait_ge(ln_done, u + 1)
                    at_least(sc, wo_done, u - 1)
                    sc.activation(miss[j % 2][:, :], lnq[:, :], ACT.Exp, scale=-1.0).then_inc(miss_ready, 1)

                def gelu_hidden(n, s, k):
                    b, half = k // 2, k % 2
                    at = slice(half * N, (half + 1) * N)
                    sc.wait_ge(up_ready, 8 * (n - 1) + k + 1)
                    sc.activation(hid[:, b, at], gp[:, at], ACT.Gelu_apprx_tanh,
                                  bias=par_g[1 - s][:, FF1 + b:FF1 + b + 1]).then_inc(hid_ready, 1)

                def norm_rstd(count):
                    sc.wait_ge(var_ready, count)
                    sc.activation(rstd[:, :], gp[:, :], ACT.Ln, bias=ln_eps[:, 0:1]).then_inc(ln_var, 1)
                    sc.wait_ge(ln_var, count)
                    sc.activation(rstd[:, :], rstd[:, :], ACT.Exp, scale=-0.5).then_inc(rstd_ready, 1)

                def copy_centred(count):
                    sc.wait_ge(centred_ready, count)
                    sc.activation(centred[:, :], gp[:, :], ACT.Copy).then_inc(copied, 1)

                stage_count = [0]

                def stage(n, s, attention=True, rest=True):
                    stage_count[0] = n
                    for j in range(CB):
                        u = 8 * n + j
                        if attention:
                            exponent(s, u, j, 0, ek, 2 * u - 1)
                        if rest and j == 2:
                            sc.wait_ge(bias_ready, n)
                            sc.wait_ge(wo_done, 8 * n)
                            sc.activation(g_act[:, :], yp[:, :], ACT.Gelu_apprx_tanh, scale=-1.0,
                                          bias=bias_y[:, 0:1]).then_inc(gelu_y, 1)
                            sc.preload_act_table_set(EXP_LN)
                        if j == 0 and rest or j > 0 and attention:
                            logarithm(u - 1, (j - 1) % CB)
                        if rest and j == 3:
                            norm_rstd(2 * n - 1)
                        if rest and j == 7:
                            norm_rstd(2 * n)
                        if rest and j == 4:
                            for k in range(4):
                                gelu_hidden(n, s, k)
                            sc.preload_act_table_set(EXP_LN)
                        if attention:
                            exponent(s, u, j, 2, eq, 2 * u)
                        if j == 0 and rest or j > 0 and attention:
                            negated(u - 1, (j - 1) % CB)
                        if rest and j == 2:
                            copy_centred(2 * n - 1)
                        if rest and j == 4:
                            for k in range(4, 8):
                                gelu_hidden(n, s, k)
                            sc.preload_act_table_set(EXP_LN)
                        if rest and j == 5:
                            sc.wait_ge(down_ready, n)
                            sc.activation(g_act[:, :], gp[:, :], ACT.Gelu_apprx_tanh,
                                          bias=par_g[1 - s][:, B2:B2 + 1]).then_inc(gelu_down, 1)
                            sc.preload_act_table_set(EXP_LN)
                        if rest and j == 6:
                            copy_centred(2 * n)

                sc.preload_act_table_set(EXP_LN)
                stage(0, 0, rest=False)
                with sc.Fori(0, LOOPS) as i:
                    stage(2 * i + 1, 1)
                    stage(2 * i + 2, 0)
                stage(STAGES - 1, 1)
                stage(STAGES, 0, attention=False)

            @block.vector
            def _(v):
                def split(g, m, layer):
                    v.wait_ge(raw_in[g], 48 * (layer + 1))
                    v.tensor_copy(wh[g][:, m, :], raw[g][:, m, :]).then_inc(w_upper[g], 1)
                    v.wait_ge(w_upper[g], 3 * layer + m + 1)
                    v.tensor_tensor(wl[g][:, m, :], raw[g][:, m, :], wh[g][:, m, :].bitcast(F32),
                                    ALU.subtract).then_inc(w_split[g], 1)

                def feature_map(u, j, m, e, s, o, total):
                    q = 0 if m == 0 else 1
                    v.wait_ge(exp_done, 2 * u + q + 1)
                    v.tensor_scalar(e[:, :], e[:, :], 1.0, -1.0 if q else 0.0, ALU.min, ALU.add).then_inc(capped, 1)
                    v.wait_ge(capped, 2 * u + q + 1)
                    v.scalar_tensor_tensor(out=o[:, :], in0=z[(3 * j + m) % 2][:, :],
                                           scalar=par_f[s][:, 3 if m == 0 else 0, j:j + 1], in1=e[:, :],
                                           op0=ALU.add, op1=ALU.max, accum_out=total).then_inc(phi_done, 1)

                def add_one(u, o):
                    v.wait_ge(phi_done, 2 * u + 2)
                    v.tensor_scalar(o[:, :], o[:, :], 1.0, None, ALU.add).then_inc(phi_q_ready, 1)

                def add_residual(a, b, ready, count, to):
                    v.wait_ge(ready, to)
                    v.tensor_tensor(r_sum[:, :], a, b, ALU.add).then_inc(sum_ready, 1)

                def square_centred(count):
                    v.wait_ge(copied, count)
                    v.tensor_tensor(square[:, :], centred[:, :], centred[:, :], ALU.mult).then_inc(squared, 1)

                def finish_norm(count, g, sc_col, o):
                    v.wait_ge(rstd_ready, count)
                    v.scalar_tensor_tensor(out=centred[:, :], in0=centred[:, :], scalar=par_g[g][:, sc_col:sc_col + 1],
                                           in1=rstd[:, :], op0=ALU.mult, op1=ALU.mult).then_inc(normed, 1)
                    v.wait_ge(normed, count)
                    v.tensor_scalar(o, centred[:, :], par_g[g][:, sc_col + 1:sc_col + 2], None, ALU.add)\
                        .then_inc(state_ready, 1)

                def scale_output(s, u, j):
                    v.wait_ge(mean_v_ready, u + 1)
                    v.tensor_scalar(wg[s][:, j, :], wo[j // 4][:, j % 4, :], mean_v[j % 2][:, 0:1], None,
                                    ALU.mult).then_inc(wg_ready, 1)

                def stage(n, s, layer=0, following=None, attention=True, rest=True):
                    p = 1 - s
                    for j in range(CB):
                        u = 8 * n + j
                        k = j % 2
                        if attention:
                            feature_map(u, j, 0, ek, s, phi_k, sum_k[k][:, 0:1])
                        if j == 0 and rest:
                            v.tensor_copy(par_g[p][:, :], table_g[:, bass.ds(layer, 1), :]
                                          .rearrange("p l k -> p (l k)")).then_inc(par_g_ready, 1)
                            scale_output(p, u - 1, CB - 1)
                        elif j > 0 and attention:
                            if j in (1, 5) and s == 0:
                                v.wait_ge(wo_in[j // 4], 16 * (following + 1))
                            scale_output(s, u - 1, j - 1)
                        if rest and j == 2:
                            v.wait_ge(const_ready, n)
                            v.wait_ge(par_g_ready, n)
                            v.tensor_scalar(bias_y[:, :], gp[:, 0:1], par_g[p][:, BO:BO + 1], None, ALU.add)\
                                .then_inc(bias_ready, 1)
                        if attention:
                            v.wait_ge(z_ready, 3 * u + 2)
                            v.wait_ge(phi_done, 2 * u + 1)
                            v.tensor_tensor_reduce(phi_k[:, :], phi_k[:, :], z[(3 * j + 1) % 2][:, :], 1.0, 0.0,
                                                   ALU.mult, ALU.add, sum_kv[k][:, 0:1]).then_inc(kv_done, 1)
                            at_least(v, ln_done, u - 1)
                            v.tensor_scalar(scale[k][:, :], sum_k[k][:, :], 1.0 / Z_EPS, None, ALU.mult)\
                                .then_inc(scale_ready, 1)
                            v.tensor_scalar(inv[k][:, :], sum_k[k][:, :], TINY, None, ALU.max).then_inc(guarded, 1)
                        if rest and j == 2:
                            add_residual(g_act[:, :], res[:, p, :], gelu_y, 2 * n - 1, n)
                        if rest and j == 6:
                            add_residual(g_act[:, :], mid[:, :], gelu_down, 2 * n, n)
                        if attention:
                            v.wait_ge(guarded, u + 1)
                            v.reciprocal(inv[k][:, :], inv[k][:, :]).then_inc(inv_ready, 1)
                            at_least(v, ln_done, u - 1)
                            feature_map(u, j, 2, eq, s, phi_q[k], None)
                            add_one(u, phi_q[k])
                            v.wait_ge(inv_ready, u + 1)
                            v.wait_ge(kv_done, u + 1)
                            v.scalar_tensor_tensor(out=mean_v[k][:, :], in0=sum_kv[k][:, :], scalar=inv[k][:, 0:1],
                                                   in1=par_f[s][:, 4, j:j + 1], op0=ALU.mult, op1=ALU.add)\
                                .then_inc(mean_v_ready, 1)
                        if rest and j == 2:
                            square_centred(2 * n - 1)
                        if rest and j == 3:
                            finish_norm(2 * n - 1, p, S1, mid[:, :])
                        if rest and j == 6:
                            square_centred(2 * n)
                        if rest and j == 7:
                            finish_norm(2 * n, p, S2, res[:, p, :])
                            v.wait_ge(state_ready, 2 * n)
                            v.tensor_copy(res_h[:, p, :], res[:, p, :]).then_inc(state_h, 1)
                            v.wait_ge(state_h, n)
                            v.tensor_tensor(res_l[:, p, :], res[:, p, :], res_h[:, p, :].bitcast(F32), ALU.subtract)\
                                .then_inc(state_l, 1)
                        if attention and j == 4 and following is not None:
                            v.tensor_copy(par_f[p][:, :, :], table_f[:, bass.ds(following, 1), :, :]
                                          .rearrange("p l k c -> p (l k) c")).then_inc(par_f_ready, 1)
                        if attention and s == 1 and 4 <= j < 7 and following is not None:
                            if j == 4:
                                v.wait_ge(z_ready, 3 * u)
                            split(0, j - 4, following)
                        if attention and s == 0 and j < 3:
                            split(1, j, following)

                v.sem_inc(state_l, SEQS)
                v.tensor_copy(par_f[0][:, :, :], table_f[:, 0, :, :]).then_inc(par_f_ready, 1)
                for m in range(3):
                    split(0, m, 0)
                stage(0, 0, following=0, rest=False)
                with v.Fori(0, LOOPS) as i:
                    stage(2 * i + 1, 1, i, i + 1)
                    stage(2 * i + 2, 0, i, i + 1)
                stage(STAGES - 1, 1, LAYERS - 1)
                stage(STAGES, 0, LAYERS - 1, attention=False)

        with ExitStack() as c:
            prod = sb("gated", [P, T], F32, c)
            back = [c.enter_context(nc.psum_tensor(f"back{q}", [P, N], F32)) for q in range(CHUNKS)]
            gated, turned = sem("gated_ready", c), sem("turned_back", c)
            added, stored = sem("output_ready", c), sem("output_stored", c)
            block = c.enter_context(nc.Block())

            @block.vector
            def _(v):
                for q in range(CHUNKS):
                    at = slice(q * N, (q + 1) * N)
                    v.tensor_tensor(prod[:, at], res[:, q // 2, q % 2 * N:(q % 2 + 1) * N], gate[:, at], ALU.mult)\
                        .then_inc(gated, 1)
                for q in range(CHUNKS):
                    v.wait_ge(turned, q + 1)
                    v.tensor_tensor(x[:, 4 * q:4 * q + 4, :], x[:, 4 * q:4 * q + 4, :],
                                    back[q][:, :].rearrange("p (b d) -> p b d", d=P), ALU.add).then_inc(added, 1)

            @block.tensor
            def _(pe):
                for q in range(CHUNKS):
                    pe.wait_ge(gated, q + 1)
                    for b in range(4):
                        at = slice((4 * q + b) * P, (4 * q + b + 1) * P)
                        ins = pe.transpose(back[q][:, b * P:(b + 1) * P], prod[:, at], ident[:, :])
                    ins.then_inc(turned, 1)

            @block.sync
            def _(sp):
                for q in range(CHUNKS):
                    sp.wait_ge(added, q + 1)
                    sp.dma_start(out_tokens[:, 4 * q:4 * q + 4, :], x[:, 4 * q:4 * q + 4, :]).then_inc(stored, 16)
                sp.wait_ge(stored, 16 * CHUNKS)


INPUTS = ["L0_attn_x"] + [f"L0_attn_{n}" for n in (
    "Wq", "bq", "Wk", "bk", "Wv", "bv", "Wo", "bo", "ln1_s", "ln1_b", "W1", "b1", "W2", "b2", "ln2_s", "ln2_b")] \
    + [f"L0_ffn_{n}" for n in (
        "gw", "gb", "w1", "b1", "w3", "b3", "w2", "b2", "sw1", "sb1", "sw3", "sb3", "sw2", "sb2")]


def kernel(**inputs):
    import concourse.bacc as bacc
    from concourse.bass_utils import run_bass_kernel_spmd

    nc = bacc.Bacc("TRN2", target_bir_lowering=False, num_devices=1)
    arrays, tensors = {}, {}
    for name in INPUTS:
        a = np.ascontiguousarray(inputs[name])
        arrays[f"in_{name}"] = a
        tensors[name] = nc.dram_tensor(f"in_{name}", a.shape, mybir.dt.from_np(a.dtype), kind="ExternalInput").ap()
    x = arrays["in_L0_attn_x"]
    out = nc.dram_tensor("out", x.shape, mybir.dt.from_np(x.dtype), kind="ExternalOutput").ap()
    recurrent_attention_gated_by_experts(nc, tensors, out)
    return run_bass_kernel_spmd(nc, [arrays], core_ids=[0]).results[0]["out"]
```

```python
from contextlib import ExitStack

import numpy as np

import concourse.bass as bass
from concourse import mybir

ALU = mybir.AluOpType
ACT = mybir.ActivationFunctionType
AXX = mybir.AxisListType.X
F32 = mybir.dt.float32
F32R = mybir.dt.float32r

P = 128
LN_EPS = 1e-6
Z_EPS = 1e-6
IN_EPS = 1e-5
TINY = 1e-38
EXP_LN = "natural_log_exp_and_others"


def at_least(engine, semaphore, value):
    if isinstance(value, int) and value <= 0:
        return
    engine.wait_ge(semaphore, value)


def over(ap, axis, shape):
    return ap.unsqueeze(axis).broadcast_to(shape)


def recurrent_attention_gated_by_experts(nc: bass.Bass, t: dict, out: bass.AP):
    x_in = t["L0_attn_x"]
    SEQS, S, D = x_in.shape
    LAYERS, HEADS, _, HK = t["L0_attn_Wq"].shape
    FF = t["L0_attn_W1"].shape[2]
    EXPERTS, _, INTER = t["L0_ffn_w1"].shape
    T = SEQS * S
    TB = T // P
    CB = HEADS * HK // P
    FB = FF // P
    PAIRS = EXPERTS // 2
    N = 512
    CHUNKS = T // N
    GROUPS, PER_GROUP, TOP_GROUPS, TOP = 8, EXPERTS // 8, 4, 4
    STAGES = SEQS * LAYERS
    assert D == P and SEQS == 2 and S == 2 * N and 2 * INTER == P and CB == 8 and FB == 4

    x_tokens = x_in.rearrange("n s d -> (n s) d").rearrange("(b p) d -> p b d", p=P)
    out_tokens = out.rearrange("n s d -> (n s) d").rearrange("(b p) d -> p b d", p=P)
    weights_by_pair = nc.dram_tensor("expert_weights", [EXPERTS, T], F32, kind="Internal").ap()

    with ExitStack() as whole:
        def sb(name, shape, dtype=F32, ctx=whole):
            return ctx.enter_context(nc.sbuf_tensor(name, shape, dtype))

        def sem(name, ctx=whole):
            return ctx.enter_context(nc.semaphore(name))

        ident = sb("ident", [P, P])
        centre = sb("centre", [P, P])
        average = sb("average", [P, P])
        ones = sb("ones", [P, 2])
        ln_eps = sb("ln_eps", [P, 1])
        x = sb("x", [P, TB, P])
        res = sb("res", [P, SEQS, S])
        res_h = sb("res_h", [P, SEQS, S], F32R)
        res_l = sb("res_l", [P, SEQS, S], F32R)
        gate = sb("gate", [P, T])
        rows_qk = sb("rows_qk", [P, P])
        rows_v1 = sb("rows_v1", [P, P])
        rows_misc = sb("rows_misc", [P, P])
        NG = FB + 6
        table_f = sb("table_f", [P, LAYERS, 4, CB])
        table_g = sb("table_g", [P, LAYERS, NG])
        moe_b13 = sb("moe_b13", [P, PAIRS + 1, 2])
        moe_sb2 = sb("moe_sb2", [P, 1])
        cwT = sb("cwT", [EXPERTS, T])

        with ExitStack() as c:
            gw = sb("gw", [P, EXPERTS], F32, c)
            gb = sb("gb", [P, EXPERTS], F32, c)
            xc = sb("xc", [P, TB, P], F32, c)
            sq = sb("sq", [P, TB, P], F32, c)
            mean = sb("mean", [P, TB], F32, c)
            var = sb("var", [P, TB], F32, c)
            root = sb("root", [P, TB], F32, c)
            rstd = sb("rstd", [P, TB], F32, c)
            corr = sb("corr", [P, TB], F32, c)
            lg = sb("lg", [P, TB, EXPERTS], F32, c)
            prob = sb("prob", [P, TB, EXPERTS], F32, c)
            col = sb("col", [P, TB], F32, c)
            tot = sb("tot", [P, TB], F32, c)
            hi2 = sb("hi2", [P, TB * GROUPS, 2], F32, c)
            lo2 = sb("lo2", [P, TB * GROUPS, 2], F32, c)
            first = sb("first", [P, TB * GROUPS], F32, c)
            second = sb("second", [P, TB * GROUPS], F32, c)
            score = sb("score", [P, TB, GROUPS], F32, c)
            above = sb("above", [P, TB, GROUPS, GROUPS], F32, c)
            equal = sb("equal", [P, TB, GROUPS, GROUPS], F32, c)
            earlier = sb("earlier", [P, GROUPS, GROUPS], F32, c)
            keep = sb("keep", [P, TB, GROUPS], F32, c)
            drop = sb("drop", [P, TB, GROUPS], F32, c)
            masked = sb("masked", [P, TB, EXPERTS], F32, c)
            best = sb("best", [P, TB, 8], F32, c)
            more = sb("more", [P, TB, EXPERTS], F32, c)
            tie = [sb(f"tie{k}", [P, TB, 2 * EXPERTS], F32, c) for k in range(2)]
            cw = sb("cw", [P, TB, EXPERTS], F32, c)
            ps = [c.enter_context(nc.psum_tensor(f"ps{k}", [P, N], F32)) for k in range(8)]

            x_in_sem, rows_in, gate_in = sem("x_loaded", c), sem("rows_loaded", c), sem("gate_weights_loaded", c)
            consts = sem("constants_ready", c)
            turned = sem("transposed", c)
            dve = sem("vector_steps", c)
            root_ready, exp_ready = sem("root_ready", c), sem("exp_ready", c)
            columns_ready = sem("weights_transposed", c)
            stored = sem("expert_weights_stored", c)

            block = c.enter_context(nc.Block())
            ROWS = []
            r = 0
            for name, tile in (("L0_attn_bq", rows_qk), ("L0_attn_bk", rows_qk)):
                ROWS.append((tile, r, t[name].rearrange("l h k -> l (h k)").rearrange("l (c p) -> (l c) p", p=P)))
                r += LAYERS * CB
            r = 0
            for ap in (t["L0_attn_bv"].rearrange("l h k -> l (h k)").rearrange("l (c p) -> (l c) p", p=P),
                       t["L0_attn_b1"].rearrange("l (c p) -> (l c) p", p=P),
                       t["L0_ffn_b1"].rearrange("e k -> (e k)").rearrange("(r p) -> r p", p=P),
                       t["L0_ffn_b3"].rearrange("e k -> (e k)").rearrange("(r p) -> r p", p=P)):
                ROWS.append((rows_v1, r, ap))
                r += ap.shape[0]
            r = 0
            for name in ("bo", "b2", "ln1_s", "ln1_b", "ln2_s", "ln2_b"):
                ROWS.append((rows_misc, r, t[f"L0_attn_{name}"]))
                r += LAYERS
            for name in ("sb1", "sb3", "sb2"):
                ROWS.append((rows_misc, r, t[f"L0_ffn_{name}"].rearrange("(r p) -> r p", p=P)))
                r += 1
            MISC = r

            mark = {}

            @block.vector
            def _(v):
                n = [0]

                def done(ins, name=None):
                    ins.then_inc(dve, 1)
                    n[0] += 1
                    if name:
                        mark[name] = n[0]
                    v.wait_ge(dve, n[0])

                def tt(o, a, b, op, name=None):
                    done(v.tensor_tensor(o, a, b, op), name)

                def ts(o, a, s1, s2, op0, op1=ALU.bypass, name=None):
                    done(v.tensor_scalar(o, a, s1, s2, op0, op1), name)

                wide = [P, TB, P]
                v.wait_ge(consts, 10)
                v.wait_ge(x_in_sem, 64)
                done(v.tensor_reduce(mean[:, :], x[:, :, :], AXX, ALU.add))
                ts(mean[:, :], mean[:, :], 1.0 / P, None, ALU.mult)
                tt(xc[:, :, :], x[:, :, :], over(mean[:, :], 2, wide), ALU.subtract)
                tt(sq[:, :, :], xc[:, :, :], xc[:, :, :], ALU.mult)
                done(v.tensor_reduce(var[:, :], sq[:, :, :], AXX, ALU.add))
                ts(var[:, :], var[:, :], 1.0 / P, IN_EPS, ALU.mult, ALU.add, name="var")
                v.wait_ge(root_ready, 1)
                done(v.reciprocal(rstd[:, :], root[:, :]))
                tt(corr[:, :], rstd[:, :], rstd[:, :], ALU.mult)
                tt(corr[:, :], corr[:, :], var[:, :], ALU.mult)
                ts(corr[:, :], corr[:, :], -0.5, 1.5, ALU.mult, ALU.add)
                tt(rstd[:, :], rstd[:, :], corr[:, :], ALU.mult)
                tt(xc[:, :, :], xc[:, :, :], over(rstd[:, :], 2, wide), ALU.mult, name="normed")
                done(v.tensor_scalar(centre[:, :], ident[:, :], -1.0 / P, None, ALU.add))
                v.wait_ge(turned, 1)
                rows = ps[0]
                qk = rows[:, 0:P].rearrange("p (m l c) -> p l m c", m=2, c=CB)
                done(v.tensor_copy(table_f[:, :, 0:2, :], qk))
                ts(table_f[:, :, 3, :], table_f[:, :, 0, :], 1.0, None, ALU.add)
                at = P
                done(v.tensor_copy(table_f[:, :, 2, :], rows[:, at:at + LAYERS * CB].rearrange("p (l c) -> p l c", c=CB)))
                at += LAYERS * CB
                done(v.tensor_copy(table_g[:, :, 6:6 + FB], rows[:, at:at + LAYERS * FB].rearrange("p (l c) -> p l c", c=FB)))
                at += LAYERS * FB
                done(v.tensor_copy(moe_b13[:, 0:PAIRS, 0], rows[:, at:at + PAIRS]))
                at += PAIRS
                done(v.tensor_copy(moe_b13[:, 0:PAIRS, 1], rows[:, at:at + PAIRS]))
                at += PAIRS
                done(v.tensor_copy(table_g[:, :, 0:6], rows[:, at:at + 6 * LAYERS].rearrange("p (k l) -> p l k", l=LAYERS)))
                at += 6 * LAYERS
                done(v.tensor_copy(moe_b13[:, PAIRS, :], rows[:, at:at + 2]))
                done(v.tensor_copy(moe_sb2[:, :], rows[:, at + 2:at + 3]))
                for q in range(CHUNKS):
                    s, h = q // 2, q % 2 * N
                    v.wait_ge(turned, 2 + q)
                    done(v.tensor_copy(res[:, s, h:h + N], ps[1 + q][:, :]), f"state{q}")
                for s in range(SEQS):
                    done(v.tensor_copy(res_h[:, s, :], res[:, s, :]))
                    tt(res_l[:, s, :], res[:, s, :], res_h[:, s, :].bitcast(F32), ALU.subtract)
                per = [P, TB, EXPERTS]
                v.wait_ge(turned, 2 + CHUNKS)
                v.wait_ge(gate_in, 32)
                logits = ps[5][:, :].rearrange("p (b e) -> p b e", e=EXPERTS)
                tt(lg[:, :, :], logits, over(gb[:, :], 1, per), ALU.add)
                done(v.tensor_reduce(col[:, :], lg[:, :, :], AXX, ALU.max))
                tt(lg[:, :, :], lg[:, :, :], over(col[:, :], 2, per), ALU.subtract, name="logits")
                v.wait_ge(exp_ready, 1)
                done(v.tensor_reduce(tot[:, :], prob[:, :, :], AXX, ALU.add))
                done(v.reciprocal(tot[:, :], tot[:, :]))
                tt(prob[:, :, :], prob[:, :, :], over(tot[:, :], 2, per), ALU.mult)
                fours = prob[:, :, :].rearrange("p b (g k) -> p (b g) k", k=PER_GROUP)
                tt(hi2[:, :, :], fours[:, :, 0:2], fours[:, :, 2:4], ALU.max)
                tt(lo2[:, :, :], fours[:, :, 0:2], fours[:, :, 2:4], ALU.min)
                tt(first[:, :], hi2[:, :, 0], hi2[:, :, 1], ALU.max)
                tt(second[:, :], hi2[:, :, 0], hi2[:, :, 1], ALU.min)
                tt(lo2[:, :, 0], lo2[:, :, 0], lo2[:, :, 1], ALU.max)
                tt(second[:, :], second[:, :], lo2[:, :, 0], ALU.max)
                tt(score[:, :, :].rearrange("p b g -> p (b g)"), first[:, :], second[:, :], ALU.add)
                by = [P, TB, GROUPS, GROUPS]
                theirs, own = over(score[:, :, :], 2, by), over(score[:, :, :], 3, by)
                tt(above[:, :, :, :], theirs, own, ALU.is_gt)
                tt(equal[:, :, :, :], theirs, own, ALU.is_equal)
                tt(equal[:, :, :, :], equal[:, :, :, :], over(earlier[:, :, :], 1, by), ALU.mult)
                tt(above[:, :, :, :], above[:, :, :, :], equal[:, :, :, :], ALU.add)
                done(v.tensor_reduce(keep[:, :, :], above[:, :, :, :], AXX, ALU.add))
                ts(keep[:, :, :], keep[:, :, :], float(TOP_GROUPS), None, ALU.is_lt)
                ts(drop[:, :, :], keep[:, :, :], -1.0, None, ALU.add)
                m4 = masked[:, :, :].rearrange("p b (g k) -> p (b g) k", k=PER_GROUP)
                grp = [P, TB * GROUPS, PER_GROUP]
                tt(m4, fours, over(keep[:, :, :].rearrange("p b g -> p (b g)"), 2, grp), ALU.mult)
                tt(m4, m4, over(drop[:, :, :].rearrange("p b g -> p (b g)"), 2, grp), ALU.add)
                for b in range(TB):
                    done(v.max(best[:, b, :], masked[:, b, :]))
                least = best[:, :, TOP - 1:TOP].broadcast_to(per)
                real = slice(EXPERTS, 2 * EXPERTS)
                tt(more[:, :, :], masked[:, :, :], least, ALU.is_gt)
                tt(tie[0][:, :, real], masked[:, :, :], least, ALU.is_equal)
                tt(cw[:, :, :], masked[:, :, :], least, ALU.is_equal)
                done(v.tensor_reduce(col[:, :], more[:, :, :], AXX, ALU.add))
                ts(col[:, :], col[:, :], -1.0, float(TOP), ALU.mult, ALU.add)
                k, a = 1, 0
                while k < EXPERTS:
                    tt(tie[1 - a][:, :, real], tie[a][:, :, real],
                       tie[a][:, :, EXPERTS - k:2 * EXPERTS - k], ALU.add)
                    k, a = 2 * k, 1 - a
                tt(lg[:, :, :], tie[a][:, :, real], over(col[:, :], 2, per), ALU.is_le)
                tt(cw[:, :, :], cw[:, :, :], lg[:, :, :], ALU.mult)
                tt(cw[:, :, :], cw[:, :, :], more[:, :, :], ALU.add)
                tt(cw[:, :, :], cw[:, :, :], prob[:, :, :], ALU.mult, name="weights")

            @block.sync
            def _(sp):
                for q in range(4):
                    sp.dma_start(x[:, 4 * q:4 * q + 4, :], x_tokens[:, 4 * q:4 * q + 4, :]).then_inc(x_in_sem, 16)
                sp.dma_start(gw[:, :], t["L0_ffn_gw"]).then_inc(gate_in, 16)
                sp.dma_start(gb[:, :], t["L0_ffn_gb"].rearrange("(a e) -> a e", a=1).broadcast_to([P, EXPERTS]))\
                    .then_inc(gate_in, 16)
                sp.wait_ge(columns_ready, CHUNKS)
                sp.dma_start(weights_by_pair, cwT[:, :]).then_inc(stored, 16)
                sp.wait_ge(stored, 16)

            @block.gpsimd
            def _(pool):
                pool.memset(ident[:, :], 0.0).then_inc(consts, 1)
                pool.memset(average[:, :], 1.0 / P).then_inc(consts, 1)
                pool.memset(ones[:, :], 1.0).then_inc(consts, 1)
                pool.memset(ln_eps[:, :], LN_EPS).then_inc(consts, 1)
                pool.memset(earlier[:, :, :], 1.0).then_inc(consts, 1)
                pool.memset(rows_misc[:, :], 0.0).then_inc(consts, 1)
                for k in range(2):
                    pool.memset(tie[k][:, :, :], 0.0).then_inc(consts, 1)
                pool.wait_ge(consts, 8)
                pool.affine_select(out=ident[:, :], in_=ident[:, :], compare_op=ALU.not_equal, fill=1.0, base=0,
                                   pattern=[[-1, P]], channel_multiplier=1).then_inc(consts, 1)
                pool.affine_select(out=earlier[:, :, :], in_=earlier[:, :, :], compare_op=ALU.is_gt, fill=0.0,
                                   base=0, pattern=[[1, GROUPS], [-1, GROUPS]], channel_multiplier=0)\
                    .then_inc(consts, 1)

            @block.scalar
            def _(sc):
                sc.wait_ge(consts, 8)
                for tile, row, ap in ROWS:
                    sc.dma_start(tile[row:row + ap.shape[0], :], ap).then_inc(rows_in, 16)
                sc.wait_ge(dve, mark["var"])
                sc.activation(root[:, :], var[:, :], ACT.Sqrt).then_inc(root_ready, 1)
                sc.wait_ge(dve, mark["logits"])
                sc.activation(prob[:, :, :], lg[:, :, :], ACT.Exp).then_inc(exp_ready, 1)
                for q in range(CHUNKS):
                    sc.wait_ge(turned, 3 + CHUNKS + q)
                    sc.activation(cwT[:, q * N:(q + 1) * N], ps[q if q else 6][0:EXPERTS, :], ACT.Copy)\
                        .then_inc(columns_ready, 1)

            @block.tensor
            def _(pe):
                pe.wait_ge(consts, 9)
                pe.wait_ge(rows_in, 16 * len(ROWS))
                pe.transpose(ps[0][:, 0:P], rows_qk[:, :], ident[:, :])
                pe.transpose(ps[0][:, P:2 * P], rows_v1[:, :], ident[:, :])
                pe.transpose(ps[0][:, 2 * P:3 * P], rows_misc[:, :], ident[:, :]).then_inc(turned, 1)
                pe.wait_ge(dve, mark["normed"])
                for q in range(CHUNKS):
                    for b in range(4):
                        ins = pe.transpose(ps[1 + q][:, b * P:(b + 1) * P], xc[:, 4 * q + b, :], ident[:, :])
                    ins.then_inc(turned, 1)
                pe.wait_ge(gate_in, 32)
                pe.wait_ge(dve, mark[f"state{CHUNKS - 1}"])
                for b in range(TB):
                    ins = pe.matmul(ps[5][:, b * EXPERTS:(b + 1) * EXPERTS],
                                    res[:, b // 8, (b % 8) * P:(b % 8 + 1) * P], gw[:, :], start=True, stop=True)
                ins.then_inc(turned, 1)
                pe.wait_ge(dve, mark["weights"])
                for q in range(CHUNKS):
                    for b in range(4):
                        ins = pe.transpose(ps[q if q else 6][0:EXPERTS, b * P:(b + 1) * P], cw[:, 4 * q + b, :],
                                           ident[:, :])
                    ins.then_inc(turned, 1)

        with ExitStack() as c:
            raw = [sb(f"expert_raw{k}", [P, 2, P], F32, c) for k in range(2)]
            w13_h = [sb(f"w13_h{k}", [P, 2, P], F32R, c) for k in range(2)]
            w13_l = [sb(f"w13_l{k}", [P, 2, P], F32R, c) for k in range(2)]
            w2 = [sb(f"w2_{k}", [P, P], F32, c) for k in range(2)]
            b13 = [sb(f"b13_{k}", [P, 2], F32, c) for k in range(2)]
            share = [sb(f"share{k}", [P, T], F32, c) for k in range(2)]
            b2 = sb("experts_b2", [EXPERTS, P], F32, c)
            act_a = [sb(f"act_a{k}", [P, N], F32, c) for k in range(2)]
            prod = [sb(f"prod{k}", [P, N], F32, c) for k in range(2)]
            hid = [sb(f"hid{k}", [P, N], F32, c) for k in range(2)]
            y = [c.enter_context(nc.psum_tensor(f"y{q}", [P, N], F32)) for q in range(CHUNKS)]
            a_ps = [c.enter_context(nc.psum_tensor(f"a_ps{k}", [P, N], F32)) for k in range(2)]
            c_ps = [c.enter_context(nc.psum_tensor(f"c_ps{k}", [P, N], F32)) for k in range(2)]

            b2_in = sem("b2_loaded", c)
            raw_in = [sem(f"w13_loaded{k}", c) for k in range(2)]
            w2_in = [sem(f"w2_loaded{k}", c) for k in range(2)]
            share_in = [sem(f"share_loaded{k}", c) for k in range(2)]
            bias_placed = sem("bias_placed", c)
            upper_ready, split_ready = sem("w13_upper_ready", c), sem("w13_split", c)
            up_ready = sem("a_and_c_ready", c)
            silu_ready = sem("silu_ready", c)
            prod_ready = sem("product_ready", c)
            hid_ready = sem("hidden_ready", c)
            down_done = sem("hidden_used", c)
            gate_ready = sem("gate_ready", c)

            block = c.enter_context(nc.Block())
            LOOPS = PAIRS // 2
            w1d, w3d, w2d = (t[f"L0_ffn_{n}"] for n in ("w1", "w3", "w2"))

            @block.sync
            def _(sp):
                def load(pair, k, used):
                    at_least(sp, split_ready, used[0])
                    for m, w in enumerate((w1d, w3d)):
                        sp.dma_start(raw[k][:, m, :].rearrange("d (e k) -> d e k", e=2),
                                     w[bass.ds(2 * pair, 2), :, :].rearrange("e d k -> d e k")).then_inc(raw_in[k], 16)
                    at_least(sp, down_done, used[1])
                    sp.dma_start(w2[k][:, :], w2d[bass.ds(2 * pair, 2), :, :].rearrange("e k d -> (e k) d"))\
                        .then_inc(w2_in[k], 16)
                    at_least(sp, hid_ready, used[1])
                    for e in range(2):
                        sp.dma_start(share[k][e * INTER:(e + 1) * INTER, :],
                                     weights_by_pair[bass.ds(2 * pair + e, 1), :].broadcast_to([INTER, T]))\
                            .then_inc(share_in[k], 16)

                sp.dma_start(b2[:, :], t["L0_ffn_b2"]).then_inc(b2_in, 16)
                load(0, 0, (0, 0))
                load(1, 1, (0, 0))
                with sp.Fori(0, LOOPS - 1) as i:
                    load(2 * i + 2, 0, (2 * i + 1, 8 * i + 4))
                    load(2 * i + 3, 1, (2 * i + 2, 8 * i + 8))
                sp.wait_ge(split_ready, PAIRS - 1)
                sp.dma_start(raw[0][:, 0, :], t["L0_ffn_sw1"]).then_inc(raw_in[0], 16)
                sp.dma_start(raw[0][:, 1, :], t["L0_ffn_sw3"]).then_inc(raw_in[0], 16)
                sp.wait_ge(down_done, 4 * PAIRS - 4)
                sp.dma_start(w2[0][:, :], t["L0_ffn_sw2"]).then_inc(w2_in[0], 16)

            @block.tensor
            def _(pe):
                def up(k, q, n, w_first):
                    if q == 0:
                        pe.wait_ge(split_ready, w_first)
                    s, h = q // 2, slice(q % 2 * N, q % 2 * N + N)
                    for m, bank in enumerate((a_ps[q % 2], c_ps[q % 2])):
                        pe.matmul(bank[:, :], w13_h[k][:, m, :], res_h[:, s, h], start=True, stop=False)
                        pe.matmul(bank[:, :], w13_h[k][:, m, :], res_l[:, s, h], start=False, stop=False)
                        ins = pe.matmul(bank[:, :], w13_l[k][:, m, :], res_h[:, s, h], start=False, stop=True)
                    ins.then_inc(up_ready, 1)

                def down(k, q, n, loads, last=False):
                    if q == 0:
                        pe.wait_ge(w2_in[k], 16 * loads)
                    pe.wait_ge(prod_ready if last else hid_ready, n + 1)
                    pe.matmul(y[q][:, :], w2[k][:, :], hid[q % 2][:, :], start=False, stop=last).then_inc(down_done, 1)

                pe.wait_ge(b2_in, 16)
                for q in range(CHUNKS):
                    pe.matmul(y[q][:, :], b2[:, :], cwT[:, q * N:(q + 1) * N], start=True, stop=False)
                up(0, 0, 0, 1)
                with pe.Fori(0, LOOPS) as i:
                    for m in range(8):
                        k1, q1 = (m + 1) // 4 % 2, (m + 1) % 4
                        up(k1, q1, 8 * i + m + 1, 2 * i + 1 + (m + 1) // 4)
                        down(m // 4, m % 4, 8 * i + m, i + 1)
                for q in range(CHUNKS):
                    if q < 3:
                        up(0, q + 1, 4 * PAIRS + q + 1, PAIRS + 1)
                    down(0, q, 4 * PAIRS + q, LOOPS + 1, last=True)

            @block.scalar
            def _(sc):
                def silu(k, q, n, pair):
                    if q == 0:
                        sc.wait_ge(split_ready, pair + 1)
                    sc.wait_ge(up_ready, n + 1)
                    sc.activation(act_a[q % 2][:, :], a_ps[q % 2][:, :], ACT.Silu,
                                  bias=b13[k][:, 0:1]).then_inc(silu_ready, 1)

                with sc.Fori(0, LOOPS) as i:
                    for m in range(8):
                        silu(m // 4, m % 4, 8 * i + m, 2 * i + m // 4)
                for q in range(CHUNKS):
                    silu(0, q, 4 * PAIRS + q, PAIRS)
                for q in range(CHUNKS):
                    if q == 0:
                        sc.wait_ge(down_done, 4 * PAIRS + CHUNKS)
                    sc.activation(gate[:, q * N:(q + 1) * N], y[q][:, :], ACT.Silu, bias=moe_sb2[:, 0:1])\
                        .then_inc(gate_ready, 1)

            @block.vector
            def _(v):
                def split(k, pair, loads):
                    v.wait_ge(raw_in[k], 32 * loads)
                    at_least(v, up_ready, 4 * (pair - 1))
                    v.tensor_scalar(b13[k][:, :], moe_b13[:, bass.ds(pair, 1), :].rearrange("p l k -> p (l k)"), 0.0, None,
                                    ALU.add).then_inc(bias_placed, 1)
                    v.wait_ge(bias_placed, pair + 1)
                    v.tensor_copy(w13_h[k][:, :, :], raw[k][:, :, :]).then_inc(upper_ready, 1)
                    v.wait_ge(upper_ready, pair + 1)
                    v.tensor_tensor(w13_l[k][:, :, :], raw[k][:, :, :], w13_h[k][:, :, :].bitcast(F32),
                                    ALU.subtract).then_inc(split_ready, 1)

                def product(q, n, k, loads, shared=False):
                    v.wait_ge(silu_ready, n + 1)
                    o = hid[q % 2] if shared else prod[q % 2]
                    v.scalar_tensor_tensor(out=o[:, :], in0=c_ps[q % 2][:, :], scalar=b13[k][:, 1:2],
                                           in1=act_a[q % 2][:, :], op0=ALU.add, op1=ALU.mult)\
                        .then_inc(prod_ready, 1)
                    if shared:
                        return
                    v.wait_ge(prod_ready, n + 1)
                    if q == 0:
                        v.wait_ge(share_in[k], 32 * loads)
                    v.tensor_tensor(hid[q % 2][:, :], o[:, :], share[k][:, q * N:(q + 1) * N], ALU.mult)\
                        .then_inc(hid_ready, 1)

                split(0, 0, 1)
                with v.Fori(0, LOOPS) as i:
                    for m in range(8):
                        if m == 0:
                            split(1, 2 * i + 1, i + 1)
                        product(m % 4, 8 * i + m, m // 4, i + 1)
                        if m == 5:
                            split(0, 2 * i + 2, i + 2)
                for q in range(CHUNKS):
                    product(q, 4 * PAIRS + q, 0, 0, shared=True)

        with ExitStack() as c:
            raw = [sb(f"qkv_raw{g}", [P, 3, S // 2], F32, c) for g in range(2)]
            wh = [sb(f"qkv_h{g}", [P, 3, S // 2], F32R, c) for g in range(2)]
            wl = [sb(f"qkv_l{g}", [P, 3, S // 2], F32R, c) for g in range(2)]
            wo = [sb(f"wo{g}", [P, 4, P], F32, c) for g in range(2)]
            wg = [sb(f"wo_scaled{s}", [P, CB, P], F32, c) for s in range(SEQS)]
            w1 = sb("ff1", [P, FF], F32, c)
            w2 = sb("ff2", [P, FB, P], F32, c)
            par_f = [sb(f"par_f{s}", [P, 4, CB], F32, c) for s in range(SEQS)]
            par_g = [sb(f"par_g{s}", [P, NG], F32, c) for s in range(SEQS)]
            exp_k, relu_k, phi_k = (sb(n, [P, S], F32, c) for n in ("exp_k", "relu_k", "phi_k"))
            exp_q, line_q, phi_q = (sb(n, [P, S], F32, c) for n in ("exp_q", "line_q", "phi_q"))
            ln_q = sb("ln_q", [P, S], F32, c)
            miss = [sb(f"miss{k}", [P, S], F32, c) for k in range(2)]
            sum_k = [sb(f"sum_k{k}", [P, 1], F32, c) for k in range(2)]
            sum_kv = [sb(f"sum_kv{k}", [P, 1], F32, c) for k in range(2)]
            scale = [sb(f"scale{k}", [P, 1], F32, c) for k in range(2)]
            inv = [sb(f"inv{k}", [P, 1], F32, c) for k in range(2)]
            mean_v = [sb(f"mean_v{k}", [P, 1], F32, c) for k in range(2)]
            bias_y = sb("bias_y", [P, 1], F32, c)
            g_act = sb("g_act", [P, S], F32, c)
            r_sum = sb("r_sum", [P, S], F32, c)
            normal = sb("normal", [P, S], F32, c)
            square = sb("square", [P, S], F32, c)
            rstd = sb("rstd_t", [P, S], F32, c)
            mid = sb("mid", [P, S], F32, c)
            hid = sb("hidden", [P, FB, S], F32, c)

            tiles = [c.enter_context(nc.psum_tensor(f"tile{k}", [P, S], F32)) for k in range(3)]
            yp = c.enter_context(nc.psum_tensor("yp", [P, S], F32))

            raw_in = [sem(f"qkv_loaded{g}", c) for g in range(2)]
            wo_in = [sem(f"wo_loaded{g}", c) for g in range(2)]
            ff_in = sem("ff_loaded", c)
            w_upper, w_split = [[sem(f"{n}{g}", c) for g in range(2)] for n in ("qkv_upper_ready", "qkv_split")]
            q_ready, k_ready, v_ready = (sem(f"{n}_projected", c) for n in "qkv")
            wo_done = sem("wo_done", c)
            exp_q_done, exp_k_done, relu_done = (sem(n, c) for n in ("exp_q_done", "exp_k_done", "relu_k_done"))
            ln_done, miss_ready = sem("ln_done", c), sem("miss_ready", c)
            line_done, curve_done = sem("line_q_done", c), sem("curve_q_done", c)
            phi_q_ready, phi_k_ready = sem("phi_q_ready", c), sem("phi_k_ready", c)
            kv_done = sem("kv_done", c)
            scale_ready, guarded, inv_ready = sem("scale_ready", c), sem("sum_guarded", c), sem("inverse_ready", c)
            mean_v_ready, wg_ready = sem("mean_v_ready", c), sem("wo_scaled_ready", c)
            par_f_ready, par_g_ready = sem("par_f_ready", c), sem("par_g_ready", c)
            const_ready, bias_ready = sem("constant_ready", c), sem("bias_ready", c)
            gelu_y = sem("gelu_y_ready", c)
            sum1_ready, centred1, squared1, var1_ready, ln_var1, rstd1_ready, normed1 = (sem(f"norm1_{n}", c) for n in (
                "sum_ready", "centred", "squared", "variance_ready", "ln_variance", "rstd_ready", "normed"))
            sum2_ready, centred2, squared2, var2_ready, ln_var2, rstd2_ready, normed2 = (sem(f"norm2_{n}", c) for n in (
                "sum_ready", "centred", "squared", "variance_ready", "ln_variance", "rstd_ready", "normed"))
            mid_ready = sem("mid_ready", c)
            state_ready = sem("state_ready", c)
            state_h, state_l = sem("state_upper_ready", c), sem("state_split", c)
            up_ready, hid_ready = ([sem(f"{n}_{h}", c) for h in "ab"] for n in ("ff_up_ready", "ff_hidden_ready"))
            down_ready, gelu_down = sem("ff_down_ready", c), sem("gelu_down_ready", c)

            block = c.enter_context(nc.Block())
            LOOPS = LAYERS - 1
            BO, B2, S1, _, S2, _, FF1 = range(7)

            PE_ORDER = """
                k:7- v:7- q:7- k:0 out:4- v:0 k:1 q:0 out:5- k:2 v:1 out:6- q:1 k:3 const out:7- v:2 v:3 q:2
                centre1_a centre1_b out:0 var1_a var1_b k:4 q:3 out:1 up:0_a up:1_a up:0_b up:1_b up:2_a
                up:2_b up:3_a up:3_b v:4 q:4 k:5 down_a down_b down_rest_a down_rest_b v:5 q:5 k:6 centre2_a
                centre2_b out:2 var2_a var2_b v:6 q:6 out:3
            """.split()
            ACT_ORDER = """
                log:5- exp_k:7- relu_k:7- miss:5- exp_q:7- exp_k:0 relu_k:0 log:6- miss:6- exp_k:1 relu_k:1
                exp_q:0 log:7- exp_k:2 relu_k:2 miss:7- exp_q:1 log:0 exp_k:3 relu_k:3 gelu_y_a gelu_y_b
                miss:0 exp_q:2 square1_a square1_b log:1 ln_var1_a rstd1_a ln_var1_b miss:1 rstd1_b exp_k:4
                relu_k:4 exp_q:3 log:2 hidden:0_a hidden:0_b hidden:1_a hidden:1_b hidden:2_a hidden:2_b
                hidden:3_a hidden:3_b miss:2 log:3 exp_q:4 exp_k:5 relu_k:5 gelu_down_a gelu_down_b miss:3
                exp_q:5 exp_k:6 square2_a square2_b relu_k:6 log:4 ln_var2_a rstd2_a ln_var2_b rstd2_b
                miss:4 exp_q:6
            """.split()
            DVE_ORDER = """
                phi_k:7- kv:7- mean_v:6- line_q:7- scale:7- curve_q:7- phi_k:0 scale_wo:6- split_even:0
                inverse:7- kv:0 phi_k:1 line_q:0 curve_q:0 mean_v:7- scale:0 inverse:0 split_even:1 mean_v:0
                kv:1 scale_wo:7- phi_k:2 line_q:1 bias_y curve_q:1 scale:1 scale_wo:0 inverse:1 mean_v:1
                scale:2 kv:2 residual1_a residual1_b phi_k:3 kv:3 line_q:2 inverse:2 curve_q:2 scale:3
                norm1_a inverse:3 scale_wo:1 mean_v:2 mid_a norm1_b mid_b line_q:3 split_odd:0 columns
                mean_v:3 split_even:2 curve_q:3 split_odd:1 phi_k:4 scale:4 kv:4 curve_q:4 line_q:4 phi_k:5
                residual2_a scale:5 kv:5 residual2_b scale_wo:2 inverse:4 mean_v:4 scale_wo:3 scale_wo:4
                inverse:5 curve_q:5 line_q:5 split_odd:2 mean_v:5 phi_k:6 scale:6 scale_wo:5 norm2_a kv:6
                norm2_b state_a state_b line_q:6 curve_q:6 inverse:6 state_upper_a state_upper_b
                state_lower_a state_lower_b
            """.split()
            POOL_ORDER = """
                phi_q:6- phi_q:7- phi_q:0 phi_q:1 phi_q:2 phi_q:3 phi_q:4 phi_q:5
            """.split()
            TILE_STEPS = [
                "v:0 v:1 v:2 k:5 v:5 v:7 const centre1 centre2 up:0 up:3".split(),
                "q:0 k:0 q:2 k:3 k:4 v:4 k:6 v:6 k:7 up:1 down".split(),
                "q:1 k:1 k:2 q:3 v:3 q:4 q:5 q:6 q:7 var1 var2 up:2".split(),
            ]
            ATTENTION = ("q", "k", "v", "out", "exp_q", "exp_k", "relu_k", "log", "miss", "line_q", "curve_q",
                         "phi_k", "scale", "kv", "inverse", "mean_v", "scale_wo", "phi_q")
            GELUS = ("gelu_y", "hidden", "gelu_down")

            def parse(step):
                late = step.endswith("-")
                name = step.rstrip("-")
                half = None
                if name[-2:] in ("_a", "_b"):
                    name, half = name[:-2], "ab".index(name[-1])
                kind, _, block_ = name.partition(":")
                return kind, int(block_) if block_ else None, half, late

            HALF = [slice(0, N), slice(N, 2 * N)]

            def attention_of(n, s, layer, late):
                if not late:
                    return n, s, layer + (1 - s)
                return n - 1, 1 - s, layer

            def absent(kind, late, n):
                if not isinstance(n, int):
                    return False
                if kind in ATTENTION:
                    return not 0 <= n - late < STAGES
                if kind == "split_odd":
                    return not (n % 2 == 1 and n < STAGES - 1)
                if kind == "split_even":
                    return not (n % 2 == 0 and n < STAGES - 1)
                if kind == "columns":
                    return n >= STAGES - 1
                return n == 0

            FILLS = []
            for step in PE_ORDER:
                kind, b, half, late = parse(step)
                if kind not in ("out", "down_rest") and (kind, b, late) not in FILLS:
                    FILLS.append((kind, b, late))
            tile_of = {parse(step)[:2]: tiles[k] for k in range(3) for step in TILE_STEPS[k]}

            def last_read(kind, b, n):
                if kind in ("q", "k", "v"):
                    return {"q": line_done, "k": relu_done, "v": kv_done}[kind], 8 * n + b + 1
                if kind == "up":
                    return hid_ready[1], FB * (n - 1) + b + 1
                if kind == "const":
                    return bias_ready, n
                return {"centre1": normed1, "centre2": normed2, "var1": ln_var1, "var2": ln_var2,
                        "down": gelu_down}[kind], 2 * n

            def tile_free(pe, kind, b, late, n):
                at, m = FILLS.index((kind, b, late)), n
                while True:
                    at -= 1
                    if at < 0:
                        if isinstance(m, int) and m == 0:
                            return
                        at, m = at + len(FILLS), m - 1
                    k, b2, l2 = FILLS[at]
                    if tile_of[(k, b2)] is not tile_of[(kind, b)] or absent(k, l2, m):
                        continue
                    semaphore, value = last_read(k, b2, m - l2 if k in ATTENTION else m)
                    pe.wait_ge(semaphore, value)
                    return

            @block.sync
            def _(sp):
                wq, wk, wv, wod = (t[f"L0_attn_{n}"] for n in ("Wq", "Wk", "Wv", "Wo"))

                def qkv(layer, g):
                    for m, w in enumerate((wq, wk, wv)):
                        heads = w[bass.ds(layer, 1), g * HEADS // 2:(g + 1) * HEADS // 2, :, :]
                        sp.dma_start(raw[g][:, m, :].rearrange("d (h k) -> d h k", k=HK),
                                     heads.rearrange("l h d k -> d (l h) k")).then_inc(raw_in[g], 16)

                def output(layer, g):
                    rows = wod[bass.ds(layer, 1), g * 4 * P:(g + 1) * 4 * P, :]
                    sp.dma_start(wo[g][:, :, :], rows.rearrange("l (c p) d -> p (l c) d", p=P)).then_inc(wo_in[g], 16)

                def ff(layer):
                    sp.dma_start(w1[:, :], t["L0_attn_W1"][bass.ds(layer, 1), :, :].rearrange("l d f -> (l d) f"))\
                        .then_inc(ff_in, 16)
                    sp.dma_start(w2[:, :, :], t["L0_attn_W2"][bass.ds(layer, 1), :, :]
                                 .rearrange("l (c p) d -> p (l c) d", p=P)).then_inc(ff_in, 16)

                for g in range(2):
                    qkv(0, g)
                for g in range(2):
                    output(0, g)
                ff(0)
                with sp.Fori(0, LOOPS) as i:
                    for g in range(2):
                        sp.wait_ge(w_split[g], 3 * (i + 1))
                        qkv(i + 1, g)
                    for g in range(2):
                        sp.wait_ge(wg_ready, 16 * i + 12 + 4 * g)
                        output(i + 1, g)
                    sp.wait_ge(down_ready, 2 * (2 * i + 2))
                    ff(i + 1)

            @block.tensor
            def _(pe):
                def project(n, s, layer, j, m, o, ready):
                    g, cols = j // 4, slice(j % 4 * P, j % 4 * P + P)
                    if j % 4 == 0 and s == 0:
                        pe.wait_ge(w_split[g], 3 * layer + m + 1)
                    if j == 0:
                        at_least(pe, state_l, 2 * (n - 1))
                    h, l = wh[g][:, m, cols], wl[g][:, m, cols]
                    for at in HALF:
                        pe.matmul(o[:, at], h, res_h[:, s, at], start=True, stop=False)
                        pe.matmul(o[:, at], h, res_l[:, s, at], start=False, stop=False)
                        ins = pe.matmul(o[:, at], l, res_h[:, s, at], start=False, stop=True)
                    ins.then_inc(ready, 1)

                def output(n, s, j):
                    u = 8 * n + j
                    if j == 0:
                        at_least(pe, gelu_y, 2 * n)
                    pe.wait_ge(wg_ready, u + 1)
                    pe.wait_ge(miss_ready, u + 1)
                    for at in HALF:
                        ins = pe.matmul(yp[:, at], wg[s][:, j, :], miss[j % 2][:, at], start=(j == 0),
                                        stop=(j == CB - 1))
                    ins.then_inc(wo_done, 1)

                def constant(n, p, o):
                    pe.wait_ge(wg_ready, 8 * n)
                    for b in range(CB):
                        ins = pe.matmul(o[:, 0:1], wg[p][:, b, :], ones[:, 0:1], start=(b == 0), stop=(b == CB - 1))
                    ins.then_inc(const_ready, 1)

                def stage(n, s, layer=0):
                    p = 1 - s
                    for step in PE_ORDER:
                        kind, b, h, late = parse(step)
                        if absent(kind, late, n):
                            continue
                        m, seq, its_layer = attention_of(n, s, layer, late)
                        if kind not in ("out", "down_rest"):
                            if h in (None, 0):
                                tile_free(pe, kind, b, late, n)
                            o = tile_of[(kind, b)]
                        at = HALF[h or 0]
                        half_done = 2 * (n - 1) + (h or 0) + 1
                        if kind == "q":
                            project(m, seq, its_layer, b, 0, o, q_ready)
                        elif kind == "k":
                            project(m, seq, its_layer, b, 1, o, k_ready)
                        elif kind == "v":
                            project(m, seq, its_layer, b, 2, o, v_ready)
                        elif kind == "out":
                            output(m, seq, b)
                        elif kind == "const":
                            constant(n, p, o)
                        elif kind == "centre1":
                            pe.wait_ge(sum1_ready, half_done)
                            pe.matmul(o[:, at], centre[:, :], r_sum[:, at], start=True, stop=True).then_inc(centred1, 1)
                        elif kind == "centre2":
                            pe.wait_ge(sum2_ready, half_done)
                            pe.matmul(o[:, at], centre[:, :], r_sum[:, at], start=True, stop=True).then_inc(centred2, 1)
                        elif kind == "var1":
                            pe.wait_ge(squared1, half_done)
                            pe.matmul(o[:, at], average[:, :], square[:, at], start=True, stop=True)\
                                .then_inc(var1_ready, 1)
                        elif kind == "var2":
                            pe.wait_ge(squared2, half_done)
                            pe.matmul(o[:, at], average[:, :], square[:, at], start=True, stop=True)\
                                .then_inc(var2_ready, 1)
                        elif kind == "up":
                            if b == 0 and h == 0:
                                pe.wait_ge(ff_in, 32 * (layer + 1))
                            if b == 0:
                                pe.wait_ge(mid_ready, half_done)
                            pe.matmul(o[:, at], w1[:, b * P:(b + 1) * P], mid[:, at], start=True, stop=True)\
                                .then_inc(up_ready[h], 1)
                        elif kind == "down":
                            for f in range(FB // 2):
                                pe.wait_ge(hid_ready[h], FB * (n - 1) + f + 1)
                                pe.matmul(o[:, at], w2[:, f, :], hid[:, f, at], start=(f == 0), stop=False)
                        elif kind == "down_rest":
                            o = tile_of[("down", None)]
                            for f in range(FB // 2, FB):
                                pe.wait_ge(hid_ready[h], FB * (n - 1) + f + 1)
                                ins = pe.matmul(o[:, at], w2[:, f, :], hid[:, f, at], start=False, stop=(f == FB - 1))
                            ins.then_inc(down_ready, 1)

                stage(0, 0, -1)
                stage(1, 1, 0)
                stage(2, 0, 0)
                with pe.Fori(1, LOOPS) as i:
                    stage(2 * i + 1, 1, i)
                    stage(2 * i + 2, 0, i)
                stage(STAGES - 1, 1, LAYERS - 1)
                stage(STAGES, 0, LAYERS - 1)

            @block.scalar
            def _(sc):
                def exp_of_q(n, s, j):
                    u = 8 * n + j
                    if j == 0:
                        sc.wait_ge(par_f_ready, n + 1)
                    sc.wait_ge(q_ready, u + 1)
                    at_least(sc, phi_q_ready, u)
                    sc.activation(exp_q[:, :], tile_of[("q", j)][:, :], ACT.Exp, bias=par_f[s][:, 0, j:j + 1])\
                        .then_inc(exp_q_done, 1)

                def exp_of_k(n, s, j):
                    u = 8 * n + j
                    if j == 0:
                        sc.wait_ge(par_f_ready, n + 1)
                    sc.wait_ge(k_ready, u + 1)
                    at_least(sc, phi_k_ready, u)
                    sc.activation(exp_k[:, :], tile_of[("k", j)][:, :], ACT.Exp, bias=par_f[s][:, 1, j:j + 1])\
                        .then_inc(exp_k_done, 1)

                def relu_of_k(n, s, j):
                    sc.activation(relu_k[:, :], tile_of[("k", j)][:, :], ACT.Relu, bias=par_f[s][:, 1, j:j + 1])\
                        .then_inc(relu_done, 1)

                def logarithm(n, j):
                    u = 8 * n + j
                    sc.wait_ge(scale_ready, u + 1)
                    sc.wait_ge(phi_q_ready, u + 1)
                    at_least(sc, miss_ready, u)
                    sc.activation(ln_q[:, :], phi_q[:, :], ACT.Ln, scale=scale[j % 2][:, 0:1], bias=1.0)\
                        .then_inc(ln_done, 1)

                def negated(n, j):
                    u = 8 * n + j
                    sc.wait_ge(ln_done, u + 1)
                    at_least(sc, wo_done, u - 1)
                    sc.activation(miss[j % 2][:, :], ln_q[:, :], ACT.Exp, scale=-1.0).then_inc(miss_ready, 1)

                def stage(n, s, layer=0):
                    p = 1 - s
                    for k, step in enumerate(ACT_ORDER):
                        kind, b, h, late = parse(step)
                        if absent(kind, late, n):
                            continue
                        m, seq, _ = attention_of(n, s, layer, late)
                        at = HALF[h or 0]
                        half_done = 2 * (n - 1) + (h or 0) + 1
                        if kind == "exp_q":
                            exp_of_q(m, seq, b)
                        elif kind == "exp_k":
                            exp_of_k(m, seq, b)
                        elif kind == "relu_k":
                            relu_of_k(m, seq, b)
                        elif kind == "log":
                            logarithm(m, b)
                        elif kind == "miss":
                            negated(m, b)
                        elif kind == "gelu_y":
                            if h == 0:
                                sc.wait_ge(bias_ready, n)
                                sc.wait_ge(wo_done, 8 * n)
                            sc.activation(g_act[:, at], yp[:, at], ACT.Gelu_apprx_tanh, bias=bias_y[:, 0:1],
                                          scale=-1.0).then_inc(gelu_y, 1)
                        elif kind == "hidden":
                            sc.wait_ge(up_ready[h], FB * (n - 1) + b + 1)
                            sc.activation(hid[:, b, at], tile_of[("up", b)][:, at], ACT.Gelu_apprx_tanh,
                                          bias=par_g[p][:, FF1 + b:FF1 + b + 1]).then_inc(hid_ready[h], 1)
                        elif kind == "gelu_down":
                            sc.wait_ge(down_ready, half_done)
                            sc.activation(g_act[:, at], tile_of[("down", None)][:, at], ACT.Gelu_apprx_tanh,
                                          bias=par_g[p][:, B2:B2 + 1]).then_inc(gelu_down, 1)
                        elif kind == "square1":
                            sc.wait_ge(centred1, half_done)
                            sc.activation(square[:, at], tile_of[("centre1", None)][:, at], ACT.Square)\
                                .then_inc(squared1, 1)
                        elif kind == "square2":
                            sc.wait_ge(centred2, half_done)
                            sc.activation(square[:, at], tile_of[("centre2", None)][:, at], ACT.Square)\
                                .then_inc(squared2, 1)
                        elif kind == "ln_var1":
                            sc.wait_ge(var1_ready, half_done)
                            sc.activation(rstd[:, at], tile_of[("var1", None)][:, at], ACT.Ln, bias=ln_eps[:, 0:1])\
                                .then_inc(ln_var1, 1)
                        elif kind == "ln_var2":
                            sc.wait_ge(var2_ready, half_done)
                            sc.activation(rstd[:, at], tile_of[("var2", None)][:, at], ACT.Ln, bias=ln_eps[:, 0:1])\
                                .then_inc(ln_var2, 1)
                        elif kind == "rstd1":
                            sc.wait_ge(ln_var1, half_done)
                            sc.activation(rstd[:, at], rstd[:, at], ACT.Exp, scale=-0.5).then_inc(rstd1_ready, 1)
                        elif kind == "rstd2":
                            sc.wait_ge(ln_var2, half_done)
                            sc.activation(rstd[:, at], rstd[:, at], ACT.Exp, scale=-0.5).then_inc(rstd2_ready, 1)
                        if kind in GELUS and not (ACT_ORDER[k + 1:] and parse(ACT_ORDER[k + 1])[0] in GELUS):
                            sc.preload_act_table_set(EXP_LN)

                sc.preload_act_table_set(EXP_LN)
                stage(0, 0)
                stage(1, 1)
                stage(2, 0)
                with sc.Fori(1, LOOPS) as i:
                    stage(2 * i + 1, 1)
                    stage(2 * i + 2, 0)
                stage(STAGES - 1, 1)
                stage(STAGES, 0)

            @block.gpsimd
            def _(pool):
                def stage(n):
                    for step in POOL_ORDER:
                        kind, j, _, late = parse(step)
                        if absent(kind, late, n):
                            continue
                        u = 8 * (n - late) + j
                        pool.wait_ge(curve_done, u + 1)
                        pool.wait_ge(line_done, u + 1)
                        at_least(pool, ln_done, u)
                        pool.tensor_tensor(phi_q[:, :], exp_q[:, :], line_q[:, :], ALU.add).then_inc(phi_q_ready, 1)

                for n in range(3):
                    stage(n)
                with pool.Fori(1, LOOPS) as i:
                    stage(2 * i + 1)
                    stage(2 * i + 2)
                stage(STAGES - 1)
                stage(STAGES)

            @block.vector
            def _(v):
                def split(g, m, layer):
                    v.wait_ge(raw_in[g], 48 * (layer + 1))
                    v.tensor_copy(wh[g][:, m, :], raw[g][:, m, :]).then_inc(w_upper[g], 1)
                    v.wait_ge(w_upper[g], 3 * layer + m + 1)
                    v.tensor_tensor(wl[g][:, m, :], raw[g][:, m, :], wh[g][:, m, :].bitcast(F32),
                                    ALU.subtract).then_inc(w_split[g], 1)

                def line_of_q(n, s, j):
                    v.wait_ge(exp_q_done, 8 * n + j + 1)
                    v.tensor_scalar(line_q[:, :], tile_of[("q", j)][:, :], par_f[s][:, 3, j:j + 1], 1.0, ALU.add,
                                    ALU.max).then_inc(line_done, 1)

                def curve_of_q(n, j):
                    v.wait_ge(exp_q_done, 8 * n + j + 1)
                    v.tensor_scalar(exp_q[:, :], exp_q[:, :], 1.0, -1.0, ALU.min, ALU.add).then_inc(curve_done, 1)

                def feature_map_k(n, j):
                    u, k = 8 * n + j, j % 2
                    v.wait_ge(relu_done, u + 1)
                    v.wait_ge(exp_k_done, u + 1)
                    at_least(v, kv_done, u)
                    at_least(v, scale_ready, u - 1)
                    at_least(v, guarded, u - 1)
                    v.scalar_tensor_tensor(out=phi_k[:, :], in0=exp_k[:, :], scalar=1.0, in1=relu_k[:, :],
                                           op0=ALU.min, op1=ALU.add, accum_out=sum_k[k][:, 0:1])\
                        .then_inc(phi_k_ready, 1)

                def scales(n, j):
                    u, k = 8 * n + j, j % 2
                    v.wait_ge(phi_k_ready, u + 1)
                    at_least(v, ln_done, u - 1)
                    v.tensor_scalar(scale[k][:, :], sum_k[k][:, :], 1.0 / Z_EPS, None, ALU.mult)\
                        .then_inc(scale_ready, 1)

                def sum_of_kv(n, j):
                    u, k = 8 * n + j, j % 2
                    v.wait_ge(v_ready, u + 1)
                    v.wait_ge(phi_k_ready, u + 1)
                    at_least(v, mean_v_ready, u - 1)
                    v.tensor_tensor_reduce(phi_k[:, :], phi_k[:, :], tile_of[("v", j)][:, :], 1.0, 0.0,
                                           ALU.mult, ALU.add, sum_kv[k][:, 0:1]).then_inc(kv_done, 1)

                def inverse(n, j):
                    u, k = 8 * n + j, j % 2
                    v.wait_ge(phi_k_ready, u + 1)
                    at_least(v, mean_v_ready, u - 1)
                    v.tensor_scalar(inv[k][:, :], sum_k[k][:, :], TINY, None, ALU.max).then_inc(guarded, 1)
                    v.wait_ge(guarded, 8 * n + j + 1)
                    v.reciprocal(inv[j % 2][:, :], inv[j % 2][:, :]).then_inc(inv_ready, 1)

                def mean_of_v(n, s, j):
                    u, k = 8 * n + j, j % 2
                    v.wait_ge(inv_ready, u + 1)
                    v.wait_ge(kv_done, u + 1)
                    at_least(v, wg_ready, u - 1)
                    v.scalar_tensor_tensor(out=mean_v[k][:, :], in0=sum_kv[k][:, :], scalar=inv[k][:, 0:1],
                                           in1=par_f[s][:, 2, j:j + 1], op0=ALU.mult, op1=ALU.add)\
                        .then_inc(mean_v_ready, 1)

                def scale_output(n, s, layer, j):
                    if s == 0 and j % 4 == 0:
                        v.wait_ge(wo_in[j // 4], 16 * (layer + 1))
                    v.wait_ge(mean_v_ready, 8 * n + j + 1)
                    v.tensor_scalar(wg[s][:, j, :], wo[j // 4][:, j % 4, :], mean_v[j % 2][:, 0:1], None,
                                    ALU.mult).then_inc(wg_ready, 1)

                def stage(n, s, layer=0, following=None):
                    p = 1 - s
                    if not absent("gelu_y", False, n):
                        v.tensor_copy(par_g[p][:, :], table_g[:, bass.ds(layer, 1), :]
                                      .rearrange("p l k -> p (l k)")).then_inc(par_g_ready, 1)
                    for step in DVE_ORDER:
                        kind, b, h, late = parse(step)
                        if absent(kind, late, n):
                            continue
                        m, seq, its_layer = attention_of(n, s, layer, late)
                        at = HALF[h or 0]
                        half_done = 2 * (n - 1) + (h or 0) + 1
                        if kind == "line_q":
                            line_of_q(m, seq, b)
                        elif kind == "curve_q":
                            curve_of_q(m, b)
                        elif kind == "phi_k":
                            feature_map_k(m, b)
                        elif kind == "scale":
                            scales(m, b)
                        elif kind == "kv":
                            sum_of_kv(m, b)
                        elif kind == "inverse":
                            inverse(m, b)
                        elif kind == "mean_v":
                            mean_of_v(m, seq, b)
                        elif kind == "scale_wo":
                            scale_output(m, seq, its_layer, b)
                        elif kind == "columns":
                            v.tensor_copy(par_f[p][:, :, :], table_f[:, bass.ds(following, 1), :, :]
                                          .rearrange("p l k c -> p (l k) c")).then_inc(par_f_ready, 1)
                        elif kind == "split_odd":
                            if s == 1:
                                v.wait_ge((q_ready, k_ready, v_ready)[b], 8 * n + 4)
                                split(0, b, following)
                        elif kind == "split_even":
                            if s == 0:
                                at_least(v, (q_ready, k_ready, v_ready)[b], 8 * n)
                                split(1, b, following)
                        elif kind == "bias_y":
                            v.wait_ge(const_ready, n)
                            v.wait_ge(par_g_ready, n)
                            v.tensor_scalar(bias_y[:, :], tile_of[("const", None)][:, 0:1], par_g[p][:, BO:BO + 1],
                                            None, ALU.add).then_inc(bias_ready, 1)
                        elif kind == "residual1":
                            v.wait_ge(gelu_y, half_done)
                            v.tensor_tensor(r_sum[:, at], g_act[:, at], res[:, p, at], ALU.add).then_inc(sum1_ready, 1)
                        elif kind == "norm1":
                            v.wait_ge(rstd1_ready, half_done)
                            v.scalar_tensor_tensor(out=normal[:, at], in0=tile_of[("centre1", None)][:, at],
                                                   scalar=par_g[p][:, S1:S1 + 1], in1=rstd[:, at],
                                                   op0=ALU.mult, op1=ALU.mult).then_inc(normed1, 1)
                        elif kind == "mid":
                            v.wait_ge(normed1, half_done)
                            v.tensor_scalar(mid[:, at], normal[:, at], par_g[p][:, S1 + 1:S1 + 2], None, ALU.add)\
                                .then_inc(mid_ready, 1)
                        elif kind == "residual2":
                            v.wait_ge(gelu_down, half_done)
                            v.tensor_tensor(r_sum[:, at], g_act[:, at], mid[:, at], ALU.add).then_inc(sum2_ready, 1)
                        elif kind == "norm2":
                            v.wait_ge(rstd2_ready, half_done)
                            v.scalar_tensor_tensor(out=normal[:, at], in0=tile_of[("centre2", None)][:, at],
                                                   scalar=par_g[p][:, S2:S2 + 1], in1=rstd[:, at],
                                                   op0=ALU.mult, op1=ALU.mult).then_inc(normed2, 1)
                        elif kind == "state":
                            v.wait_ge(normed2, half_done)
                            v.tensor_scalar(res[:, p, at], normal[:, at], par_g[p][:, S2 + 1:S2 + 2], None, ALU.add)\
                                .then_inc(state_ready, 1)
                        elif kind == "state_upper":
                            v.wait_ge(state_ready, half_done)
                            v.tensor_copy(res_h[:, p, at], res[:, p, at]).then_inc(state_h, 1)
                        elif kind == "state_lower":
                            v.wait_ge(state_h, half_done)
                            v.tensor_tensor(res_l[:, p, at], res[:, p, at], res_h[:, p, at].bitcast(F32),
                                            ALU.subtract).then_inc(state_l, 1)

                v.tensor_copy(par_f[0][:, :, :], table_f[:, 0, :, :]).then_inc(par_f_ready, 1)
                for m in range(3):
                    split(0, m, 0)
                stage(0, 0, -1, 0)
                stage(1, 1, 0, 1)
                stage(2, 0, 0, 1)
                with v.Fori(1, LOOPS) as i:
                    stage(2 * i + 1, 1, i, i + 1)
                    stage(2 * i + 2, 0, i, i + 1)
                stage(STAGES - 1, 1, LAYERS - 1)
                stage(STAGES, 0, LAYERS - 1)

        with ExitStack() as c:
            prod = sb("gated", [P, T], F32, c)
            back = [c.enter_context(nc.psum_tensor(f"back{q}", [P, N], F32)) for q in range(CHUNKS)]
            gated, turned = sem("gated_ready", c), sem("turned_back", c)
            added, stored = sem("output_ready", c), sem("output_stored", c)
            block = c.enter_context(nc.Block())

            @block.vector
            def _(v):
                for q in range(CHUNKS):
                    at = slice(q * N, (q + 1) * N)
                    v.tensor_tensor(prod[:, at], res[:, q // 2, q % 2 * N:(q % 2 + 1) * N], gate[:, at], ALU.mult)\
                        .then_inc(gated, 1)
                for q in range(CHUNKS):
                    v.wait_ge(turned, q + 1)
                    v.tensor_tensor(x[:, 4 * q:4 * q + 4, :], x[:, 4 * q:4 * q + 4, :],
                                    back[q][:, :].rearrange("p (b d) -> p b d", d=P), ALU.add).then_inc(added, 1)

            @block.tensor
            def _(pe):
                for q in range(CHUNKS):
                    pe.wait_ge(gated, q + 1)
                    for b in range(4):
                        at = slice((4 * q + b) * P, (4 * q + b + 1) * P)
                        ins = pe.transpose(back[q][:, b * P:(b + 1) * P], prod[:, at], ident[:, :])
                    ins.then_inc(turned, 1)

            @block.sync
            def _(sp):
                for q in range(CHUNKS):
                    sp.wait_ge(added, q + 1)
                    sp.dma_start(out_tokens[:, 4 * q:4 * q + 4, :], x[:, 4 * q:4 * q + 4, :]).then_inc(stored, 16)
                sp.wait_ge(stored, 16 * CHUNKS)


INPUTS = ["L0_attn_x"] + [f"L0_attn_{n}" for n in (
    "Wq", "bq", "Wk", "bk", "Wv", "bv", "Wo", "bo", "ln1_s", "ln1_b", "W1", "b1", "W2", "b2", "ln2_s", "ln2_b")] \
    + [f"L0_ffn_{n}" for n in (
        "gw", "gb", "w1", "b1", "w3", "b3", "w2", "b2", "sw1", "sb1", "sw3", "sb3", "sw2", "sb2")]


def kernel(**inputs):
    import concourse.bacc as bacc
    from concourse.bass_utils import run_bass_kernel_spmd

    nc = bacc.Bacc("TRN2", target_bir_lowering=False, num_devices=1)
    arrays, tensors = {}, {}
    for name in INPUTS:
        a = np.ascontiguousarray(inputs[name])
        arrays[f"in_{name}"] = a
        tensors[name] = nc.dram_tensor(f"in_{name}", a.shape, mybir.dt.from_np(a.dtype), kind="ExternalInput").ap()
    x = arrays["in_L0_attn_x"]
    out = nc.dram_tensor("out", x.shape, mybir.dt.from_np(x.dtype), kind="ExternalOutput").ap()
    recurrent_attention_gated_by_experts(nc, tensors, out)
    return run_bass_kernel_spmd(nc, [arrays], core_ids=[0]).results[0]["out"]
```

```python
from contextlib import ExitStack

import numpy as np

import concourse.bass as bass
from concourse import mybir

ALU = mybir.AluOpType
ACT = mybir.ActivationFunctionType
AXX = mybir.AxisListType.X
F32 = mybir.dt.float32
F32R = mybir.dt.float32r

P = 128
LN_EPS = 1e-6
Z_EPS = 1e-6
IN_EPS = 1e-5
TINY = 1e-38
EXP_LN = "natural_log_exp_and_others"


def at_least(engine, semaphore, value):
    if isinstance(value, int) and value <= 0:
        return
    engine.wait_ge(semaphore, value)


def over(ap, axis, shape):
    return ap.unsqueeze(axis).broadcast_to(shape)


def recurrent_attention_gated_by_experts(nc: bass.Bass, t: dict, out: bass.AP):
    x_in = t["L0_attn_x"]
    SEQS, S, D = x_in.shape
    LAYERS, HEADS, _, HK = t["L0_attn_Wq"].shape
    FF = t["L0_attn_W1"].shape[2]
    EXPERTS, _, INTER = t["L0_ffn_w1"].shape
    T = SEQS * S
    TB = T // P
    CB = HEADS * HK // P
    FB = FF // P
    PAIRS = EXPERTS // 2
    N = 512
    CHUNKS = T // N
    GROUPS, PER_GROUP, TOP_GROUPS, TOP = 8, EXPERTS // 8, 4, 4
    STAGES = SEQS * LAYERS
    assert D == P and SEQS == 2 and S == 2 * N and 2 * INTER == P and CB == 8 and FB == 4

    x_tokens = x_in.rearrange("n s d -> (n s) d").rearrange("(b p) d -> p b d", p=P)
    out_tokens = out.rearrange("n s d -> (n s) d").rearrange("(b p) d -> p b d", p=P)
    weights_by_pair = nc.dram_tensor("expert_weights", [EXPERTS, T], F32, kind="Internal").ap()

    with ExitStack() as whole:
        def sb(name, shape, dtype=F32, ctx=whole):
            return ctx.enter_context(nc.sbuf_tensor(name, shape, dtype))

        def sem(name, ctx=whole):
            return ctx.enter_context(nc.semaphore(name))

        ident = sb("ident", [P, P])
        centre = sb("centre", [P, P])
        average = sb("average", [P, P])
        ones = sb("ones", [P, 2])
        ln_eps = sb("ln_eps", [P, 1])
        x = sb("x", [P, TB, P])
        res = sb("res", [P, SEQS, S])
        res_h = sb("res_h", [P, SEQS, S], F32R)
        res_l = sb("res_l", [P, SEQS, S], F32R)
        gate = sb("gate", [P, T])
        rows_qk = sb("rows_qk", [P, P])
        rows_v1 = sb("rows_v1", [P, P])
        rows_misc = sb("rows_misc", [P, P])
        NG = FB + 6
        table_f = sb("table_f", [P, LAYERS, 4, CB])
        table_g = sb("table_g", [P, LAYERS, NG])
        moe_b13 = sb("moe_b13", [P, PAIRS + 1, 2])
        moe_sb2 = sb("moe_sb2", [P, 1])
        qkv_raw = [sb(f"qkv_raw{g}", [P, 3, S // 2]) for g in range(2)]
        qkv_h = [sb(f"qkv_h{g}", [P, 3, S // 2], F32R) for g in range(2)]
        qkv_l = [sb(f"qkv_l{g}", [P, 3, S // 2], F32R) for g in range(2)]
        w1 = sb("ff1", [P, FF])
        w1_h, w1_l = (sb(f"ff1_{k}", [P, FF], F32R) for k in "hl")
        qkv_in = [sem(f"qkv_loaded{g}") for g in range(2)]
        qkv_upper, qkv_split = [[sem(f"{n}{g}") for g in range(2)] for n in ("qkv_upper_ready", "qkv_split")]
        w1_in, w1_upper, w1_split = sem("ff1_loaded"), sem("ff1_upper_ready"), sem("ff1_split")

        routing = whole.enter_context(ExitStack())
        cwT = sb("cwT", [EXPERTS, T], F32, routing)
        EARLY = 3
        early_w13 = [sb(f"early_w13_{u}", [P, 2, P], F32, routing) for u in range(EARLY)]
        early_w2 = [sb(f"early_w2_{u}", [P, P], F32, routing) for u in range(EARLY)]
        early_hid = [sb(f"early_hidden{u}", [P, T], F32, routing) for u in range(EARLY)]
        expert_raw = [sb(f"expert_raw{k}", [P, 2, P], F32, routing) for k in range(2)]
        w13_h = [sb(f"w13_h{k}", [P, 2, P], F32R, routing) for k in range(2)]
        w13_l = [sb(f"w13_l{k}", [P, 2, P], F32R, routing) for k in range(2)]
        b13 = [sb(f"b13_{k}", [P, 2], F32, routing) for k in range(2)]
        expert_b2 = sb("experts_b2", [EXPERTS, P], F32, routing)
        expert_in = [sem(f"w13_loaded{k}", routing) for k in range(2)]
        b2_in = sem("b2_loaded", routing)
        weights_stored = sem("expert_weights_stored", routing)
        bias_placed = sem("bias_placed", routing)
        upper_ready, split_ready = sem("w13_upper_ready", routing), sem("w13_split", routing)
        w1d, w3d, w2d = (t[f"L0_ffn_{n}"] for n in ("w1", "w3", "w2"))

        def load_w13(sp, pair, k):
            for m, w in enumerate((w1d, w3d)):
                sp.dma_start(expert_raw[k][:, m, :].rearrange("d (e k) -> d e k", e=2),
                             w[bass.ds(2 * pair, 2), :, :].rearrange("e d k -> d e k")).then_inc(expert_in[k], 16)

        def split_w13(v, k, turn, pair, loads):
            v.wait_ge(expert_in[k], 32 * loads)
            v.tensor_scalar(b13[k][:, :], moe_b13[:, bass.ds(pair, 1), :].rearrange("p l k -> p (l k)"), 0.0, None,
                            ALU.add).then_inc(bias_placed, 1)
            v.wait_ge(bias_placed, turn + 1)
            v.tensor_copy(w13_h[k][:, :, :], expert_raw[k][:, :, :]).then_inc(upper_ready, 1)
            v.wait_ge(upper_ready, turn + 1)
            v.tensor_tensor(w13_l[k][:, :, :], expert_raw[k][:, :, :], w13_h[k][:, :, :].bitcast(F32),
                            ALU.subtract).then_inc(split_ready, 1)

        def load_qkv(sp, layer, g):
            for m, n in enumerate(("Wq", "Wk", "Wv")):
                heads = t[f"L0_attn_{n}"][bass.ds(layer, 1), g * HEADS // 2:(g + 1) * HEADS // 2, :, :]
                sp.dma_start(qkv_raw[g][:, m, :].rearrange("d (h k) -> d h k", k=HK),
                             heads.rearrange("l h d k -> d (l h) k")).then_inc(qkv_in[g], 16)

        def split_qkv(v, g, m, layer):
            v.wait_ge(qkv_in[g], 48 * (layer + 1))
            v.tensor_copy(qkv_h[g][:, m, :], qkv_raw[g][:, m, :]).then_inc(qkv_upper[g], 1)
            v.wait_ge(qkv_upper[g], 3 * layer + m + 1)
            v.tensor_tensor(qkv_l[g][:, m, :], qkv_raw[g][:, m, :], qkv_h[g][:, m, :].bitcast(F32),
                            ALU.subtract).then_inc(qkv_split[g], 1)

        def load_w1(sp, layer):
            sp.dma_start(w1[:, :], t["L0_attn_W1"][bass.ds(layer, 1), :, :].rearrange("l d f -> (l d) f"))\
                .then_inc(w1_in, 16)

        def split_w1(v, layer):
            v.wait_ge(w1_in, 16 * (layer + 1))
            v.tensor_copy(w1_h[:, :], w1[:, :]).then_inc(w1_upper, 1)
            v.wait_ge(w1_upper, layer + 1)
            v.tensor_tensor(w1_l[:, :], w1[:, :], w1_h[:, :].bitcast(F32), ALU.subtract).then_inc(w1_split, 1)

        with ExitStack() as c:
            gw = sb("gw", [P, EXPERTS], F32, c)
            gb = sb("gb", [P, EXPERTS], F32, c)
            xc = sb("xc", [P, TB, P], F32, c)
            sq = sb("sq", [P, TB, P], F32, c)
            mean = sb("mean", [P, TB], F32, c)
            var = sb("var", [P, TB], F32, c)
            root = sb("root", [P, TB], F32, c)
            rstd = sb("rstd", [P, TB], F32, c)
            corr = sb("corr", [P, TB], F32, c)
            lg = sb("lg", [P, TB, EXPERTS], F32, c)
            prob = sb("prob", [P, TB, EXPERTS], F32, c)
            col = sb("col", [P, TB], F32, c)
            tot = sb("tot", [P, TB], F32, c)
            hi2 = sb("hi2", [P, TB * GROUPS, 2], F32, c)
            lo2 = sb("lo2", [P, TB * GROUPS, 2], F32, c)
            first = sb("first", [P, TB * GROUPS], F32, c)
            second = sb("second", [P, TB * GROUPS], F32, c)
            score = sb("score", [P, TB, GROUPS], F32, c)
            above = sb("above", [P, TB, GROUPS, GROUPS], F32, c)
            equal = sb("equal", [P, TB, GROUPS, GROUPS], F32, c)
            earlier = sb("earlier", [P, GROUPS, GROUPS], F32, c)
            keep = sb("keep", [P, TB, GROUPS], F32, c)
            drop = sb("drop", [P, TB, GROUPS], F32, c)
            masked = sb("masked", [P, TB, EXPERTS], F32, c)
            best = sb("best", [P, TB, 8], F32, c)
            more = sb("more", [P, TB, EXPERTS], F32, c)
            tie = [sb(f"tie{k}", [P, TB, 2 * EXPERTS], F32, c) for k in range(2)]
            cw = sb("cw", [P, TB, EXPERTS], F32, c)
            early_a = [sb(f"early_a{k}", [P, N], F32, c) for k in range(2)]
            early_c = [sb(f"early_c{k}", [P, N], F32, c) for k in range(2)]
            ps = [c.enter_context(nc.psum_tensor(f"ps{k}", [P, N], F32)) for k in range(8)]
            TURN_BANKS = ps[0], ps[5], ps[6], ps[7]

            x_in_sem, rows_in, gate_in = sem("x_loaded", c), sem("rows_loaded", c), sem("gate_weights_loaded", c)
            consts = sem("constants_ready", c)
            turned = sem("transposed", c)
            dve = sem("vector_steps", c)
            state_ready = sem("state_copied", c)
            root_ready, exp_ready = sem("root_ready", c), sem("exp_ready", c)
            columns_ready = sem("weights_transposed", c)
            early_in = sem("early_weights_loaded", c)
            early_up, early_silu, early_linear, early_ready = (sem(n, c) for n in (
                "early_up_ready", "early_silu_ready", "early_linear_ready", "early_hidden_ready"))

            block = c.enter_context(nc.Block())
            ROWS = []
            r = 0
            for name, tile in (("L0_attn_bq", rows_qk), ("L0_attn_bk", rows_qk)):
                ROWS.append((tile, r, t[name].rearrange("l h k -> l (h k)").rearrange("l (c p) -> (l c) p", p=P)))
                r += LAYERS * CB
            r = 0
            for ap in (t["L0_attn_bv"].rearrange("l h k -> l (h k)").rearrange("l (c p) -> (l c) p", p=P),
                       t["L0_attn_b1"].rearrange("l (c p) -> (l c) p", p=P),
                       t["L0_ffn_b1"].rearrange("e k -> (e k)").rearrange("(r p) -> r p", p=P),
                       t["L0_ffn_b3"].rearrange("e k -> (e k)").rearrange("(r p) -> r p", p=P)):
                ROWS.append((rows_v1, r, ap))
                r += ap.shape[0]
            r = 0
            for name in ("bo", "b2", "ln1_s", "ln1_b", "ln2_s", "ln2_b"):
                ROWS.append((rows_misc, r, t[f"L0_attn_{name}"]))
                r += LAYERS
            for name in ("sb1", "sb3", "sb2"):
                ROWS.append((rows_misc, r, t[f"L0_ffn_{name}"].rearrange("(r p) -> r p", p=P)))
                r += 1
            MISC = r

            mark = {}

            @block.vector
            def _(v):
                n = [0]

                def done(ins, name=None):
                    free(ins, name)
                    v.wait_ge(dve, n[0])

                def free(ins, name=None):
                    ins.then_inc(dve, 1)
                    n[0] += 1
                    if name:
                        mark[name] = n[0]

                def tt(o, a, b, op, name=None):
                    done(v.tensor_tensor(o, a, b, op), name)

                def ts(o, a, s1, s2, op0, op1=ALU.bypass, name=None):
                    done(v.tensor_scalar(o, a, s1, s2, op0, op1), name)

                wide = [P, TB, P]
                v.wait_ge(consts, 10)
                v.wait_ge(x_in_sem, 64)
                done(v.tensor_reduce(mean[:, :], x[:, :, :], AXX, ALU.add))
                ts(mean[:, :], mean[:, :], 1.0 / P, None, ALU.mult)
                tt(xc[:, :, :], x[:, :, :], over(mean[:, :], 2, wide), ALU.subtract)
                tt(sq[:, :, :], xc[:, :, :], xc[:, :, :], ALU.mult)
                done(v.tensor_reduce(var[:, :], sq[:, :, :], AXX, ALU.add))
                ts(var[:, :], var[:, :], 1.0 / P, IN_EPS, ALU.mult, ALU.add, name="var")
                v.wait_ge(root_ready, 1)
                done(v.reciprocal(rstd[:, :], root[:, :]))
                tt(corr[:, :], rstd[:, :], rstd[:, :], ALU.mult)
                tt(corr[:, :], corr[:, :], var[:, :], ALU.mult)
                ts(corr[:, :], corr[:, :], -0.5, 1.5, ALU.mult, ALU.add)
                tt(rstd[:, :], rstd[:, :], corr[:, :], ALU.mult)
                for q in range(CHUNKS):
                    blocks = slice(4 * q, 4 * q + 4)
                    free(v.tensor_tensor(xc[:, blocks, :], xc[:, blocks, :], over(rstd[:, blocks], 2, [P, 4, P]),
                                         ALU.mult), f"normed{q}")
                free(v.tensor_scalar(centre[:, :], ident[:, :], -1.0 / P, None, ALU.add))
                v.wait_ge(turned, 1)
                rows = ps[0]
                qk = rows[:, 0:P].rearrange("p (m l c) -> p l m c", m=2, c=CB)
                done(v.tensor_copy(table_f[:, :, 0:2, :], qk))
                free(v.tensor_scalar(table_f[:, :, 3, :], table_f[:, :, 0, :], 1.0, None, ALU.add))
                at = P
                free(v.tensor_copy(table_f[:, :, 2, :], rows[:, at:at + LAYERS * CB].rearrange("p (l c) -> p l c", c=CB)))
                at += LAYERS * CB
                free(v.tensor_copy(table_g[:, :, 6:6 + FB], rows[:, at:at + LAYERS * FB].rearrange("p (l c) -> p l c", c=FB)))
                at += LAYERS * FB
                free(v.tensor_copy(moe_b13[:, 0:PAIRS, 0], rows[:, at:at + PAIRS]))
                at += PAIRS
                free(v.tensor_copy(moe_b13[:, 0:PAIRS, 1], rows[:, at:at + PAIRS]))
                at += PAIRS
                free(v.tensor_copy(table_g[:, :, 0:6], rows[:, at:at + 6 * LAYERS].rearrange("p (k l) -> p l k", l=LAYERS)))
                at += 6 * LAYERS
                free(v.tensor_copy(moe_b13[:, PAIRS, :], rows[:, at:at + 2]))
                free(v.tensor_copy(moe_sb2[:, :], rows[:, at + 2:at + 3]), "columns")
                for s in range(SEQS):
                    v.wait_ge(state_ready, 4 * (s + 1))
                    free(v.tensor_tensor(res_l[:, s, :], res[:, s, :], res_h[:, s, :].bitcast(F32), ALU.subtract))
                per = [P, TB, EXPERTS]
                v.wait_ge(turned, 2 + CHUNKS)
                v.wait_ge(gate_in, 32)
                logits = ps[5][:, :].rearrange("p (b e) -> p b e", e=EXPERTS)
                tt(lg[:, :, :], logits, over(gb[:, :], 1, per), ALU.add)
                done(v.tensor_reduce(col[:, :], lg[:, :, :], AXX, ALU.max))
                tt(lg[:, :, :], lg[:, :, :], over(col[:, :], 2, per), ALU.subtract, name="logits")
                v.wait_ge(exp_ready, 1)
                done(v.tensor_reduce(tot[:, :], prob[:, :, :], AXX, ALU.add))
                done(v.reciprocal(tot[:, :], tot[:, :]))
                tt(prob[:, :, :], prob[:, :, :], over(tot[:, :], 2, per), ALU.mult)
                fours = prob[:, :, :].rearrange("p b (g k) -> p (b g) k", k=PER_GROUP)
                free(v.tensor_tensor(hi2[:, :, :], fours[:, :, 0:2], fours[:, :, 2:4], ALU.max))
                tt(lo2[:, :, :], fours[:, :, 0:2], fours[:, :, 2:4], ALU.min)
                free(v.tensor_tensor(first[:, :], hi2[:, :, 0], hi2[:, :, 1], ALU.max))
                free(v.tensor_tensor(second[:, :], hi2[:, :, 0], hi2[:, :, 1], ALU.min))
                tt(lo2[:, :, 0], lo2[:, :, 0], lo2[:, :, 1], ALU.max)
                tt(second[:, :], second[:, :], lo2[:, :, 0], ALU.max)
                tt(score[:, :, :].rearrange("p b g -> p (b g)"), first[:, :], second[:, :], ALU.add)
                by = [P, TB, GROUPS, GROUPS]
                theirs, own = over(score[:, :, :], 2, by), over(score[:, :, :], 3, by)
                free(v.tensor_tensor(above[:, :, :, :], theirs, own, ALU.is_gt))
                tt(equal[:, :, :, :], theirs, own, ALU.is_equal)
                tt(equal[:, :, :, :], equal[:, :, :, :], over(earlier[:, :, :], 1, by), ALU.mult)
                tt(above[:, :, :, :], above[:, :, :, :], equal[:, :, :, :], ALU.add)
                done(v.tensor_reduce(keep[:, :, :], above[:, :, :, :], AXX, ALU.add))
                ts(keep[:, :, :], keep[:, :, :], float(TOP_GROUPS), None, ALU.is_lt)
                ts(drop[:, :, :], keep[:, :, :], -1.0, None, ALU.add)
                m4 = masked[:, :, :].rearrange("p b (g k) -> p (b g) k", k=PER_GROUP)
                grp = [P, TB * GROUPS, PER_GROUP]
                tt(m4, fours, over(keep[:, :, :].rearrange("p b g -> p (b g)"), 2, grp), ALU.mult)
                tt(m4, m4, over(drop[:, :, :].rearrange("p b g -> p (b g)"), 2, grp), ALU.add)
                for b in range(TB):
                    free(v.max(best[:, b, :], masked[:, b, :]))
                v.wait_ge(dve, n[0])
                least = best[:, :, TOP - 1:TOP].broadcast_to(per)
                real = slice(EXPERTS, 2 * EXPERTS)
                free(v.tensor_tensor(more[:, :, :], masked[:, :, :], least, ALU.is_gt))
                free(v.tensor_tensor(tie[0][:, :, real], masked[:, :, :], least, ALU.is_equal))
                tt(cw[:, :, :], masked[:, :, :], least, ALU.is_equal)
                done(v.tensor_reduce(col[:, :], more[:, :, :], AXX, ALU.add))
                ts(col[:, :], col[:, :], -1.0, float(TOP), ALU.mult, ALU.add)
                k, a = 1, 0
                while k < EXPERTS:
                    tt(tie[1 - a][:, :, real], tie[a][:, :, real],
                       tie[a][:, :, EXPERTS - k:2 * EXPERTS - k], ALU.add)
                    k, a = 2 * k, 1 - a
                tt(lg[:, :, :], tie[a][:, :, real], over(col[:, :], 2, per), ALU.is_le)
                tt(cw[:, :, :], cw[:, :, :], lg[:, :, :], ALU.mult)
                tt(cw[:, :, :], cw[:, :, :], more[:, :, :], ALU.add)
                tt(cw[:, :, :], cw[:, :, :], prob[:, :, :], ALU.mult, name="weights")
                split_w13(v, 0, 0, EARLY - 1, 1)

            @block.sync
            def _(sp):
                for q in range(4):
                    sp.dma_start(x[:, 4 * q:4 * q + 4, :], x_tokens[:, 4 * q:4 * q + 4, :]).then_inc(x_in_sem, 16)
                sp.dma_start(gw[:, :], t["L0_ffn_gw"]).then_inc(gate_in, 16)
                sp.dma_start(gb[:, :], t["L0_ffn_gb"].rearrange("(a e) -> a e", a=1).broadcast_to([P, EXPERTS]))\
                    .then_inc(gate_in, 16)
                for u in range(EARLY - 1):
                    for m, w in enumerate((w1d, w3d)):
                        sp.dma_start(early_w13[u][:, m, :].rearrange("d (e k) -> d e k", e=2),
                                     w[2 * u:2 * u + 2, :, :].rearrange("e d k -> d e k")).then_inc(early_in, 16)
                for m, n in enumerate(("sw1", "sw3")):
                    sp.dma_start(early_w13[EARLY - 1][:, m, :], t[f"L0_ffn_{n}"]).then_inc(early_in, 16)
                for k in range(2):
                    load_w13(sp, EARLY - 1 + k, k)
                sp.dma_start(expert_b2[:, :], t["L0_ffn_b2"]).then_inc(b2_in, 16)
                sp.wait_ge(columns_ready, CHUNKS)
                sp.dma_start(weights_by_pair, cwT[:, :]).then_inc(weights_stored, 16)

            @block.gpsimd
            def _(pool):
                pool.memset(ident[:, :], 0.0).then_inc(consts, 1)
                pool.memset(average[:, :], 1.0 / P).then_inc(consts, 1)
                pool.memset(ones[:, :], 1.0).then_inc(consts, 1)
                pool.memset(ln_eps[:, :], LN_EPS).then_inc(consts, 1)
                pool.memset(earlier[:, :, :], 1.0).then_inc(consts, 1)
                pool.memset(rows_misc[:, :], 0.0).then_inc(consts, 1)
                for k in range(2):
                    pool.memset(tie[k][:, :, :], 0.0).then_inc(consts, 1)
                pool.wait_ge(consts, 8)
                pool.affine_select(out=ident[:, :], in_=ident[:, :], compare_op=ALU.not_equal, fill=1.0, base=0,
                                   pattern=[[-1, P]], channel_multiplier=1).then_inc(consts, 1)
                pool.affine_select(out=earlier[:, :, :], in_=earlier[:, :, :], compare_op=ALU.is_gt, fill=0.0,
                                   base=0, pattern=[[1, GROUPS], [-1, GROUPS]], channel_multiplier=0)\
                    .then_inc(consts, 1)
                for n in range(CHUNKS * EARLY):
                    pool.wait_ge(early_silu, n + 1)
                    pool.wait_ge(early_linear, n + 1)
                    pool.tensor_tensor(early_hid[n // CHUNKS][:, n % CHUNKS * N:(n % CHUNKS + 1) * N],
                                       early_a[n % 2][:, :], early_c[n % 2][:, :], ALU.mult).then_inc(early_ready, 1)

            @block.scalar
            def _(sc):
                sc.wait_ge(consts, 8)
                for tile, row, ap in ROWS:
                    sc.dma_start(tile[row:row + ap.shape[0], :], ap).then_inc(rows_in, 16)
                sc.wait_ge(dve, mark["var"])
                sc.activation(root[:, :], var[:, :], ACT.Sqrt).then_inc(root_ready, 1)
                for q in range(CHUNKS):
                    s, at = q // 2, slice(q % 2 * N, q % 2 * N + N)
                    sc.wait_ge(turned, 2 + q)
                    sc.activation(res[:, s, at], ps[1 + q][:, :], ACT.Copy).then_inc(state_ready, 1)
                    sc.activation(res_h[:, s, at], ps[1 + q][:, :], ACT.Copy).then_inc(state_ready, 1)
                sc.wait_ge(dve, mark["logits"])
                sc.activation(prob[:, :, :], lg[:, :, :], ACT.Exp).then_inc(exp_ready, 1)
                sc.wait_ge(dve, mark["columns"])
                for n in range(CHUNKS * EARLY):
                    u, k = n // CHUNKS, n % 2
                    biases = moe_b13[:, u if u < EARLY - 1 else PAIRS, :]
                    sc.wait_ge(early_up, n + 1)
                    at_least(sc, early_ready, n - 1)
                    sc.activation(early_a[k][:, :], ps[1 + 2 * k][:, :], ACT.Silu, bias=biases[:, 0:1])\
                        .then_inc(early_silu, 1)
                    sc.activation(early_c[k][:, :], ps[2 + 2 * k][:, :], ACT.Identity, bias=biases[:, 1:2])\
                        .then_inc(early_linear, 1)
                for q in range(CHUNKS):
                    sc.wait_ge(turned, 3 + CHUNKS + q)
                    sc.activation(cwT[:, q * N:(q + 1) * N], TURN_BANKS[q][0:EXPERTS, :], ACT.Copy)\
                        .then_inc(columns_ready, 1)

            @block.tensor
            def _(pe):
                pe.wait_ge(consts, 9)
                pe.wait_ge(rows_in, 16 * len(ROWS))
                pe.transpose(ps[0][:, 0:P], rows_qk[:, :], ident[:, :])
                pe.transpose(ps[0][:, P:2 * P], rows_v1[:, :], ident[:, :])
                pe.transpose(ps[0][:, 2 * P:3 * P], rows_misc[:, :], ident[:, :]).then_inc(turned, 1)
                for q in range(CHUNKS):
                    pe.wait_ge(dve, mark[f"normed{q}"])
                    for b in range(4):
                        ins = pe.transpose(ps[1 + q][:, b * P:(b + 1) * P], xc[:, 4 * q + b, :], ident[:, :])
                    ins.then_inc(turned, 1)
                pe.wait_ge(gate_in, 32)
                for b in range(TB):
                    if b % 4 == 0:
                        pe.wait_ge(state_ready, b // 2 + 1)
                    ins = pe.matmul(ps[5][:, b * EXPERTS:(b + 1) * EXPERTS],
                                    res[:, b // 8, (b % 8) * P:(b % 8 + 1) * P], gw[:, :], start=True, stop=True)
                ins.then_inc(turned, 1)
                pe.wait_ge(early_in, 32 * EARLY)
                pe.wait_ge(state_ready, 2 * CHUNKS)
                for n in range(CHUNKS * EARLY):
                    u, q, k = n // CHUNKS, n % CHUNKS, n % 2
                    at_least(pe, early_linear, n - 1)
                    for m in range(2):
                        ins = pe.matmul(ps[1 + 2 * k + m][:, :], early_w13[u][:, m, :],
                                        res[:, q // 2, q % 2 * N:q % 2 * N + N], start=True, stop=True)
                    ins.then_inc(early_up, 1)
                pe.wait_ge(dve, mark["weights"])
                for q in range(CHUNKS):
                    for b in range(4):
                        ins = pe.transpose(TURN_BANKS[q][0:EXPERTS, b * P:(b + 1) * P], cw[:, 4 * q + b, :],
                                           ident[:, :])
                    ins.then_inc(turned, 1)

        with ExitStack() as c:
            w2 = [sb(f"w2_{k}", [P, P], F32, c) for k in range(2)]
            share = [sb(f"share{k}", [P, T], F32, c) for k in range(2)]
            early_share = [sb(f"early_share{u}", [P, T], F32, c) for u in range(EARLY - 1)]
            act_a = [sb(f"act_a{k}", [P, N], F32, c) for k in range(2)]
            prod = [sb(f"prod{k}", [P, N], F32, c) for k in range(2)]
            w2_h, w2_l = ([sb(f"w2_{part}{k}", [P, P], F32R, c) for k in range(2)] for part in "hl")
            DEEP = 4
            hid = [sb(f"hid{k}", [P, N], F32, c) for k in range(DEEP)]
            hid_h, hid_l = ([sb(f"hid_{part}{k}", [P, N], F32R, c) for k in range(DEEP)] for part in "hl")
            y = [c.enter_context(nc.psum_tensor(f"y{q}", [P, N], F32)) for q in range(CHUNKS)]
            a_ps = [c.enter_context(nc.psum_tensor(f"a_ps{k}", [P, N], F32)) for k in range(2)]
            c_ps = [c.enter_context(nc.psum_tensor(f"c_ps{k}", [P, N], F32)) for k in range(2)]

            w2_in = [sem(f"w2_loaded{k}", c) for k in range(2)]
            early_w2_in = sem("early_w2_loaded", c)
            share_in = [sem(f"share_loaded{k}", c) for k in range(2)]
            early_share_in = sem("early_share_loaded", c)
            early_weighted = sem("early_hidden_weighted", c)
            up_ready = sem("a_and_c_ready", c)
            silu_ready = sem("silu_ready", c)
            prod_ready = sem("product_ready", c)
            hid_ready = sem("hidden_ready", c)
            hid_h_ready, hid_l_ready = sem("hidden_upper_ready", c), sem("hidden_split", c)
            w2_upper, w2_split = sem("w2_upper_ready", c), sem("w2_split", c)
            down_done = sem("hidden_used", c)
            y_ready = sem("y_ready", c)
            gate_ready = sem("gate_ready", c)

            block = c.enter_context(nc.Block())
            FIRST = EARLY - 1
            LOOPS = (PAIRS - FIRST) // 2

            def spread(queue, tile, pair, loaded):
                for e in range(2):
                    queue.dma_start(tile[e * INTER:(e + 1) * INTER, :],
                                 weights_by_pair[bass.ds(2 * pair + e, 1), :].broadcast_to([INTER, T]))\
                        .then_inc(loaded, 16)

            def down_weights(queue, tile, pair, loaded):
                queue.dma_start(tile[:, :], w2d[bass.ds(2 * pair, 2), :, :].rearrange("e k d -> (e k) d"))\
                    .then_inc(loaded, 16)

            @block.sync
            def _(sp):
                for k in range(2):
                    down_weights(sp, w2[k], FIRST + k, w2_in[k])
                sp.wait_ge(weights_stored, 16)
                for k in range(2):
                    spread(sp, share[k], FIRST + k, share_in[k])
                def replace(i):
                    for k in range(2):
                        sp.wait_ge(split_ready, 2 * i + k + 1)
                        load_w13(sp, 2 * i + 2 + k + FIRST, k)
                        sp.wait_ge(w2_split, 2 * i + k + 1)
                        down_weights(sp, w2[k], 2 * i + 2 + k + FIRST, w2_in[k])
                        sp.wait_ge(hid_ready, 8 * i + 4 + 4 * k)
                        spread(sp, share[k], 2 * i + 2 + k + FIRST, share_in[k])

                with sp.Fori(0, LOOPS - 1) as i:
                    replace(i)

            @block.tensor
            def _(pe):
                def up(k, q, turn, n):
                    if q == 0:
                        pe.wait_ge(split_ready, turn + 1)
                    at_least(pe, prod_ready, n - 1)
                    s, h = q // 2, slice(q % 2 * N, q % 2 * N + N)
                    for m, bank in enumerate((a_ps[q % 2], c_ps[q % 2])):
                        pe.matmul(bank[:, :], w13_h[k][:, m, :], res_h[:, s, h], start=True, stop=False)
                        pe.matmul(bank[:, :], w13_h[k][:, m, :], res_l[:, s, h], start=False, stop=False)
                        ins = pe.matmul(bank[:, :], w13_l[k][:, m, :], res_h[:, s, h], start=False, stop=True)
                    ins.then_inc(up_ready, 1)

                def down(k, q, n, turn):
                    if q == 0:
                        pe.wait_ge(w2_split, turn + 1)
                    pe.wait_ge(hid_l_ready, n + 1)
                    pe.matmul(y[q][:, :], w2_h[k][:, :], hid_h[q][:, :], start=False, stop=False)
                    pe.matmul(y[q][:, :], w2_l[k][:, :], hid_h[q][:, :], start=False, stop=False)
                    pe.matmul(y[q][:, :], w2_h[k][:, :], hid_l[q][:, :], start=False, stop=False)\
                        .then_inc(down_done, 1)

                def finish(q):
                    if q == 0:
                        pe.wait_ge(early_w2_in, 16 * EARLY)
                    at = slice(q * N, (q + 1) * N)
                    for u in range(EARLY):
                        if u < EARLY - 1:
                            pe.wait_ge(early_weighted, 2 * q + u + 1)
                        ins = pe.matmul(y[q][:, :], early_w2[u][:, :], early_hid[u][:, at], start=False,
                                        stop=(u == EARLY - 1))
                    ins.then_inc(y_ready, 1)

                pe.wait_ge(b2_in, 16)
                for q in range(CHUNKS):
                    pe.matmul(y[q][:, :], expert_b2[:, :], cwT[:, q * N:(q + 1) * N], start=True, stop=False)
                for q in range(3):
                    up(0, q, 0, q)
                with pe.Fori(0, LOOPS - 1) as i:
                    for m in range(8):
                        up((m + 3) // 4 % 2, (m + 3) % 4, 2 * i + (m + 3) // 4, 8 * i + m + 3)
                        down(m // 4, m % 4, 8 * i + m, 2 * i + m // 4)
                i = LOOPS - 1
                for m in range(8):
                    if m < 5:
                        up((m + 3) // 4, (m + 3) % 4, 2 * i + (m + 3) // 4, 8 * i + m + 3)
                    down(m // 4, m % 4, 8 * i + m, 2 * i + m // 4)
                    if m >= 4:
                        finish(m - 4)

            @block.scalar
            def _(sc):
                def silu(k, q, n, turn):
                    if q == 0:
                        sc.wait_ge(split_ready, turn + 1)
                    sc.wait_ge(up_ready, n + 1)
                    sc.activation(act_a[q % 2][:, :], a_ps[q % 2][:, :], ACT.Silu,
                                  bias=b13[k][:, 0:1]).then_inc(silu_ready, 1)

                def upper_part(q, n):
                    sc.wait_ge(hid_ready, n + 1)
                    sc.activation(hid_h[q][:, :], hid[q][:, :], ACT.Copy).then_inc(hid_h_ready, 1)

                for g in range(2):
                    load_qkv(sc, 0, g)
                load_w1(sc, 0)
                sc.wait_ge(weights_stored, 16)
                for u in range(EARLY - 1):
                    spread(sc, early_share[u], u, early_share_in)
                    down_weights(sc, early_w2[u], u, early_w2_in)
                sc.dma_start(early_w2[EARLY - 1][:, :], t["L0_ffn_sw2"]).then_inc(early_w2_in, 16)
                silu(0, 0, 0, 0)
                with sc.Fori(0, LOOPS - 1) as i:
                    for m in range(8):
                        silu((m + 1) // 4 % 2, (m + 1) % 4, 8 * i + m + 1, 2 * i + (m + 1) // 4)
                        upper_part(m % 4, 8 * i + m)
                for m in range(8):
                    i = LOOPS - 1
                    if m < 7:
                        silu((m + 1) // 4, (m + 1) % 4, 8 * i + m + 1, 2 * i + (m + 1) // 4)
                    upper_part(m % 4, 8 * i + m)
                for q in range(CHUNKS):
                    sc.wait_ge(y_ready, q + 1)
                    sc.activation(gate[:, q * N:(q + 1) * N], y[q][:, :], ACT.Silu, bias=moe_sb2[:, 0:1])\
                        .then_inc(gate_ready, 1)

            @block.gpsimd
            def _(pool):
                def lower_part(q, n):
                    pool.wait_ge(hid_h_ready, n + 1)
                    pool.tensor_tensor(hid_l[q][:, :], hid[q][:, :], hid_h[q][:, :].bitcast(F32), ALU.subtract)\
                        .then_inc(hid_l_ready, 1)

                with pool.Fori(0, LOOPS) as i:
                    for m in range(8):
                        lower_part(m % 4, 8 * i + m)

            @block.vector
            def _(v):
                def product(q, n, k, loads):
                    v.wait_ge(silu_ready, n + 1)
                    v.scalar_tensor_tensor(out=prod[q % 2][:, :], in0=c_ps[q % 2][:, :], scalar=b13[k][:, 1:2],
                                           in1=act_a[q % 2][:, :], op0=ALU.add, op1=ALU.mult)\
                        .then_inc(prod_ready, 1)
                    v.wait_ge(prod_ready, n + 1)
                    if q == 0:
                        v.wait_ge(share_in[k], 32 * loads)
                    at_least(v, down_done, n - 3)
                    v.tensor_tensor(hid[q][:, :], prod[q % 2][:, :], share[k][:, q * N:(q + 1) * N], ALU.mult)\
                        .then_inc(hid_ready, 1)

                def split_w2(k, turn, loads):
                    v.wait_ge(w2_in[k], 16 * loads)
                    at_least(v, down_done, 4 * (turn - 1))
                    v.tensor_copy(w2_h[k][:, :], w2[k][:, :]).then_inc(w2_upper, 1)
                    v.wait_ge(w2_upper, turn + 1)
                    v.tensor_tensor(w2_l[k][:, :], w2[k][:, :], w2_h[k][:, :].bitcast(F32), ALU.subtract)\
                        .then_inc(w2_split, 1)

                def body(i, last=False):
                    for m in range(8):
                        if m == 0:
                            at_least(v, up_ready, 8 * i)
                            split_w13(v, 1, 2 * i + 1, 2 * i + 1 + FIRST, i + 1)
                        product(m % 4, 8 * i + m, m // 4, i + 1)
                        if m == 4:
                            split_w2(1, 2 * i + 1, i + 1)
                        if m == 7 and not last:
                            split_w2(0, 2 * i + 2, i + 2)
                        if last:
                            if m == 0:
                                v.wait_ge(early_share_in, 32 * (EARLY - 1))
                            u, at = m % 2, slice(m // 2 * N, (m // 2 + 1) * N)
                            v.tensor_tensor(early_hid[u][:, at], early_hid[u][:, at], early_share[u][:, at], ALU.mult)\
                                .then_inc(early_weighted, 1)
                        if m == 5 and not last:
                            v.wait_ge(up_ready, 8 * i + 4)
                            split_w13(v, 0, 2 * i + 2, 2 * i + 2 + FIRST, i + 2)

                split_w2(0, 0, 1)
                body(0)
                with v.Fori(1, LOOPS - 1) as i:
                    body(i)
                body(LOOPS - 1, last=True)
                for g in range(2):
                    for m in range(3):
                        split_qkv(v, g, m, 0)
                split_w1(v, 0)

        routing.close()

        with ExitStack() as c:
            wo = [sb(f"wo{g}", [P, 4, P], F32, c) for g in range(2)]
            wg_h, wg_l = ([sb(f"wo_scaled_{k}{s}", [P, CB, P], F32R, c) for s in range(SEQS)] for k in "hl")
            wg_sum = [sb(f"wo_scaled_sum{s}", [P, P], F32, c) for s in range(SEQS)]
            w2 = sb("ff2", [P, FB, P], F32, c)
            par_f = [sb(f"par_f{s}", [P, 4, CB], F32, c) for s in range(SEQS)]
            par_g = [sb(f"par_g{s}", [P, NG], F32, c) for s in range(SEQS)]
            exp_k = [sb(f"exp_k{k}", [P, S], F32, c) for k in range(2)]
            relu_k = sb("relu_k", [P, S], F32, c)
            exp_q, line_q, phi_q = ([sb(f"{n}{k}", [P, S], F32, c) for k in range(2)]
                                    for n in ("exp_q", "line_q", "phi_q"))
            ln_q = sb("ln_q", [P, S], F32, c)
            miss = [sb(f"miss{k}", [P, S], F32, c) for k in range(2)]
            miss_h, miss_l = ([sb(f"miss_{part}{k}", [P, S], F32R, c) for k in range(2)] for part in "hl")
            sum_k = [sb(f"sum_k{k}", [P, 1], F32, c) for k in range(2)]
            sum_kv = [sb(f"sum_kv{k}", [P, 1], F32, c) for k in range(2)]
            scale = [sb(f"scale{k}", [P, 1], F32, c) for k in range(2)]
            inv = [sb(f"inv{k}", [P, 1], F32, c) for k in range(2)]
            mean_v = [sb(f"mean_v{k}", [P, 1], F32, c) for k in range(2)]
            bias_y = sb("bias_y", [P, 1], F32, c)
            norm_buf = sb("norm_buf", [P, S], F32, c)
            mid = sb("mid", [P, S], F32, c)
            mid_h, mid_l = (sb(f"mid_{k}", [P, S], F32R, c) for k in "hl")
            hid = sb("hidden", [P, FB, S], F32, c)

            tiles = [c.enter_context(nc.psum_tensor(f"tile{k}", [P, S], F32)) for k in range(3)]
            yp = c.enter_context(nc.psum_tensor("yp", [P, S], F32))

            wo_in = [sem(f"wo_loaded{g}", c) for g in range(2)]
            w2_in = sem("ff2_loaded", c)
            first_gated = sem("first_sequence_gated", c)
            wg_sum_ready = sem("wo_scaled_sum_ready", c)
            miss_h_ready, miss_l_ready = sem("miss_upper_ready", c), sem("miss_split", c)
            wg_h_ready = sem("wo_scaled_upper_ready", c)
            mid_h_ready, mid_l_ready = sem("mid_upper_ready", c), sem("mid_split", c)
            q_ready, k_ready, v_ready = (sem(f"{n}_projected", c) for n in "qkv")
            wo_done = sem("wo_done", c)
            exp_q_done, exp_k_done, relu_done = (sem(n, c) for n in ("exp_q_done", "exp_k_done", "relu_k_done"))
            ln_done, miss_ready = sem("ln_done", c), sem("miss_ready", c)
            line_done, curve_done = sem("line_q_done", c), sem("curve_q_done", c)
            phi_q_ready, phi_k_ready = sem("phi_q_ready", c), sem("phi_k_ready", c)
            kv_done = sem("kv_done", c)
            scale_ready, guarded, inv_ready = sem("scale_ready", c), sem("sum_guarded", c), sem("inverse_ready", c)
            mean_v_ready, wg_ready = sem("mean_v_ready", c), sem("wo_scaled_ready", c)
            par_f_ready, par_g_ready = sem("par_f_ready", c), sem("par_g_ready", c)
            const_ready, bias_ready = sem("constant_ready", c), sem("bias_ready", c)
            gelu_y = sem("gelu_y_ready", c)
            sum1_ready, centred1, squared1, var1_ready, ln_var1, rstd1_ready, normed1 = (sem(f"norm1_{n}", c) for n in (
                "sum_ready", "centred", "squared", "variance_ready", "ln_variance", "rstd_ready", "normed"))
            sum2_ready, centred2, squared2, var2_ready, ln_var2, rstd2_ready, normed2 = (sem(f"norm2_{n}", c) for n in (
                "sum_ready", "centred", "squared", "variance_ready", "ln_variance", "rstd_ready", "normed"))
            mid_ready = sem("mid_ready", c)
            state_ready = sem("state_ready", c)
            state_h, state_l = sem("state_upper_ready", c), sem("state_split", c)
            up_ready, hid_ready = ([sem(f"{n}_{h}", c) for h in "ab"] for n in ("ff_up_ready", "ff_hidden_ready"))
            down_ready, gelu_down = sem("ff_down_ready", c), sem("gelu_down_ready", c)

            block = c.enter_context(nc.Block())
            LOOPS = LAYERS - 1
            BO, B2, S1, _, S2, _, FF1 = range(7)

            PE_ORDER = """
                q:0 k:0 v:7- out:4- k:1 v:0 q:1 out:5- k:2 q:2 out:6- const out:7- q:3 v:1 k:3 centre1_a
                centre1_b v:2 var1_a var1_b k:4 q:4 out:0 v:3 up:0_a up:0_b up:1_a up:1_b up:2_a up:3_a
                up:2_b up:3_b down_a q:5 k:5 down_rest_a down_b q:6 v:4 down_rest_b out:1 centre2_a v:5
                centre2_b var2_a var2_b k:6 out:2 k:7 v:6 q:7 out:3
            """.split()
            ACT_ORDER = """
                exp_q:0 log:6- exp_k:0 miss:6- relu_k:0 log:7- exp_k:1 miss:7- relu_k:1 exp_q:1 log:0
                exp_k:2 exp_q:2 relu_k:2 miss:0 gelu_y_a gelu_y_b exp_q:3 exp_k:3 square1_a relu_k:3
                square1_b log:1 ln_var1_a rstd1_a ln_var1_b rstd1_b exp_k:4 relu_k:4 miss:1 exp_q:4
                hidden:0_a hidden:0_b hidden:1_a hidden:1_b hidden:2_a hidden:3_a hidden:2_b hidden:3_b
                log:2 exp_q:5 exp_k:5 miss:2 relu_k:5 log:3 exp_q:6 gelu_down_a gelu_down_b miss:3 square2_a
                log:4 square2_b ln_var2_a rstd2_a ln_var2_b rstd2_b exp_k:6 relu_k:6 miss:4 exp_k:7 log:5
                relu_k:7 exp_q:7 miss:5
            """.split()
            DVE_ORDER = """
                inverse:6- line_q:0 scale:7- mean_v:6- curve_q:0 kv:7- inverse:7- phi_k:0 miss_upper:6-
                scale_wo:6- mean_v:7- scale:0 scale_wo:7- kv:0 miss_upper:7- phi_k:1 line_q:1 split_even:0
                curve_q:1 bias_y line_q:2 curve_q:2 inverse:0 phi_k:2 residual1_a kv:1 residual1_b line_q:3
                scale:1 miss_upper:0 split_even:1 mean_v:0 inverse:1 kv:2 phi_k:3 norm1_a scale_wo:0 mid_a
                mid_upper_a norm1_b mean_v:1 mid_b mid_upper_b scale:2 scale:3 kv:3 line_q:4 inverse:2
                curve_q:3 curve_q:4 split_odd:0 phi_k:4 inverse:3 mean_v:2 miss_upper:1 scale_wo:1 columns
                split_up mean_v:3 split_odd:1 split_odd:2 scale:4 scale_wo:2 line_q:5 scale_wo:3
                split_even:2 curve_q:5 phi_k:5 miss_upper:2 inverse:4 scale:5 curve_q:6 kv:4 residual2_a
                residual2_b inverse:5 mean_v:4 line_q:6 miss_upper:3 kv:5 mean_v:5 scale_wo:4 scale_wo:5
                norm2_a state_a norm2_b state_upper_a state_b state_lower_a state_upper_b phi_k:6
                state_lower_b miss_upper:4 kv:6 scale:6 phi_k:7 curve_q:7 line_q:7 miss_upper:5
            """.split()
            POOL_ORDER = """
                phi_q:7- miss_lower:5- phi_q:0 miss_lower:6- miss_lower:7- phi_q:1 miss_lower:0 phi_q:2
                mid_lower_a mid_lower_b phi_q:3 miss_lower:1 phi_q:4 miss_lower:2 phi_q:5 phi_q:6
                miss_lower:3 miss_lower:4
            """.split()
            TILE_STEPS = [
                "q:0 k:1 k:2 v:2 q:3 v:3 k:4 v:5 k:6 v:6 up:1 down".split(),
                "k:0 v:0 q:2 k:3 q:4 q:5 q:6 k:7 var1 var2 up:2".split(),
                "q:1 v:1 v:4 k:5 q:7 v:7 const centre1 centre2 up:0 up:3".split(),
            ]
            ATTENTION = ("q", "k", "v", "out", "exp_q", "exp_k", "relu_k", "log", "miss", "line_q", "curve_q",
                         "phi_k", "scale", "kv", "inverse", "mean_v", "scale_wo", "phi_q", "miss_upper", "miss_lower")
            GELUS = ("gelu_y", "hidden", "gelu_down")
            EITHER_TABLE = ("relu_k", "square1", "square2")

            def parse(step):
                late = step.endswith("-")
                name = step.rstrip("-")
                half = None
                if name[-2:] in ("_a", "_b"):
                    name, half = name[:-2], "ab".index(name[-1])
                kind, _, block_ = name.partition(":")
                return kind, int(block_) if block_ else None, half, late

            HALF = [slice(0, N), slice(N, 2 * N)]

            def attention_of(n, s, layer, late):
                if not late:
                    return n, s, layer + (1 - s)
                return n - 1, 1 - s, layer

            def absent(kind, late, n):
                if not isinstance(n, int):
                    return False
                if kind in ATTENTION:
                    return not 0 <= n - late < STAGES
                if kind == "split_odd":
                    return not (n % 2 == 1 and n < STAGES - 1)
                if kind == "split_even":
                    return not (n % 2 == 0 and 0 < n < STAGES - 1)
                if kind == "split_up":
                    return not (n % 2 == 0 and 0 < n < STAGES - 1)
                if kind == "columns":
                    return n >= STAGES - 1
                return n == 0

            FILLS = []
            for step in PE_ORDER:
                kind, b, half, late = parse(step)
                if kind not in ("out", "down_rest") and (kind, b, late) not in FILLS:
                    FILLS.append((kind, b, late))
            tile_of = {parse(step)[:2]: tiles[k] for k in range(3) for step in TILE_STEPS[k]}

            def last_read(kind, b, n):
                if kind in ("q", "k", "v"):
                    return {"q": line_done, "k": relu_done, "v": kv_done}[kind], 8 * n + b + 1
                if kind == "up":
                    return hid_ready[1], FB * (n - 1) + b + 1
                if kind == "const":
                    return bias_ready, n
                return {"centre1": normed1, "centre2": normed2, "var1": ln_var1, "var2": ln_var2,
                        "down": gelu_down}[kind], 2 * n

            def tile_free(pe, kind, b, late, n):
                at, m = FILLS.index((kind, b, late)), n
                while True:
                    at -= 1
                    if at < 0:
                        if isinstance(m, int) and m == 0:
                            return
                        at, m = at + len(FILLS), m - 1
                    k, b2, l2 = FILLS[at]
                    if tile_of[(k, b2)] is not tile_of[(kind, b)] or absent(k, l2, m):
                        continue
                    semaphore, value = last_read(k, b2, m - l2 if k in ATTENTION else m)
                    pe.wait_ge(semaphore, value)
                    return

            @block.sync
            def _(sp):
                wod = t["L0_attn_Wo"]

                def output(layer, g):
                    rows = wod[bass.ds(layer, 1), g * 4 * P:(g + 1) * 4 * P, :]
                    sp.dma_start(wo[g][:, :, :], rows.rearrange("l (c p) d -> p (l c) d", p=P)).then_inc(wo_in[g], 16)

                def down_weights(layer):
                    sp.dma_start(w2[:, :, :], t["L0_attn_W2"][bass.ds(layer, 1), :, :]
                                 .rearrange("l (c p) d -> p (l c) d", p=P)).then_inc(w2_in, 16)

                for g in range(2):
                    output(0, g)
                down_weights(0)
                with sp.Fori(0, LOOPS) as i:
                    for g in range(2):
                        sp.wait_ge(qkv_split[g], 3 * (i + 1))
                        load_qkv(sp, i + 1, g)
                    for g in range(2):
                        sp.wait_ge(wg_ready, 16 * i + 12 + 4 * g)
                        output(i + 1, g)
                    sp.wait_ge(w1_split, i + 1)
                    load_w1(sp, i + 1)
                    sp.wait_ge(down_ready, 2 * (2 * i + 2))
                    down_weights(i + 1)

            @block.tensor
            def _(pe):
                def project(n, s, layer, j, m, o, ready):
                    g, cols = j // 4, slice(j % 4 * P, j % 4 * P + P)
                    if j % 4 == 0 and s == 0:
                        pe.wait_ge(qkv_split[g], 3 * layer + m + 1)
                    if j == 0:
                        at_least(pe, state_l, 2 * (n - 1))
                    h, l = qkv_h[g][:, m, cols], qkv_l[g][:, m, cols]
                    for at in HALF:
                        pe.matmul(o[:, at], h, res_h[:, s, at], start=True, stop=False)
                        pe.matmul(o[:, at], h, res_l[:, s, at], start=False, stop=False)
                        ins = pe.matmul(o[:, at], l, res_h[:, s, at], start=False, stop=True)
                    ins.then_inc(ready, 1)

                def output(n, s, j):
                    u = 8 * n + j
                    if j == 0:
                        at_least(pe, gelu_y, 2 * n)
                    pe.wait_ge(wg_ready, u + 1)
                    pe.wait_ge(miss_l_ready, u + 1)
                    h, l, mh, ml = wg_h[s][:, j, :], wg_l[s][:, j, :], miss_h[j % 2], miss_l[j % 2]
                    for at in HALF:
                        pe.matmul(yp[:, at], h, mh[:, at], start=(j == 0), stop=False)
                        pe.matmul(yp[:, at], l, mh[:, at], start=False, stop=False)
                        ins = pe.matmul(yp[:, at], h, ml[:, at], start=False, stop=(j == CB - 1))
                    ins.then_inc(wo_done, 1)

                def constant(n, p, o):
                    pe.wait_ge(wg_sum_ready, 8 * n)
                    pe.matmul(o[:, 0:1], wg_sum[p][:, :], ones[:, 0:1], start=True, stop=True).then_inc(const_ready, 1)

                def stage(n, s, layer=0):
                    p = 1 - s
                    for step in PE_ORDER:
                        kind, b, h, late = parse(step)
                        if absent(kind, late, n):
                            continue
                        m, seq, its_layer = attention_of(n, s, layer, late)
                        if kind not in ("out", "down_rest"):
                            if h in (None, 0):
                                tile_free(pe, kind, b, late, n)
                            o = tile_of[(kind, b)]
                        at = HALF[h or 0]
                        half_done = 2 * (n - 1) + (h or 0) + 1
                        if kind == "q":
                            project(m, seq, its_layer, b, 0, o, q_ready)
                        elif kind == "k":
                            project(m, seq, its_layer, b, 1, o, k_ready)
                        elif kind == "v":
                            project(m, seq, its_layer, b, 2, o, v_ready)
                        elif kind == "out":
                            output(m, seq, b)
                        elif kind == "const":
                            constant(n, p, o)
                        elif kind == "centre1":
                            pe.wait_ge(sum1_ready, half_done)
                            pe.matmul(o[:, at], centre[:, :], norm_buf[:, at], start=True, stop=True)\
                                .then_inc(centred1, 1)
                        elif kind == "centre2":
                            pe.wait_ge(sum2_ready, half_done)
                            pe.matmul(o[:, at], centre[:, :], norm_buf[:, at], start=True, stop=True)\
                                .then_inc(centred2, 1)
                        elif kind == "var1":
                            pe.wait_ge(squared1, half_done)
                            pe.matmul(o[:, at], average[:, :], norm_buf[:, at], start=True, stop=True)\
                                .then_inc(var1_ready, 1)
                        elif kind == "var2":
                            pe.wait_ge(squared2, half_done)
                            pe.matmul(o[:, at], average[:, :], norm_buf[:, at], start=True, stop=True)\
                                .then_inc(var2_ready, 1)
                        elif kind == "up":
                            if b == 0 and h == 0:
                                pe.wait_ge(w1_split, layer + 1)
                            if b == 0:
                                pe.wait_ge(mid_l_ready, half_done)
                            cols = slice(b * P, (b + 1) * P)
                            pe.matmul(o[:, at], w1_h[:, cols], mid_h[:, at], start=True, stop=False)
                            pe.matmul(o[:, at], w1_l[:, cols], mid_h[:, at], start=False, stop=False)
                            pe.matmul(o[:, at], w1_h[:, cols], mid_l[:, at], start=False, stop=True)\
                                .then_inc(up_ready[h], 1)
                        elif kind == "down":
                            if h == 0:
                                pe.wait_ge(w2_in, 16 * (layer + 1))
                            for f in range(FB // 2):
                                pe.wait_ge(hid_ready[h], FB * (n - 1) + f + 1)
                                pe.matmul(o[:, at], w2[:, f, :], hid[:, f, at], start=(f == 0), stop=False)
                        elif kind == "down_rest":
                            o = tile_of[("down", None)]
                            for f in range(FB // 2, FB):
                                pe.wait_ge(hid_ready[h], FB * (n - 1) + f + 1)
                                ins = pe.matmul(o[:, at], w2[:, f, :], hid[:, f, at], start=False, stop=(f == FB - 1))
                            ins.then_inc(down_ready, 1)

                stage(0, 0, -1)
                stage(1, 1, 0)
                stage(2, 0, 0)
                with pe.Fori(1, LOOPS) as i:
                    stage(2 * i + 1, 1, i)
                    stage(2 * i + 2, 0, i)
                stage(STAGES - 1, 1, LAYERS - 1)
                stage(STAGES, 0, LAYERS - 1)

            @block.scalar
            def _(sc):
                def exp_of_q(n, s, j):
                    u = 8 * n + j
                    if j == 0:
                        sc.wait_ge(par_f_ready, n + 1)
                    sc.wait_ge(q_ready, u + 1)
                    at_least(sc, phi_q_ready, u - 1)
                    sc.activation(exp_q[j % 2][:, :], tile_of[("q", j)][:, :], ACT.Exp, bias=par_f[s][:, 0, j:j + 1])\
                        .then_inc(exp_q_done, 1)

                def exp_of_k(n, s, j):
                    u = 8 * n + j
                    if j == 0:
                        sc.wait_ge(par_f_ready, n + 1)
                    sc.wait_ge(k_ready, u + 1)
                    at_least(sc, kv_done, u - 1)
                    sc.activation(exp_k[j % 2][:, :], tile_of[("k", j)][:, :], ACT.Exp, bias=par_f[s][:, 1, j:j + 1])\
                        .then_inc(exp_k_done, 1)

                def relu_of_k(n, s, j):
                    sc.wait_ge(k_ready, 8 * n + j + 1)
                    at_least(sc, phi_k_ready, 8 * n + j)
                    sc.activation(relu_k[:, :], tile_of[("k", j)][:, :], ACT.Relu, bias=par_f[s][:, 1, j:j + 1])\
                        .then_inc(relu_done, 1)

                def logarithm(n, j):
                    u = 8 * n + j
                    sc.wait_ge(scale_ready, u + 1)
                    sc.wait_ge(phi_q_ready, u + 1)
                    at_least(sc, miss_ready, u)
                    sc.activation(ln_q[:, :], phi_q[j % 2][:, :], ACT.Ln, scale=scale[j % 2][:, 0:1], bias=1.0)\
                        .then_inc(ln_done, 1)

                def negated(n, j):
                    u = 8 * n + j
                    sc.wait_ge(ln_done, u + 1)
                    at_least(sc, miss_l_ready, u - 1)
                    sc.activation(miss[j % 2][:, :], ln_q[:, :], ACT.Exp, scale=-1.0).then_inc(miss_ready, 1)

                def stage(n, s, layer=0):
                    p = 1 - s
                    for k, step in enumerate(ACT_ORDER):
                        kind, b, h, late = parse(step)
                        if absent(kind, late, n):
                            continue
                        m, seq, _ = attention_of(n, s, layer, late)
                        at = HALF[h or 0]
                        half_done = 2 * (n - 1) + (h or 0) + 1
                        if kind == "exp_q":
                            exp_of_q(m, seq, b)
                        elif kind == "exp_k":
                            exp_of_k(m, seq, b)
                        elif kind == "relu_k":
                            relu_of_k(m, seq, b)
                        elif kind == "log":
                            logarithm(m, b)
                        elif kind == "miss":
                            negated(m, b)
                        elif kind == "gelu_y":
                            if h == 0:
                                sc.wait_ge(bias_ready, n)
                                sc.wait_ge(wo_done, 8 * n)
                            sc.activation(norm_buf[:, at], yp[:, at], ACT.Gelu_apprx_tanh, bias=bias_y[:, 0:1],
                                          scale=-1.0).then_inc(gelu_y, 1)
                        elif kind == "hidden":
                            sc.wait_ge(up_ready[h], FB * (n - 1) + b + 1)
                            sc.activation(hid[:, b, at], tile_of[("up", b)][:, at], ACT.Gelu_apprx_tanh,
                                          bias=par_g[p][:, FF1 + b:FF1 + b + 1]).then_inc(hid_ready[h], 1)
                        elif kind == "gelu_down":
                            sc.wait_ge(down_ready, half_done)
                            sc.activation(norm_buf[:, at], tile_of[("down", None)][:, at], ACT.Gelu_apprx_tanh,
                                          bias=par_g[p][:, B2:B2 + 1]).then_inc(gelu_down, 1)
                        elif kind == "square1":
                            sc.wait_ge(centred1, half_done)
                            sc.activation(norm_buf[:, at], tile_of[("centre1", None)][:, at], ACT.Square)\
                                .then_inc(squared1, 1)
                        elif kind == "square2":
                            sc.wait_ge(centred2, half_done)
                            sc.activation(norm_buf[:, at], tile_of[("centre2", None)][:, at], ACT.Square)\
                                .then_inc(squared2, 1)
                        elif kind == "ln_var1":
                            sc.wait_ge(var1_ready, half_done)
                            sc.activation(norm_buf[:, at], tile_of[("var1", None)][:, at], ACT.Ln, bias=ln_eps[:, 0:1])\
                                .then_inc(ln_var1, 1)
                        elif kind == "ln_var2":
                            sc.wait_ge(var2_ready, half_done)
                            sc.activation(norm_buf[:, at], tile_of[("var2", None)][:, at], ACT.Ln, bias=ln_eps[:, 0:1])\
                                .then_inc(ln_var2, 1)
                        elif kind == "rstd1":
                            sc.wait_ge(ln_var1, half_done)
                            sc.activation(norm_buf[:, at], norm_buf[:, at], ACT.Exp, scale=-0.5)\
                                .then_inc(rstd1_ready, 1)
                        elif kind == "rstd2":
                            sc.wait_ge(ln_var2, half_done)
                            sc.activation(norm_buf[:, at], norm_buf[:, at], ACT.Exp, scale=-0.5)\
                                .then_inc(rstd2_ready, 1)
                        if kind in GELUS:
                            others = [parse(later)[0] for later in ACT_ORDER[k + 1:]]
                            if next((o for o in others if o not in EITHER_TABLE), None) not in GELUS:
                                sc.preload_act_table_set(EXP_LN)

                sc.preload_act_table_set(EXP_LN)
                stage(0, 0)
                stage(1, 1)
                stage(2, 0)
                with sc.Fori(1, LOOPS) as i:
                    stage(2 * i + 1, 1)
                    stage(2 * i + 2, 0)
                stage(STAGES - 1, 1)
                stage(STAGES, 0)

            @block.gpsimd
            def _(pool):
                def feature_map_q(n, j):
                    u = 8 * n + j
                    pool.wait_ge(curve_done, u + 1)
                    pool.wait_ge(line_done, u + 1)
                    at_least(pool, ln_done, u - 1)
                    k = j % 2
                    pool.tensor_tensor(phi_q[k][:, :], exp_q[k][:, :], line_q[k][:, :], ALU.add)\
                        .then_inc(phi_q_ready, 1)

                def lower_part_of_miss(n, j):
                    k = j % 2
                    pool.wait_ge(miss_h_ready, 8 * n + j + 1)
                    pool.tensor_tensor(miss_l[k][:, :], miss[k][:, :], miss_h[k][:, :].bitcast(F32), ALU.subtract)\
                        .then_inc(miss_l_ready, 1)

                def stage(n):
                    for step in POOL_ORDER:
                        kind, j, h, late = parse(step)
                        if absent(kind, late, n):
                            continue
                        at = HALF[h or 0]
                        if kind == "phi_q":
                            feature_map_q(n - late, j)
                        elif kind == "miss_lower":
                            lower_part_of_miss(n - late, j)
                        elif kind == "mid_lower":
                            pool.wait_ge(mid_h_ready, 2 * (n - 1) + h + 1)
                            pool.tensor_tensor(mid_l[:, at], mid[:, at], mid_h[:, at].bitcast(F32), ALU.subtract)\
                                .then_inc(mid_l_ready, 1)

                for n in range(3):
                    stage(n)
                with pool.Fori(1, LOOPS) as i:
                    stage(2 * i + 1)
                    stage(2 * i + 2)
                stage(STAGES - 1)
                stage(STAGES)

            @block.vector
            def _(v):
                def line_of_q(n, s, j):
                    v.wait_ge(exp_q_done, 8 * n + j + 1)
                    at_least(v, phi_q_ready, 8 * n + j - 1)
                    v.tensor_scalar(line_q[j % 2][:, :], tile_of[("q", j)][:, :], par_f[s][:, 3, j:j + 1], 1.0, ALU.add,
                                    ALU.max).then_inc(line_done, 1)

                def curve_of_q(n, j):
                    v.wait_ge(exp_q_done, 8 * n + j + 1)
                    k = j % 2
                    v.tensor_scalar(exp_q[k][:, :], exp_q[k][:, :], 1.0, -1.0, ALU.min, ALU.add).then_inc(curve_done, 1)

                def feature_map_k(n, j):
                    u, k = 8 * n + j, j % 2
                    v.wait_ge(relu_done, u + 1)
                    v.wait_ge(exp_k_done, u + 1)
                    at_least(v, scale_ready, u - 1)
                    at_least(v, guarded, u - 1)
                    v.scalar_tensor_tensor(out=exp_k[k][:, :], in0=exp_k[k][:, :], scalar=1.0, in1=relu_k[:, :],
                                           op0=ALU.min, op1=ALU.add, accum_out=sum_k[k][:, 0:1])\
                        .then_inc(phi_k_ready, 1)

                def scales(n, j):
                    u, k = 8 * n + j, j % 2
                    v.wait_ge(phi_k_ready, u + 1)
                    at_least(v, ln_done, u - 1)
                    v.tensor_scalar(scale[k][:, :], sum_k[k][:, :], 1.0 / Z_EPS, None, ALU.mult)\
                        .then_inc(scale_ready, 1)
                    at_least(v, mean_v_ready, u - 1)
                    v.tensor_scalar(inv[k][:, :], sum_k[k][:, :], TINY, None, ALU.max).then_inc(guarded, 1)

                def sum_of_kv(n, j):
                    u, k = 8 * n + j, j % 2
                    v.wait_ge(v_ready, u + 1)
                    v.wait_ge(phi_k_ready, u + 1)
                    at_least(v, mean_v_ready, u - 1)
                    v.tensor_tensor_reduce(exp_k[k][:, :], exp_k[k][:, :], tile_of[("v", j)][:, :], 1.0, 0.0,
                                           ALU.mult, ALU.add, sum_kv[k][:, 0:1]).then_inc(kv_done, 1)

                def inverse(n, j):
                    v.wait_ge(guarded, 8 * n + j + 1)
                    v.reciprocal(inv[j % 2][:, :], inv[j % 2][:, :]).then_inc(inv_ready, 1)

                def mean_of_v(n, s, j):
                    u, k = 8 * n + j, j % 2
                    v.wait_ge(inv_ready, u + 1)
                    v.wait_ge(kv_done, u + 1)
                    at_least(v, wg_ready, u - 1)
                    v.scalar_tensor_tensor(out=mean_v[k][:, :], in0=sum_kv[k][:, :], scalar=inv[k][:, 0:1],
                                           in1=par_f[s][:, 2, j:j + 1], op0=ALU.mult, op1=ALU.add)\
                        .then_inc(mean_v_ready, 1)

                def scale_output(n, s, layer, j):
                    if s == 0 and j % 4 == 0:
                        v.wait_ge(wo_in[j // 4], 16 * (layer + 1))
                    v.wait_ge(mean_v_ready, 8 * n + j + 1)
                    matrix, mean = wo[j // 4][:, j % 4, :], mean_v[j % 2][:, 0:1]
                    v.tensor_scalar(wg_h[s][:, j, :], matrix, mean, None, ALU.mult).then_inc(wg_h_ready, 1)
                    if j == 0:
                        v.tensor_scalar(wg_sum[s][:, :], matrix, mean, None, ALU.mult).then_inc(wg_sum_ready, 1)
                    else:
                        v.wait_ge(wg_sum_ready, 8 * n + j)
                        v.scalar_tensor_tensor(out=wg_sum[s][:, :], in0=matrix, scalar=mean, in1=wg_sum[s][:, :],
                                               op0=ALU.mult, op1=ALU.add).then_inc(wg_sum_ready, 1)
                    v.wait_ge(wg_h_ready, 8 * n + j + 1)
                    v.scalar_tensor_tensor(out=wg_l[s][:, j, :], in0=matrix, scalar=mean,
                                           in1=wg_h[s][:, j, :].bitcast(F32), op0=ALU.mult, op1=ALU.subtract)\
                        .then_inc(wg_ready, 1)

                def upper_part_of_miss(n, j):
                    u, k = 8 * n + j, j % 2
                    v.wait_ge(miss_ready, u + 1)
                    at_least(v, wo_done, u - 1)
                    v.tensor_copy(miss_h[k][:, :], miss[k][:, :]).then_inc(miss_h_ready, 1)

                def stage(n, s, layer=0, following=None):
                    p = 1 - s
                    if not absent("gelu_y", False, n):
                        v.tensor_copy(par_g[p][:, :], table_g[:, bass.ds(layer, 1), :]
                                      .rearrange("p l k -> p (l k)")).then_inc(par_g_ready, 1)
                    for step in DVE_ORDER:
                        kind, b, h, late = parse(step)
                        if absent(kind, late, n):
                            continue
                        m, seq, its_layer = attention_of(n, s, layer, late)
                        at = HALF[h or 0]
                        half_done = 2 * (n - 1) + (h or 0) + 1
                        if kind == "line_q":
                            line_of_q(m, seq, b)
                        elif kind == "curve_q":
                            curve_of_q(m, b)
                        elif kind == "phi_k":
                            feature_map_k(m, b)
                        elif kind == "scale":
                            scales(m, b)
                        elif kind == "kv":
                            sum_of_kv(m, b)
                        elif kind == "inverse":
                            inverse(m, b)
                        elif kind == "mean_v":
                            mean_of_v(m, seq, b)
                        elif kind == "scale_wo":
                            scale_output(m, seq, its_layer, b)
                        elif kind == "miss_upper":
                            upper_part_of_miss(m, b)
                        elif kind == "mid_upper":
                            v.wait_ge(mid_ready, half_done)
                            v.tensor_copy(mid_h[:, at], mid[:, at]).then_inc(mid_h_ready, 1)
                        elif kind == "split_up":
                            if s == 0:
                                v.wait_ge(up_ready[0], FB * n)
                                v.wait_ge(up_ready[1], FB * n)
                                split_w1(v, following)
                        elif kind == "columns":
                            v.tensor_copy(par_f[p][:, :, :], table_f[:, bass.ds(following, 1), :, :]
                                          .rearrange("p l k c -> p (l k) c")).then_inc(par_f_ready, 1)
                        elif kind == "split_odd":
                            if s == 1:
                                v.wait_ge((q_ready, k_ready, v_ready)[b], 8 * n + 4)
                                split_qkv(v, 0, b, following)
                        elif kind == "split_even":
                            if s == 0:
                                at_least(v, (q_ready, k_ready, v_ready)[b], 8 * n)
                                split_qkv(v, 1, b, following)
                        elif kind == "bias_y":
                            v.wait_ge(const_ready, n)
                            v.wait_ge(par_g_ready, n)
                            v.tensor_scalar(bias_y[:, :], tile_of[("const", None)][:, 0:1], par_g[p][:, BO:BO + 1],
                                            None, ALU.add).then_inc(bias_ready, 1)
                            if isinstance(n, int) and n == STAGES:
                                v.wait_ge(state_ready, 2 * (STAGES - 1))
                                v.tensor_tensor(res[:, 0, :], res[:, 0, :], gate[:, 0:S], ALU.mult)\
                                    .then_inc(first_gated, 1)
                        elif kind == "residual1":
                            v.wait_ge(gelu_y, half_done)
                            v.tensor_tensor(norm_buf[:, at], norm_buf[:, at], res[:, p, at], ALU.add).then_inc(sum1_ready, 1)
                        elif kind == "norm1":
                            v.wait_ge(rstd1_ready, half_done)
                            v.scalar_tensor_tensor(out=mid[:, at], in0=tile_of[("centre1", None)][:, at],
                                                   scalar=par_g[p][:, S1:S1 + 1], in1=norm_buf[:, at],
                                                   op0=ALU.mult, op1=ALU.mult).then_inc(normed1, 1)
                        elif kind == "mid":
                            v.wait_ge(normed1, half_done)
                            v.tensor_scalar(mid[:, at], mid[:, at], par_g[p][:, S1 + 1:S1 + 2], None, ALU.add)\
                                .then_inc(mid_ready, 1)
                        elif kind == "residual2":
                            v.wait_ge(gelu_down, half_done)
                            v.tensor_tensor(norm_buf[:, at], norm_buf[:, at], mid[:, at], ALU.add).then_inc(sum2_ready, 1)
                        elif kind == "norm2":
                            v.wait_ge(rstd2_ready, half_done)
                            v.scalar_tensor_tensor(out=res[:, p, at], in0=tile_of[("centre2", None)][:, at],
                                                   scalar=par_g[p][:, S2:S2 + 1], in1=norm_buf[:, at],
                                                   op0=ALU.mult, op1=ALU.mult).then_inc(normed2, 1)
                        elif kind == "state":
                            v.wait_ge(normed2, half_done)
                            v.tensor_scalar(res[:, p, at], res[:, p, at], par_g[p][:, S2 + 1:S2 + 2], None, ALU.add)\
                                .then_inc(state_ready, 1)
                        elif kind == "state_upper":
                            v.wait_ge(state_ready, half_done)
                            v.tensor_copy(res_h[:, p, at], res[:, p, at]).then_inc(state_h, 1)
                        elif kind == "state_lower":
                            v.wait_ge(state_h, half_done)
                            v.tensor_tensor(res_l[:, p, at], res[:, p, at], res_h[:, p, at].bitcast(F32),
                                            ALU.subtract).then_inc(state_l, 1)

                v.tensor_copy(par_f[0][:, :, :], table_f[:, 0, :, :]).then_inc(par_f_ready, 1)
                stage(0, 0, -1, 0)
                stage(1, 1, 0, 1)
                stage(2, 0, 0, 1)
                with v.Fori(1, LOOPS) as i:
                    stage(2 * i + 1, 1, i, i + 1)
                    stage(2 * i + 2, 0, i, i + 1)
                stage(STAGES - 1, 1, LAYERS - 1)
                stage(STAGES, 0, LAYERS - 1)

        with ExitStack() as c:
            back = [c.enter_context(nc.psum_tensor(f"back{q}", [P, N], F32)) for q in range(CHUNKS)]
            gated, turned = sem("gated_ready", c), sem("turned_back", c)
            added, stored = sem("output_ready", c), sem("output_stored", c)
            block = c.enter_context(nc.Block())

            @block.vector
            def _(v):
                for h in range(2):
                    at = slice(h * N, (h + 1) * N)
                    v.tensor_tensor(res[:, 1, at], res[:, 1, at], gate[:, S + h * N:S + (h + 1) * N], ALU.mult)\
                        .then_inc(gated, 1)
                for q in range(CHUNKS):
                    v.wait_ge(turned, q + 1)
                    v.tensor_tensor(x[:, 4 * q:4 * q + 4, :], x[:, 4 * q:4 * q + 4, :],
                                    back[q][:, :].rearrange("p (b d) -> p b d", d=P), ALU.add).then_inc(added, 1)

            @block.tensor
            def _(pe):
                for q in range(CHUNKS):
                    at_least(pe, gated, q - 1)
                    for b in range(4):
                        at = q % 2 * N + b * P
                        ins = pe.transpose(back[q][:, b * P:(b + 1) * P], res[:, q // 2, at:at + P], ident[:, :])
                    ins.then_inc(turned, 1)

            @block.sync
            def _(sp):
                for q in range(CHUNKS):
                    sp.wait_ge(added, q + 1)
                    sp.dma_start(out_tokens[:, 4 * q:4 * q + 4, :], x[:, 4 * q:4 * q + 4, :]).then_inc(stored, 16)
                sp.wait_ge(stored, 16 * CHUNKS)


INPUTS = ["L0_attn_x"] + [f"L0_attn_{n}" for n in (
    "Wq", "bq", "Wk", "bk", "Wv", "bv", "Wo", "bo", "ln1_s", "ln1_b", "W1", "b1", "W2", "b2", "ln2_s", "ln2_b")] \
    + [f"L0_ffn_{n}" for n in (
        "gw", "gb", "w1", "b1", "w3", "b3", "w2", "b2", "sw1", "sb1", "sw3", "sb3", "sw2", "sb2")]


def kernel(**inputs):
    import concourse.bacc as bacc
    from concourse.bass_utils import run_bass_kernel_spmd

    nc = bacc.Bacc("TRN2", target_bir_lowering=False, num_devices=1)
    arrays, tensors = {}, {}
    for name in INPUTS:
        a = np.ascontiguousarray(inputs[name])
        arrays[f"in_{name}"] = a
        tensors[name] = nc.dram_tensor(f"in_{name}", a.shape, mybir.dt.from_np(a.dtype), kind="ExternalInput").ap()
    x = arrays["in_L0_attn_x"]
    out = nc.dram_tensor("out", x.shape, mybir.dt.from_np(x.dtype), kind="ExternalOutput").ap()
    recurrent_attention_gated_by_experts(nc, tensors, out)
    return run_bass_kernel_spmd(nc, [arrays], core_ids=[0]).results[0]["out"]
```
